# Optimizing a Trainium2 kernel written in Bass

```python
import numpy as np
import jax
import jax.numpy as jnp

def _softmax(x, axis=-1):
    return jax.nn.softmax(x, axis=axis)

def _gelu(x):
    return jax.nn.gelu(x, approximate=True)

def _silu(x):
    return jax.nn.silu(x)

def _sigmoid(x):
    return jax.nn.sigmoid(x)

def _layernorm(x, axis=-1, eps=1e-05):
    m = jnp.mean(x, axis=axis, keepdims=True)
    v = jnp.var(x, axis=axis, keepdims=True)
    return (x - m) / jnp.sqrt(v + eps)

def _scatter_add(tgt, idx, src, axis=0):
    return tgt.at[idx].add(src)

def _segment_sum(src, seg, n):
    return jax.ops.segment_sum(src, seg, n)
kernel_name = 'mk_sandwich_d2_jaxref_r8_c45b1c'

def setup_inputs(seed: int=0):
    np.random.seed(seed)
    _w = jnp.asarray

    def _L0_attn_setup():
        import jax, jax.numpy as jnp
        import numpy as np
        N_HEADS = 16
        key = jax.random.key(seed)
        ks = jax.random.split(key, 9)
        B, S, D = (2, 256, 256)
        s = 0.02
        return {'X': jax.random.normal(ks[0], (B, S, D), jnp.float32), 'Wq': jax.random.normal(ks[1], (D, D), jnp.float32) * s, 'bq': jax.random.normal(ks[2], (D,), jnp.float32) * s, 'Wk': jax.random.normal(ks[3], (D, D), jnp.float32) * s, 'bk': jax.random.normal(ks[4], (D,), jnp.float32) * s, 'Wv': jax.random.normal(ks[5], (D, D), jnp.float32) * s, 'bv': jax.random.normal(ks[6], (D,), jnp.float32) * s, 'Wo': jax.random.normal(ks[7], (D, D), jnp.float32) * s, 'bo': jax.random.normal(ks[8], (D,), jnp.float32) * s}
    _L0_attn_in = _L0_attn_setup()

    def _L0_ffn_setup():
        import jax, jax.numpy as jnp
        import numpy as np
        HIDDEN = 256
        INTER = 1024
        B, S = (4, 128)

        def _qmatmul(x, w_int8, scale):
            y = jnp.einsum('bsh,ho->bso', x, w_int8.astype(x.dtype))
            return y * scale
        key = jax.random.key(seed)
        ks = jax.random.split(key, 7)
        x = jax.random.normal(ks[0], (B, S, HIDDEN), dtype=jnp.float32)
        w_gate = jax.random.randint(ks[1], (HIDDEN, INTER), -128, 128, dtype=jnp.int32).astype(jnp.int8)
        w_up = jax.random.randint(ks[2], (HIDDEN, INTER), -128, 128, dtype=jnp.int32).astype(jnp.int8)
        w_down = jax.random.randint(ks[3], (INTER, HIDDEN), -128, 128, dtype=jnp.int32).astype(jnp.int8)
        s_gate = jax.random.uniform(ks[4], (INTER,), dtype=jnp.float32) * 0.02 + 0.001
        s_up = jax.random.uniform(ks[5], (INTER,), dtype=jnp.float32) * 0.02 + 0.001
        s_down = jax.random.uniform(ks[6], (HIDDEN,), dtype=jnp.float32) * 0.02 + 0.001
        return {'x': x, 'w_gate': w_gate, 'w_up': w_up, 'w_down': w_down, 's_gate': s_gate, 's_up': s_up, 's_down': s_down}
    _L0_ffn_in = _L0_ffn_setup()

    def _L1_attn_setup():
        import jax, jax.numpy as jnp
        import numpy as np
        D_MODEL = 256
        key = jax.random.key(seed)
        kx, kw, kb = jax.random.split(key, 3)
        B, T, D = (4, 512, D_MODEL)
        x = jax.random.normal(kx, (B, T, D), dtype=jnp.float32)
        scale = 1.0 / np.sqrt(D)
        W = jax.random.uniform(kw, (D, 3 * D), dtype=jnp.float32, minval=-scale, maxval=scale)
        b = jax.random.uniform(kb, (3 * D,), dtype=jnp.float32, minval=-scale, maxval=scale)
        return {'x': x, 'W': W, 'b': b}
    _L1_attn_in = _L1_attn_setup()

    def _L1_ffn_setup():
        import jax, jax.numpy as jnp
        import numpy as np
        EPS = 1e-08

        def _bit_quant(w):
            scale = jnp.maximum(jnp.mean(jnp.abs(w)), EPS)
            w_ternary = jnp.clip(jnp.round(w / scale), -1.0, 1.0)
            return w + jax.lax.stop_gradient(w_ternary - w)
        key = jax.random.key(seed)
        k = jax.random.split(key, 5)
        emb, dff = (256, 1024)
        B, S = (4, 256)
        x = jax.random.normal(k[0], (B, S, emb), dtype=jnp.float32)
        w1 = jax.random.normal(k[1], (dff, emb), dtype=jnp.float32) * 0.02
        b1 = jax.random.normal(k[2], (dff,), dtype=jnp.float32) * 0.02
        w2 = jax.random.normal(k[3], (emb, dff), dtype=jnp.float32) * 0.02
        b2 = jax.random.normal(k[4], (emb,), dtype=jnp.float32) * 0.02
        return {'x': x, 'w1': w1, 'b1': b1, 'w2': w2, 'b2': b2}
    _L1_ffn_in = _L1_ffn_setup()
    _d = {'L0_attn_X': _L0_attn_in['X'], 'L0_attn_Wq': _L0_attn_in['Wq'], 'L0_attn_bq': _L0_attn_in['bq'], 'L0_attn_Wk': _L0_attn_in['Wk'], 'L0_attn_bk': _L0_attn_in['bk'], 'L0_attn_Wv': _L0_attn_in['Wv'], 'L0_attn_bv': _L0_attn_in['bv'], 'L0_attn_Wo': _L0_attn_in['Wo'], 'L0_attn_bo': _L0_attn_in['bo'], 'L0_ffn_w_gate': _L0_ffn_in['w_gate'], 'L0_ffn_w_up': _L0_ffn_in['w_up'], 'L0_ffn_w_down': _L0_ffn_in['w_down'], 'L0_ffn_s_gate': _L0_ffn_in['s_gate'], 'L0_ffn_s_up': _L0_ffn_in['s_up'], 'L0_ffn_s_down': _L0_ffn_in['s_down'], 'L1_attn_W': _L1_attn_in['W'], 'L1_attn_b': _L1_attn_in['b'], 'L1_ffn_w1': _L1_ffn_in['w1'], 'L1_ffn_b1': _L1_ffn_in['b1'], 'L1_ffn_w2': _L1_ffn_in['w2'], 'L1_ffn_b2': _L1_ffn_in['b2']}
    _x0 = _d['L0_attn_X']
    _d['L0_attn_X'] = jax.random.normal(jax.random.fold_in(jax.random.key(seed), 1), (2, 1024, 256), dtype=_x0.dtype)
    del _x0
    return _d

def reference(L0_attn_X, L0_attn_Wq, L0_attn_bq, L0_attn_Wk, L0_attn_bk, L0_attn_Wv, L0_attn_bv, L0_attn_Wo, L0_attn_bo, L0_ffn_w_gate, L0_ffn_w_up, L0_ffn_w_down, L0_ffn_s_gate, L0_ffn_s_up, L0_ffn_s_down, L1_attn_W, L1_attn_b, L1_ffn_w1, L1_ffn_b1, L1_ffn_w2, L1_ffn_b2):

    def _L0_attn_ref(X, Wq, bq, Wk, bk, Wv, bv, Wo, bo):
        import jax, jax.numpy as jnp
        import numpy as np
        N_HEADS = 16
        B, S, D = X.shape
        H = N_HEADS
        d_head = D // H
        scale = jnp.asarray(1.0 / np.sqrt(np.sqrt(d_head)), X.dtype)
        Q = (X @ Wq.T + bq).reshape(B, S, H, d_head) * scale
        K = (X @ Wk.T + bk).reshape(B, S, H, d_head) * scale
        V = (X @ Wv.T + bv).reshape(B, S, H, d_head)
        scores = jnp.einsum('bqhd,bkhd->bhqk', Q, K)
        causal = jnp.tril(jnp.ones((S, S), bool))
        scores = jnp.where(causal[None, None], scores, -jnp.inf)
        attn = jax.nn.softmax(scores.astype(jnp.float32), axis=-1).astype(X.dtype)
        out = jnp.einsum('bhqk,bkhd->bqhd', attn, V).reshape(B, S, D)
        return out @ Wo.T + bo

    def _L0_ffn_ref(x, w_gate, w_up, w_down, s_gate, s_up, s_down):
        import jax, jax.numpy as jnp
        import numpy as np
        HIDDEN = 256
        INTER = 1024
        B, S = (4, 128)

        def _qmatmul(x, w_int8, scale):
            y = jnp.einsum('bsh,ho->bso', x, w_int8.astype(x.dtype))
            return y * scale
        gate = jax.nn.silu(_qmatmul(x, w_gate, s_gate))
        up = _qmatmul(x, w_up, s_up)
        fuse = gate * up
        return _qmatmul(fuse, w_down, s_down)

    def _L1_attn_ref(x, W, b):
        import jax, jax.numpy as jnp
        import numpy as np
        D_MODEL = 256
        qkv = x @ W + b
        q, k, v = jnp.split(qkv, 3, axis=-1)
        qn = q / jnp.linalg.norm(q, axis=1, keepdims=True)
        kn = k / jnp.linalg.norm(k, axis=1, keepdims=True)
        kv = jnp.sum(kn * v, axis=1, keepdims=True)
        return qn * kv

    def _L1_ffn_ref(x, w1, b1, w2, b2):
        import jax, jax.numpy as jnp
        import numpy as np
        EPS = 1e-08

        def _bit_quant(w):
            scale = jnp.maximum(jnp.mean(jnp.abs(w)), EPS)
            w_ternary = jnp.clip(jnp.round(w / scale), -1.0, 1.0)
            return w + jax.lax.stop_gradient(w_ternary - w)
        w1q = _bit_quant(w1)
        w2q = _bit_quant(w2)
        h = jnp.einsum('bsd,fd->bsf', x, w1q) + b1
        h = jax.nn.gelu(h, approximate=False)
        return jnp.einsum('bsf,df->bsd', h, w2q) + b2
    x = L0_attn_X
    x = x + _layernorm(_L0_attn_ref(_layernorm(x, axis=-1), L0_attn_Wq, L0_attn_bq, L0_attn_Wk, L0_attn_bk, L0_attn_Wv, L0_attn_bv, L0_attn_Wo, L0_attn_bo), axis=-1)
    x = x + _layernorm(_L0_ffn_ref(_layernorm(x, axis=-1), L0_ffn_w_gate, L0_ffn_w_up, L0_ffn_w_down, L0_ffn_s_gate, L0_ffn_s_up, L0_ffn_s_down), axis=-1)
    x = x + _layernorm(_L1_attn_ref(_layernorm(x, axis=-1), L1_attn_W, L1_attn_b), axis=-1)
    x = x + _layernorm(_L1_ffn_ref(_layernorm(x, axis=-1), L1_ffn_w1, L1_ffn_b1, L1_ffn_w2, L1_ffn_b2), axis=-1)
    return x

_drawn_inputs = setup_inputs


def setup_inputs(seed=0):
    import zlib

    import numpy as np

    out = dict(_drawn_inputs(seed))
    spreads = {}
    factors = {'L0_attn_bq': 8.0, 'L0_attn_bk': 64.0, 'L1_ffn_b1': 64.0, 'L1_ffn_b2': 64.0}
    for name, (base, spread) in spreads.items():
        noise = np.random.default_rng([zlib.crc32(name.encode()), seed]).standard_normal(out[name].shape)
        drawn = base * np.exp(spread * noise) if base else spread * noise
        out[name] = jnp.asarray(drawn.astype(out[name].dtype))
    for name, factor in factors.items():
        out[name] = (out[name] * factor).astype(out[name].dtype)
    return out
```

```python
from contextlib import ExitStack

import numpy as np
from concourse import mybir

F32 = mybir.dt.float32
F16 = mybir.dt.float16
BF16 = mybir.dt.bfloat16
I8 = mybir.dt.int8
ALU = mybir.AluOpType
ACT = mybir.ActivationFunctionType
AX_X = mybir.AxisListType.X

P = 128
HEADS = 16
QUAD = 4
BANK = 512
EPS = 1e-5
QUANT_EPS = 1e-8
XS = 16.0
WS = 64.0
QS = 16.0
FS = 1.0 / 16.0
BIG = 3.0e38
TWICE_QQ = float(np.array([QS * QS] * 2, np.float16).view(np.float32)[0])


class Tally:

    def __init__(self, sem, step=1):
        self.sem, self.step, self.count, self.value = sem, step, 0, {}

    def mark(self, *key):
        self.count += self.step
        self.value[key] = self.count


def sandwich(nc, x_in, wq, wk, wv, wo, bqk, bv, bo, wg, wu, wd, sg, su, sd, w2, b2qkv, w1t, b1, w2t, b2, out):
    B, S, D = x_in.shape
    TOK = B * S
    NT = TOK // P
    CH = BANK
    TC = CH // P
    NC = TOK // CH
    CB = S // CH
    KC = D // P
    DH = D // HEADS
    INTER = 4 * wg.shape[1]
    FB = INTER // P
    NQ = HEADS // QUAD
    NQUADS = B * NQ
    KT = S // P
    NST = 3
    assert D == KC * P and DH * 8 == P and QUAD * 32 == P and CB == 2 and NC == 4

    whole = ExitStack()
    with whole:
        def sem(name):
            return whole.enter_context(nc.semaphore(name))

        def sb(stack, name, shape, dt):
            return stack.enter_context(nc.sbuf_tensor(name, shape, dt))

        def pb(stack, name, shape, dt):
            return stack.enter_context(nc.psum_tensor(name, shape, dt))

        x = sb(whole, "x", [P, NT, D], F32)
        ident = sb(whole, "ident", [P, P], F32)
        wo_pad = sb(whole, "wo_pad", [P, NQ, D], F32)
        wg16 = sb(whole, "wg16", [P, KC, INTER], F16)
        wu16 = sb(whole, "wu16", [P, KC, INTER], F16)
        wd16 = sb(whole, "wd16", [P, FB, D], F16)
        w1_16 = sb(whole, "w1_16", [P, KC, INTER], F16)
        w2_16 = sb(whole, "w2_16", [P, FB, D], F16)
        wl_hi = sb(whole, "wl_hi", [P, KC, 3 * D], F16)
        wl_lo = sb(whole, "wl_lo", [P, KC, 3 * D], F16)
        sg_sb = sb(whole, "sg_sb", [P, FB], F32)
        su_sb = sb(whole, "su_sb", [P, FB], F32)
        b1_sb = sb(whole, "b1_sb", [P, FB], F32)
        bl_sb = sb(whole, "bl_sb", [P, 3 * KC], F32)
        sd_b = sb(whole, "sd_b", [P, D], F32)
        b2_b = sb(whole, "b2_b", [P, D], F32)
        attn = sb(whole, "attn", [P, NQ, TOK], F32)
        minus_half = sb(whole, "minus_half", [P, 8], F32)
        scratch = nc.dram_tensor("qk_scratch", [4, D, TOK], F16, kind="Internal")
        den_scr = nc.dram_tensor("den_scratch", [NQUADS, QUAD, S], F32, kind="Internal")
        rec_scr = nc.dram_tensor("rec_scratch", [NQUADS, QUAD, S], F32, kind="Internal")

        x_loaded = [sem(f"x_loaded{c}") for c in range(NC)]
        qkv_w_loaded = sem("qkv_w_loaded")
        wl_loaded = sem("wl_loaded")
        i8_loaded = sem("i8_loaded")
        tern_loaded = sem("tern_loaded")
        wo_zero = sem("wo_zero")
        wo_loaded = sem("wo_loaded")
        small_loaded = sem("small_loaded")
        consts = sem("consts")
        dve_step = sem("dve_step")
        pool_step = sem("pool_step")
        act_step = sem("act_step")
        qk_stored = [sem(f"qk_stored{c}") for c in range(TOK // BANK)]
        steps = {"dve": 0, "pool": 0, "act": 0}
        step_sem = {"dve": dve_step, "pool": pool_step, "act": act_step}

        def then(engine, name, instruction):
            steps[name] += 1
            instruction.then_inc(step_sem[name], 1)
            engine.wait_ge(step_sem[name], steps[name])

        def ln_rows(dve, pool_sems, mv, stats, tiles):
            for i, t in enumerate(tiles):
                last = nc.vector.bn_stats(stats[:, i, :], t)
            then(dve, "dve", last)
            for i in range(len(tiles)):
                last = nc.vector.bn_aggr(mv[:, i, :], stats[:, i, :])
            return last

        with ExitStack() as life:
            VW = DH + 1
            v_aug = sb(life, "v_aug", [P, NT, HEADS * VW + 32 - VW], F32)
            q_st = [sb(life, f"q_st{i}", [P, QUAD, S], F16) for i in range(NST)]
            k_st = [sb(life, f"k_st{i}", [P, QUAD, S], F16) for i in range(NST)]
            mask = sb(life, "mask", [P, BANK], F32)

            with ExitStack() as ph:
                w0_hi = sb(ph, "w0_hi", [P, KC, 3 * D], F16)
                w0_lo = sb(ph, "w0_lo", [P, KC, 3 * D], F16)
                wlf = sb(ph, "wlf", [P, KC, 3 * D], F32)
                i8_words = sb(ph, "i8_words", [P, 3, 512], mybir.dt.int32)
                i8 = i8_words[:].bitcast(I8)
                w12f = attn[:, 0:2, :]
                below = attn[:, 2, :]
                w0f = attn[:, 3, 0:KC * 3 * D].rearrange("p (k n) -> p k n", k=KC)
                assert TOK == KC * INTER
                bqk_sb = sb(ph, "bqk_sb", [P, 4], F32)
                bqk16 = sb(ph, "bqk16", [P, 4], F32)
                bv_b = sb(ph, "bv_b", [P, D], F32)
                ones = sb(ph, "ones", [P, P], F32)
                wsum = sb(ph, "wsum", [P, 2], F32)
                thr = sb(ph, "thr", [P, 2, 2], F32)
                stats = sb(ph, "stats", [P, TC, 6], F32)
                mv = sb(ph, "mv", [P, 2, TC, 2], F32)
                rstd = sb(ph, "rstd", [P, 2, TC], F32)
                xn = sb(ph, "xn", [P, 2, TC, D], F32)
                xt_hi = sb(ph, "xt_hi", [P, 2, KC, CH], F16)
                xt_lo = sb(ph, "xt_lo", [P, 2, KC, CH], F16)
                t32 = sb(ph, "t32", [P, 2, CH], F32)
                qk16 = sb(ph, "qk16", [P, 2, 4, KC, CH], F16)
                ps_t = pb(ph, "ps_t", [P, 2, KC, CH], F32)
                ps_v = pb(ph, "ps_v", [P, TC, D], F32)
                ps_q = pb(ph, "ps_q", [P, 2, CH], F32)

                stats_done = sem("p0_stats_done")
                rstd_done = sem("p0_rstd_done")
                xn_done = sem("p0_xn_done")
                turned = sem("p0_turned")
                xt_hi_done = sem("p0_xt_hi_done")
                xt_lo_done = sem("p0_xt_lo_done")
                w0_hi_done = sem("w0_hi_done")
                w0_done = sem("w0_done")
                qk_made = sem("qk_made")
                qk_t32 = sem("qk_t32")
                qk_hi = sem("qk_hi")
                qk_lo = sem("qk_lo")
                v_made = sem("v_made")
                v_done = sem("v_done")
                wsum_done = sem("wsum_done")
                wsum_all = sem("wsum_all")
                wl_hi_done = sem("wl_hi_done")
                bq_done = sem("bq_done")

                with nc.Block() as block:
                    @block.sync
                    def _(sp):
                        def load_x(c):
                            src = x_in.rearrange("b (n p) d -> p (b n) d", p=P)[:, TC * c:TC * (c + 1), :]
                            sp.dma_start(x[:, TC * c:TC * (c + 1), :], src).then_inc(x_loaded[c], 16)
                        load_x(0)
                        for n, w in enumerate((wq, wk, wv)):
                            sp.dma_start(w0f[:, :, n * D:(n + 1) * D],
                                         w.rearrange("(k p) n -> p k n", p=P)).then_inc(qkv_w_loaded, 16)
                        for c in range(1, NC):
                            load_x(c)
                        for c in range(NC):
                            for a in range(4):
                                for m in range(KC):
                                    sp.wait_ge(qk_lo, 4 * c + 2 * (a // 2) + m + 1)
                                    sp.dma_start(scratch[a, m * P:(m + 1) * P, c * CH:(c + 1) * CH],
                                                 qk16[:, c % 2, a, m, :]).then_inc(qk_stored[c], 16)

                    @block.gpsimd
                    def _(pool):
                        nc.gpsimd.memset(ident[:], 0.0).then_inc(pool_step, 1)
                        steps["pool"] += 1
                        pool.wait_ge(pool_step, steps["pool"])
                        nc.gpsimd.affine_select(out=ident[:], in_=ident[:], compare_op=ALU.not_equal, fill=1.0,
                                                base=0, pattern=[[-1, P]], channel_multiplier=1).then_inc(consts, 1)
                        nc.gpsimd.memset(minus_half[:], -0.5).then_inc(consts, 1)
                        nc.gpsimd.memset(ones[:], 1.0).then_inc(consts, 1)
                        pool.wait_ge(consts, 3)

                        def rstd_of(c):
                            pool.wait_ge(stats_done, c + 1)
                            if c >= 2:
                                pool.wait_ge(xn_done, c - 1)
                            r = rstd[:, c % 2, :]
                            then(pool, "pool", nc.gpsimd.tensor_scalar(r, mv[:, c % 2, :, 1], EPS, None, ALU.add))
                            then(pool, "pool", nc.gpsimd.tensor_tensor(r, r, minus_half[:, 0:TC], ALU.pow))
                            nc.gpsimd.tensor_scalar(r, r, XS, None, ALU.mult).then_inc(rstd_done, 1)

                        rstd_of(0)
                        rstd_of(1)
                        nc.gpsimd.memset(v_aug[:], 1.0).then_inc(consts, 1)
                        for t in (*q_st, *k_st):
                            last = nc.gpsimd.memset(t[:].rearrange("p a b -> p (a b)").bitcast(F32), 0.0)
                        then(pool, "pool", last)
                        for t in k_st:
                            last = nc.gpsimd.memset(t[64:66].rearrange("p a b -> p (a b)").bitcast(F32), TWICE_QQ)
                        then(pool, "pool", last)
                        for c in range(NC):
                            if c + 2 < NC:
                                rstd_of(c + 2)
                            for u in range(4):
                                n = 4 * c + u
                                pool.wait_ge(qk_hi, n + 1)
                                if c >= 2:
                                    pool.wait_ge(qk_stored[c - 2], 16 * 8)
                                nc.gpsimd.tensor_tensor(qk16[:, c % 2, 2 * (u // 2) + 1, u % 2, :], t32[:, n % 2, :],
                                                        qk16[:, c % 2, 2 * (u // 2), u % 2, :],
                                                        ALU.subtract).then_inc(qk_lo, 1)
                        nc.gpsimd.memset(mask[:], 0.0).then_inc(consts, 1)
                        pool.wait_ge(consts, 5)
                        nc.gpsimd.affine_select(out=mask[:, BANK - P:BANK], in_=mask[:, BANK - P:BANK],
                                                compare_op=ALU.is_ge, fill=-BIG, base=0, pattern=[[-1, P]],
                                                channel_multiplier=1).then_inc(consts, 1)

                    @block.scalar
                    def _(act):
                        act.dma_start(bqk_sb[:], bqk).then_inc(small_loaded, 16)
                        act.dma_start(bv_b[:], bv.partition_broadcast(P)).then_inc(small_loaded, 16)
                        for dst, src in ((sg_sb, sg), (su_sb, su), (b1_sb, b1), (bl_sb, b2qkv)):
                            act.dma_start(dst[:], src).then_inc(small_loaded, 16)
                        act.dma_start(sd_b[:], sd.partition_broadcast(P)).then_inc(small_loaded, 16)
                        act.dma_start(b2_b[:], b2.partition_broadcast(P)).then_inc(small_loaded, 16)
                        act.dma_start(wlf[:], w2.rearrange("(k p) n -> p k n", p=P)).then_inc(wl_loaded, 16)
                        act.dma_start(w12f[:, 0, :].rearrange("p (k n) -> p k n", k=KC),
                                      w1t.rearrange("(k p) n -> p k n", p=P)).then_inc(tern_loaded, 16)
                        act.dma_start(w12f[:, 1, :].rearrange("p (k n) -> p k n", k=FB),
                                      w2t.rearrange("(k p) n -> p k n", p=P)).then_inc(tern_loaded, 16)
                        for n, w in enumerate((wg, wu, wd)):
                            act.dma_start(i8_words[:, n, :].rearrange("p (k n) -> p k n", n=w.shape[1]),
                                          w.rearrange("(k p) n -> p k n", p=P)).then_inc(i8_loaded, 16)
                        act.wait_ge(wo_zero, 1)
                        for h in range(QUAD):
                            act.dma_start(wo_pad[32 * h:32 * h + DH, :, :],
                                          wo.rearrange("(g h d) n -> h d g n", h=QUAD, d=DH)[h]).then_inc(wo_loaded, 16)
                        act.dma_start(wo_pad[DH:DH + 1, 0, :], bo).then_inc(wo_loaded, 16)

                        act.wait_ge(qkv_w_loaded, 48)
                        nc.scalar.activation(w0_hi[:], w0f, ACT.Copy, scale=WS).then_inc(w0_hi_done, 1)

                        def high(c):
                            act.wait_ge(turned, c + 1)
                            if c >= 2:
                                act.wait_ge(v_made, c - 1)
                            nc.scalar.activation(xt_hi[:, c % 2], ps_t[:, c % 2], ACT.Copy).then_inc(xt_hi_done, 1)

                        high(0)
                        act.wait_ge(bq_done, 1)
                        for c in range(NC):
                            for u in range(4):
                                n = 4 * c + u
                                if u == 1 and c + 1 < NC:
                                    high(c + 1)
                                act.wait_ge(qk_made, n + 1)
                                if n >= 2:
                                    act.wait_ge(qk_lo, n - 1)
                                nc.scalar.activation(t32[:, n % 2, :], ps_q[:, u % 2, :], ACT.Identity, bias=bqk16[:, u:u + 1],
                                                     scale=QS / (XS * WS)).then_inc(qk_t32, 1)
                                act.wait_ge(qk_t32, n + 1)
                                if c >= 2:
                                    act.wait_ge(qk_stored[c - 2], 16 * 8)
                                nc.scalar.activation(qk16[:, c % 2, 2 * (u // 2), u % 2, :], t32[:, n % 2, :],
                                                     ACT.Copy).then_inc(qk_hi, 1)
                            if c == 0:
                                act.wait_ge(wl_loaded, 16)
                                nc.scalar.activation(wl_hi[:], wlf[:], ACT.Copy, scale=WS).then_inc(wl_hi_done, 1)
                            if c == 1:
                                act.wait_ge(tern_loaded, 32)
                                for n in range(2):
                                    then(act, "act", nc.scalar.activation(below, w12f[:, n, :], ACT.Abs,
                                                                          accum_out=wsum[:, n:n + 1]))
                            if c == 2:
                                act.wait_ge(i8_loaded, 48)
                                nc.scalar.activation(wg16[:].rearrange("p a b -> p (a b)"), i8[:, 0, :], ACT.Copy)
                                nc.scalar.activation(wu16[:].rearrange("p a b -> p (a b)"), i8[:, 1, :], ACT.Copy)
                                nc.scalar.activation(wd16[:].rearrange("p a b -> p (a b)"), i8[:, 2, :], ACT.Copy)

                    @block.tensor
                    def _(pe):
                        pe.wait_ge(consts, 3)

                        def turn(c):
                            pe.wait_ge(xn_done, c + 1)
                            if c >= 2:
                                pe.wait_ge(xt_lo_done, c - 1)
                            for i in range(TC):
                                for k in range(KC):
                                    last = nc.tensor.transpose(ps_t[:, c % 2, k, i * P:(i + 1) * P],
                                                               xn[:, c % 2, i, k * P:(k + 1) * P], ident[:])
                            last.then_inc(turned, 1)

                        turn(0)
                        for c in range(NC):
                            if c + 1 < NC:
                                turn(c + 1)
                            if c == 0:
                                pe.wait_ge(w0_done, 1)
                            pe.wait_ge(xt_lo_done, c + 1)
                            hi, lo = xt_hi[:, c % 2], xt_lo[:, c % 2]
                            for u in range(4):
                                n = 4 * c + u
                                if n >= 2:
                                    pe.wait_ge(qk_t32, n - 1)
                                cols = slice(u * P, (u + 1) * P)
                                terms = [(w, r, k) for k in range(KC) for w, r in ((w0_hi, hi), (w0_hi, lo), (w0_lo, hi))]
                                for j, (w, r, k) in enumerate(terms):
                                    last = nc.tensor.matmul(ps_q[:, u % 2, :], w[:, k, cols], r[:, k, :],
                                                            start=j == 0, stop=j == len(terms) - 1)
                                last.then_inc(qk_made, 1)
                            if c >= 1:
                                pe.wait_ge(v_done, c)
                            for i in range(TC):
                                rows = slice(i * P, (i + 1) * P)
                                terms = [(r, w, k) for k in range(KC) for r, w in ((hi, w0_hi), (hi, w0_lo), (lo, w0_hi))]
                                for j, (r, w, k) in enumerate(terms):
                                    last = nc.tensor.matmul(ps_v[:, i, :], r[:, k, rows], w[:, k, 2 * D:3 * D],
                                                            start=j == 0, stop=j == len(terms) - 1)
                            last.then_inc(v_made, 1)
                            if c == NC - 2:
                                pe.wait_ge(act_step, 2)
                                nc.tensor.matmul(ps_t[:, c % 2, 0, 0:2], ones[:], wsum[:], start=True,
                                                 stop=True).then_inc(wsum_all, 1)

                    @block.vector
                    def _(dve):
                        def ln(c):
                            dve.wait_ge(x_loaded[c], 16)
                            if c >= 2:
                                dve.wait_ge(rstd_done, c - 1)
                            ln_rows(dve, None, mv[:, c % 2], stats,
                                    [x[:, TC * c + i, :] for i in range(TC)]).then_inc(stats_done, 1)

                        def normalise(c):
                            dve.wait_ge(rstd_done, c + 1)
                            dve.wait_ge(stats_done, c + 1)
                            if c >= 2:
                                dve.wait_ge(turned, c - 1)
                            for i in range(TC):
                                last = nc.vector.tensor_scalar(xn[:, c % 2, i, :], x[:, TC * c + i, :], mv[:, c % 2, i, 0:1],
                                                               rstd[:, c % 2, i:i + 1], ALU.subtract, ALU.mult)
                            last.then_inc(xn_done, 1)

                        ln(0)
                        nc.vector.memset(wo_pad[:], 0.0).then_inc(wo_zero, 1)
                        dve.wait_ge(small_loaded, 128)
                        nc.vector.tensor_scalar(bqk16[:], bqk_sb[:], QS, None, ALU.mult).then_inc(bq_done, 1)
                        normalise(0)
                        ln(1)
                        dve.wait_ge(w0_hi_done, 1)
                        nc.vector.scalar_tensor_tensor(w0_lo[:].rearrange("p a b -> p (a b)"), w0f.rearrange("p a b -> p (a b)"),
                                                       WS, w0_hi[:].rearrange("p a b -> p (a b)"),
                                                       ALU.mult, ALU.subtract).then_inc(w0_done, 1)
                        normalise(1)

                        def low(c):
                            dve.wait_ge(xt_hi_done, c + 1)
                            if c >= 2:
                                dve.wait_ge(v_made, c - 1)
                            nc.vector.tensor_tensor(xt_lo[:, c % 2], ps_t[:, c % 2], xt_hi[:, c % 2], ALU.subtract).then_inc(xt_lo_done, 1)

                        low(0)
                        for c in range(NC):
                            if c + 2 < NC:
                                ln(c + 2)
                            if c + 1 < NC:
                                low(c + 1)
                            if c + 2 < NC:
                                normalise(c + 2)
                            dve.wait_ge(v_made, c + 1)
                            if c == 0:
                                dve.wait_ge(consts, 4)
                            for i in range(TC):
                                last = nc.vector.scalar_tensor_tensor(
                                    v_aug[:, TC * c + i, 0:HEADS * VW].rearrange("p (h e) -> p h e", e=VW)[:, :, 0:DH],
                                    ps_v[:, i, :].rearrange("p (h d) -> p h d", d=DH),
                                    1.0 / (XS * WS), bv_b[:].rearrange("p (h d) -> p h d", d=DH), ALU.mult, ALU.add)
                            last.then_inc(v_done, 1)
                            if c == 0:
                                dve.wait_ge(wl_hi_done, 1)
                                nc.vector.scalar_tensor_tensor(wl_lo[:].rearrange("p a b -> p (a b)"), wlf[:].rearrange("p a b -> p (a b)"),
                                                               WS, wl_hi[:].rearrange("p a b -> p (a b)"), ALU.mult, ALU.subtract)
                            if c == NC - 2:
                                dve.wait_ge(wsum_all, 1)
                                then(dve, "dve", nc.vector.tensor_scalar(thr[:, 0, :], ps_t[:, (NC - 2) % 2, 0, 0:2], 1.0 / (D * INTER), QUANT_EPS,
                                                                         ALU.mult, ALU.max))
                                then(dve, "dve", nc.vector.tensor_scalar(thr[:, 1, :], thr[:, 0, :], -0.5, None, ALU.mult))
                                nc.vector.tensor_scalar(thr[:, 0, :], thr[:, 0, :], 0.5, None, ALU.mult).then_inc(wsum_done, 1)
                                dve.wait_ge(wsum_done, 1)
                                dve.wait_ge(act_step, 2)
                                for n, dst in enumerate((w1_16, w2_16)):
                                    then(dve, "dve", nc.vector.tensor_scalar(below, w12f[:, n, :], thr[:, 1, n:n + 1], None, ALU.is_lt))
                                    then(dve, "dve", nc.vector.scalar_tensor_tensor(
                                        dst[:].rearrange("p a b -> p (a b)"), w12f[:, n, :], thr[:, 0, n:n + 1], below,
                                        ALU.is_gt, ALU.subtract))
                        nc.vector.tensor_scalar(sg_sb[:], sg_sb[:], 1.0 / XS, None, ALU.mult)
                        nc.vector.tensor_scalar(su_sb[:], su_sb[:], FS / XS, None, ALU.mult)
                        nc.vector.tensor_scalar(sd_b[:], sd_b[:], 1.0 / FS, None, ALU.mult)


            with ExitStack() as ph:
                probs = sb(ph, "probs", [P, 3, QUAD, CH], F32)
                o_sb = sb(ph, "o_sb", [P, 2, S], F32)
                den = sb(ph, "den", [P, 2, 32], F32)
                rec_b = sb(ph, "rec_b", [P, 2, S], F32)
                parts = sb(ph, "parts", [P, 2, QUAD, 12], F32)
                rowmax = sb(ph, "rowmax", [P, 2, QUAD, KT], F32)
                max_hi = sb(ph, "max_hi", [QUAD * KT, 2, P], F16)
                max_lo = sb(ph, "max_lo", [QUAD * KT, 2, P], F16)
                junk = sb(ph, "junk", [P, 4, CH], BF16)
                ps_s = pb(ph, "ps_s", [P, 2, 2, CH], F32)
                ps_m = pb(ph, "ps_m", [P, 3, CH], F32)
                ps_o = pb(ph, "ps_o", [P, CH], F32)

                PIECES = [(t, p) for t in range(KT) for p in range(t // TC + 1)]
                NP = len(PIECES)
                MAXES = QUAD * NP
                UNITS = [(c, j) for c in range(CB) for j in range(TC * (c + 1))]
                NU = len(UNITS)
                DIAGS = [u for u, (c, j) in enumerate(UNITS) if j >= TC * c]
                LEAD = 3
                LAG = 2

                stacks_in = [sem(f"stacks_in{i}") for i in range(NST)]
                max_made = sem("max_made")
                max_read = sem("max_read")
                max_full = sem("max_full")
                max_turned = sem("max_turned")
                max_split = sem("max_split")
                max_rows_in = [sem(f"max_rows_in{i}") for i in range(2)]
                scores_made = sem("scores_made")
                exp_done = sem("exp_done")
                masked = sem("masked")
                pv_done = sem("pv_done")
                o_copied = sem("o_copied")
                den_out = sem("den_out")
                den_in = sem("den_in")
                rec_done = sem("rec_done")
                rec_out = sem("rec_out")
                rec_in = [sem(f"rec_in{i}") for i in range(2)]
                attn_done = sem("attn_done")

                def width(u):
                    c, j = UNITS[u]
                    first = max(CH * c, P * j)
                    return first, CH * (c + 1) - first

                def max_slot(i, n):
                    return (i * (MAXES + 1) + n) % 3

                with nc.Block() as block:
                    @block.sync
                    def _(sp):
                        def stacks(i):
                            b, g = i // NQ, i % NQ
                            if i % NQ == 0:
                                for c in range(CB * b, CB * (b + 1)):
                                    sp.wait_ge(qk_stored[c], 16 * 8)
                            if i >= NST:
                                sp.wait_ge(scores_made, 2 * NU * (i - NST + 1))
                            rows = scratch[:, g * QUAD * DH:(g + 1) * QUAD * DH, b * S:(b + 1) * S]\
                                .rearrange("a (h d) t -> a d h t", d=DH)
                            for r, (a_q, a_k) in enumerate(((0, 2), (0, 3), (1, 2), (1, 3))):
                                for st, a in ((q_st, a_q), (k_st, a_k)):
                                    sp.dma_start(st[i % NST][r * DH:(r + 1) * DH], rows[a]).then_inc(stacks_in[i % NST], 16)

                        def max_rows(i):
                            sp.wait_ge(max_split, i + 1)
                            for r, part in enumerate((max_hi, max_lo)):
                                sp.dma_start(q_st[i % NST][64 + r:65 + r].rearrange("o h (t n) -> o (h t) n", n=P),
                                             part[:, i % 2, :]).then_inc(max_rows_in[i % 2], 16)

                        def denominators(i):
                            sp.wait_ge(o_copied, CB * (i + 1))
                            for h in range(QUAD):
                                sp.dma_start(den_scr[i, h:h + 1, :], o_sb[32 * h + DH:32 * h + DH + 1, i % 2, :])\
                                    .then_inc(den_out, 16)
                            sp.wait_ge(den_out, 16 * QUAD * (i + 1))
                            sp.dma_start(den[:, i % 2, :], den_scr[i].rearrange("h (a b) -> (h a) b", b=32)).then_inc(den_in, 16)
                            sp.wait_ge(rec_done, i + 1)
                            sp.dma_start(rec_scr[i].rearrange("h (a b) -> (h a) b", b=32), den[:, i % 2, :]).then_inc(rec_out, 16)
                            sp.wait_ge(rec_out, 16 * (i + 1))
                            if i >= 2:
                                sp.wait_ge(attn_done, i - 1)
                            for h in range(QUAD):
                                sp.dma_start(rec_b[32 * h:32 * h + 32, i % 2, :],
                                             rec_scr[i, h, :].partition_broadcast(32)).then_inc(rec_in[i % 2], 16)

                        for i in range(NST):
                            stacks(i)
                        max_rows(0)
                        for i in range(NQUADS):
                            if i >= 1 and i + NST - 1 < NQUADS:
                                stacks(i + NST - 1)
                            if i >= 1:
                                denominators(i - 1)
                            if i + 1 < NQUADS:
                                max_rows(i + 1)
                        denominators(NQUADS - 1)

                    @block.tensor
                    def _(pe):
                        def piece(i, n):
                            h, (t, p) = n // NP, PIECES[n % NP]
                            if n == 0:
                                pe.wait_ge(stacks_in[i % NST], 16 * 8 * (i // NST + 1))
                            if n == 2 and i:
                                pe.wait_ge(max_split, i)
                            elif i or n >= 3:
                                pe.wait_ge(max_read, i * MAXES + n - 2 + (1 if n < 2 else 0))
                            keys = slice(CH * p, min(CH * (p + 1), P * (t + 1)))
                            nc.tensor.matmul(ps_m[:, max_slot(i, n), 0:keys.stop - keys.start],
                                             q_st[i % NST][0:64, h, t * P:(t + 1) * P], k_st[i % NST][0:64, h, keys],
                                             start=True, stop=True).then_inc(max_made, 1)

                        def turn_max(i):
                            pe.wait_ge(max_full, i + 1)
                            nc.tensor.transpose(ps_m[0:QUAD * KT, max_slot(i, MAXES), 0:P],
                                                rowmax[:, i % 2].rearrange("p h t -> p (h t)"), ident[:]).then_inc(max_turned, 1)

                        def scores(i, u, pair):
                            c, j = UNITS[u]
                            first, w = width(u)
                            if u == 0 and pair == 0:
                                pe.wait_ge(max_rows_in[i % 2], 32 * (i // 2 + 1))
                            n = 2 * (i * NU + u) + pair
                            if n >= 2:
                                pe.wait_ge(exp_done, n - 1)
                            for h in range(2):
                                last = nc.tensor.matmul(ps_s[:, pair, h, 0:w], k_st[i % NST][:, 2 * pair + h, j * P:(j + 1) * P],
                                                        q_st[i % NST][:, 2 * pair + h, first:first + w], start=True, stop=True)
                            last.then_inc(scores_made, 1)

                        def product(i, u):
                            c, j = UNITS[u]
                            first, w = width(u)
                            n = i * NU + u
                            pe.wait_ge(exp_done, 2 * n + 2)
                            if u in DIAGS:
                                pe.wait_ge(masked, i * len(DIAGS) + DIAGS.index(u) + 1)
                            if j == 0 and i * CB + c >= 1:
                                pe.wait_ge(o_copied, i * CB + c)
                            at = first - CH * c
                            tile = (i // NQ) * KT + j
                            for h in range(QUAD):
                                head = QUAD * (i % NQ) + h
                                last = nc.tensor.matmul(ps_o[32 * h:32 * h + 32, at:at + w],
                                                        v_aug[:, tile, VW * head:VW * head + 32], probs[:, n % 3, h, 0:w],
                                                        start=j == 0, stop=j == TC * (c + 1) - 1)
                            last.then_inc(pv_done, 1)

                        def pieces(start, stop):
                            for m in range(start, min(stop, NQUADS * MAXES)):
                                i, k = divmod(m, MAXES)
                                piece(i, k)
                                if k == 1 and i:
                                    turn_max(i - 1)
                            if start < NQUADS * MAXES <= stop:
                                turn_max(NQUADS - 1)

                        PER = MAXES // NU
                        pieces(0, PER * (NU + LEAD))
                        assert PER == 4
                        for n in range(NQUADS * NU):
                            ahead = PER * (n + NU + LEAD)
                            for pair in range(2):
                                scores(*divmod(n, NU), pair)
                                pieces(ahead + pair, ahead + pair + 1)
                            if n >= LAG:
                                product(*divmod(n - LAG, NU))
                            pieces(ahead + 2, ahead + 4)
                        for u in range(NU - LAG, NU):
                            product(NQUADS - 1, u)

                    @block.scalar
                    def _(act):
                        def copy_out(n):
                            i, c = divmod(n, CB)
                            act.wait_ge(pv_done, i * NU + (TC if c == 0 else NU))
                            if i >= 2 and c == 0:
                                act.wait_ge(attn_done, i - 1)
                            nc.scalar.activation(o_sb[:, i % 2, c * CH:(c + 1) * CH], ps_o[:], ACT.Copy).then_inc(o_copied, 1)

                        copied = 0
                        for i in range(NQUADS):
                            for u in range(NU):
                                n = i * NU + u
                                first, w = width(u)
                                if n >= 3:
                                    act.wait_ge(pv_done, n - 2)
                                for pair in range(2):
                                    act.wait_ge(scores_made, 2 * n + pair + 1)
                                    nc.scalar.activation(probs[:, n % 3, 2 * pair:2 * pair + 2, 0:w], ps_s[:, pair, :, 0:w],
                                                         ACT.Exp, scale=0.25 / (QS * QS)).then_inc(exp_done, 1)
                                if (u == TC - 1 + LAG) or (u == LAG - 1 and i):
                                    copy_out(copied)
                                    copied += 1
                        copy_out(copied)

                    @block.gpsimd
                    def _(pool):
                        def normalise(i):
                            pool.wait_ge(rec_in[i % 2], 16 * QUAD * (i // 2 + 1))
                            pool.wait_ge(o_copied, CB * (i + 1))
                            b, g = i // NQ, i % NQ
                            nc.gpsimd.tensor_tensor(attn[:, g, b * S:(b + 1) * S], o_sb[:, i % 2, :], rec_b[:, i % 2, :],
                                                    ALU.mult).then_inc(attn_done, 1)

                        for i in range(NQUADS):
                            for k, u in enumerate(DIAGS):
                                n = i * NU + u
                                pool.wait_ge(exp_done, 2 * n + 2)
                                tri = probs[:, n % 3, :, 0:P]
                                nc.gpsimd.affine_select(out=tri, in_=tri, compare_op=ALU.is_ge, fill=0.0, base=0,
                                                        pattern=[[0, QUAD], [1, P]], channel_multiplier=-1).then_inc(masked, 1)
                                if k == len(DIAGS) - 1 and i >= 1:
                                    normalise(i - 1)
                        normalise(NQUADS - 1)

                    @block.vector
                    def _(dve):
                        def maxima(i, n):
                            h, (t, p) = n // NP, PIECES[n % NP]
                            w = min(CH, P * (t + 1) - CH * p)
                            dve.wait_ge(max_made, i * MAXES + n + 1)
                            src, dst = ps_m[:, max_slot(i, n), 0:w], parts[:, i % 2, h, n % NP:n % NP + 1]
                            m = i * MAXES + n
                            if p == t // TC:
                                if m >= 4:
                                    dve.wait_ge(max_read, m - 3)
                                nc.vector.tensor_tensor_reduce(junk[:, m % 4, 0:w], src, mask[:, CH - w:CH], 1.0, -BIG, ALU.add,
                                                               ALU.max, dst).then_inc(max_read, 1)
                            else:
                                nc.vector.tensor_reduce(dst, src, axis=AX_X, op=ALU.max).then_inc(max_read, 1)

                        def finish_max(i):
                            pi, mi = parts[:, i % 2], rowmax[:, i % 2]
                            dve.wait_ge(max_read, MAXES * (i + 1))
                            nc.vector.tensor_copy(mi[:, :, 0:TC], pi[:, :, 0:TC])
                            two = pi[:, :, TC:NP].rearrange("p h (t c) -> p h t c", c=2)
                            nc.vector.tensor_tensor(mi[:, :, TC:KT], two[:, :, :, 0], two[:, :, :, 1], ALU.max).then_inc(max_full, 1)

                        def split_max(i):
                            dve.wait_ge(max_turned, i + 1)
                            if i >= 2:
                                dve.wait_ge(max_rows_in[i % 2], 32 * (i // 2))
                            src = ps_m[0:QUAD * KT, max_slot(i, MAXES), 0:P]
                            then(dve, "dve", nc.vector.tensor_scalar(max_hi[:, i % 2, :], src, -1.0 / (QS * QS), None, ALU.mult))
                            nc.vector.scalar_tensor_tensor(max_lo[:, i % 2, :], src, -1.0 / (QS * QS), max_hi[:, i % 2, :],
                                                           ALU.mult, ALU.subtract).then_inc(max_split, 1)

                        def reciprocals(i):
                            dve.wait_ge(den_in, 16 * (i + 1))
                            nc.vector.reciprocal(den[:, i % 2, :], den[:, i % 2, :]).then_inc(rec_done, 1)

                        for i in range(NQUADS):
                            for n in range(MAXES):
                                maxima(i, n)
                                if n == 1 and i:
                                    split_max(i - 1)
                                if n == 3 * NP and i >= 2:
                                    reciprocals(i - 2)
                            finish_max(i)
                        split_max(NQUADS - 1)
                        reciprocals(NQUADS - 2)
                        reciprocals(NQUADS - 1)

        with ExitStack() as ph:
            stats = sb(ph, "stats2", [P, TC, 6], F32)
            mv_o = sb(ph, "mv_o", [P, TC, 2], F32)
            rstd_o = sb(ph, "rstd_o", [P, TC], F32)
            mv_x = sb(ph, "mv_x", [P, TC, 2], F32)
            rstd_x = sb(ph, "rstd_x", [P, TC], F32)
            y = sb(ph, "y", [P, TC, D], F32)
            xn = sb(ph, "xn2", [P, 2, TC, D], F32)
            xt_hi = sb(ph, "xt_hi2", [P, 2, KC, CH], F16)
            xt_lo = sb(ph, "xt_lo2", [P, 2, KC, CH], F16)
            act_out = sb(ph, "act_out", [P, 2, CH], F32)
            h32 = sb(ph, "h32", [P, 3, CH], F32)
            h_hi = sb(ph, "h_hi", [P, 2, FB, CH], F16)
            h_lo = sb(ph, "h_lo", [P, 2, FB, CH], F16)
            qt = sb(ph, "qt", [P, KC, TOK], F32)
            kt32 = sb(ph, "kt32", [P, 2, CH], F32)
            vt32 = sb(ph, "vt32", [P, 2, CH], F32)
            sums = sb(ph, "sums", [P, 3, KC, NC], F32)
            tot = sb(ph, "tot", [P, B, 3, KC], F32)
            sq_junk = sb(ph, "sq_junk", [P, CH], BF16)
            kv_junk = sb(ph, "kv_junk", [P, CH], BF16)
            ps_slot = [pb(ph, f"ps_slot{i}", [P, 2 * CH], F32) for i in range(2)]
            ps_blk = [pb(ph, f"ps_blk{i}", [P, 2, CH], F32) for i in range(2)]

            ORDER = [(w[:-2], int(w[-1])) for w in (
                "WO:0 OUT0:0 LN1:0 WO:1 TURN1:0 OUT0:1 LN1:1 GU:0 WO:2 TURN1:1 OUT0:2 LN1:2 GU:1 DOWN1:0 OUT1:0 WO:3 "
                "TURN1:2 OUT0:3 LN1:3 GU:2 DOWN1:1 OUT1:1 TURN1:3 LN2:0 GU:3 DOWN1:2 OUT1:2 TURN2:0 LN2:1 QKV:0 "
                "DOWN1:3 OUT1:3 TURN2:1 LN2:2 QKV:1 BACK:0 TURN2:2 OUT2:0 LN2:3 QKV:2 BACK:1 OUT2:1 TURN2:3 LN3:0 "
                "QKV:3 TURN3:0 LN3:1 UP:0 BACK:2 OUT2:2 TURN3:1 LN3:2 UP:1 DOWN3:0 OUT3:0 BACK:3 OUT2:3 TURN3:2 LN3:3 "
                "UP:2 DOWN3:1 OUT3:1 TURN3:3 UP:3 DOWN3:2 OUT3:2 DOWN3:3 OUT3:3").split()]
            SLOTTED = ("WO", "TURN1", "DOWN1", "TURN2", "BACK", "TURN3", "DOWN3")
            slot_use = {s: n for n, s in enumerate(s for s in ORDER if s[0] in SLOTTED)}
            NPAIR = {"GU": FB, "QKV": 3, "UP": FB // 2}
            pair_use, n_pairs = {}, 0
            for s in ORDER:
                for f in range(NPAIR.get(s[0], 0)):
                    pair_use[s + (f,)] = n_pairs
                    n_pairs += 1
            outs = {s: n for n, s in enumerate(s for s in ORDER if s[0].startswith("OUT"))}
            lns = {s: n for n, s in enumerate(s for s in ORDER if s[0].startswith("LN"))}
            turns = {s: n for n, s in enumerate(s for s in ORDER if s[0].startswith("TURN"))}
            products = {s: n for n, s in enumerate(s for s in ORDER if s[0] in ("GU", "QKV", "UP"))}
            hiddens = {s: n for n, s in enumerate(s for s in ORDER if s[0] in ("GU", "UP"))}
            downs = {s: n for n, s in enumerate(s for s in ORDER if s[0] in ("DOWN1", "DOWN3"))}
            BEFORE = {"LN1": "OUT0", "LN2": "OUT1", "LN3": "OUT2", "GU": "TURN1", "QKV": "TURN2", "UP": "TURN3",
                      "OUT0": "WO", "OUT1": "DOWN1", "OUT2": "BACK", "OUT3": "DOWN3", "DOWN1": "GU", "DOWN3": "UP"}

            list_gu = [(s[1], f) for s in ORDER if s[0] == "GU" for f in range(FB)]
            hcount = {}
            for s in hiddens:
                for f in range(FB):
                    hcount[s + (f,)] = len(hcount) + 1
            used = {n: s for s, n in slot_use.items()}
            freed = {}
            for s in ORDER:
                if s[0].startswith("OUT"):
                    freed[(BEFORE[s[0]], s[1])] = len(freed) + 1
                elif s[0].startswith("TURN"):
                    freed[s] = len(freed) + 1
            down_slot = {hiddens[(BEFORE[s[0]], s[1])]: slot_use[s] + 1 for s in downs}
            xn_turned = [slot_use[t] + 1 for t in turns]

            def high_half(engine, n, f, s):
                m = hcount[s + (f,)]
                engine.wait_ge(h32_done, m)
                if n >= 2 and f == 0:
                    engine.wait_ge(slot_made, down_slot[n - 2])
                src, dst = h32[:, (m - 1) % 3, :], h_hi[:, n % 2, f, :]
                if s[0] == "GU":
                    nc.scalar.activation(dst, src, ACT.Copy).then_inc(hi_done, 1)
                else:
                    nc.vector.tensor_copy(dst, src).then_inc(hi_done, 1)

            slot_made = sem("slot_made")
            slot_free = sem("slot_free")
            pair_made = sem("pair_made")
            out_stats = sem("out_stats")
            out_rstd = sem("out_rstd")
            x_stats = sem("x_stats")
            x_rstd = sem("x_rstd")
            xn_ready = sem("xn_ready")
            turn_hi = sem("turn_hi")
            product_done = sem("product_done")
            silu_done = sem("silu_done")
            h32_done = sem("h32_done")
            hi_done = sem("hi_done")
            lo_done = sem("lo_done")
            down_done = sem("down_done")
            k_done = sem("k_done")
            q_done = sem("q_done")
            kv_done = sem("kv_done")
            factor_done = sem("factor_done")
            q_scaled = sem("q_scaled")
            x_final = sem("x_final")
            stored = sem("stored")

            pair_freed = {}
            for key, n in pair_use.items():
                kind, c, f = key
                if kind == "GU":
                    pair_freed[n] = (h32_done, hcount[key])
                elif kind == "UP":
                    pair_freed[n] = (h32_done, hcount[(kind, c, 2 * f + 1)])
                elif f < 2:
                    pair_freed[n] = (q_done, 4 * c + 2 * f + 2)
                else:
                    pair_freed[n] = (kv_done, 2 * (c + 1))

            def slot_of(s):
                return ps_slot[slot_use[s] % 2]

            def pair_of(key):
                return ps_blk[pair_use[key] % 2]

            with nc.Block() as block:
                @block.tensor
                def _(pe):
                    def take_slot(s):
                        if slot_use[s] >= 2:
                            pe.wait_ge(slot_free, freed[used[slot_use[s] - 2]])
                        return slot_of(s)

                    def take_pair(key):
                        if pair_use[key] >= 2:
                            pe.wait_ge(*pair_freed[pair_use[key] - 2])
                        return pair_of(key)

                    def blocks(s, halves, f):
                        par = turns[(BEFORE[s[0]], s[1])] % 2
                        ps = take_pair(s + (f,))
                        for i, (terms, col) in enumerate(halves):
                            cols = slice(col * P, (col + 1) * P)
                            jobs = [(w, r, k) for k in range(KC) for w, r in terms]
                            for j, (w, r, k) in enumerate(jobs):
                                last = nc.tensor.matmul(ps[:, i, :], w[:, k, cols], r[:, par, k, :],
                                                        start=j == 0, stop=j == len(jobs) - 1)
                        last.then_inc(pair_made, 1)

                    pe.wait_ge(wo_loaded, 16 * (QUAD + 1))
                    for s in ORDER:
                        kind, c = s
                        if kind == "WO":
                            ps = take_slot(s)
                            for i in range(TC):
                                rows = slice((TC * c + i) * P, (TC * c + i + 1) * P)
                                for g in range(NQ):
                                    last = nc.tensor.matmul(ps[:, i * D:(i + 1) * D], attn[:, g, rows], wo_pad[:, g, :],
                                                            start=g == 0, stop=g == NQ - 1)
                            last.then_inc(slot_made, 1)
                        elif kind.startswith("TURN"):
                            ps = take_slot(s)
                            pe.wait_ge(xn_ready, turns[s] + 1)
                            for i in range(TC):
                                for k in range(KC):
                                    last = nc.tensor.transpose(ps[:, k * CH + i * P:k * CH + (i + 1) * P],
                                                               xn[:, turns[s] % 2, i, k * P:(k + 1) * P], ident[:])
                            last.then_inc(slot_made, 1)
                        elif kind in ("GU", "UP", "QKV"):
                            turn = (BEFORE[kind], c)
                            pe.wait_ge(slot_free, freed[turn])
                            for f in range(NPAIR[kind]):
                                if kind == "GU":
                                    halves = [([(w, xt_hi), (w, xt_lo)], f) for w in (wg16, wu16)]
                                elif kind == "UP":
                                    halves = [([(w1_16, xt_hi), (w1_16, xt_lo)], 2 * f + i) for i in range(2)]
                                else:
                                    halves = [([(wl_hi, xt_hi), (wl_hi, xt_lo), (wl_lo, xt_hi)], 2 * f + i) for i in range(2)]
                                blocks(s, halves, f)
                        elif kind in ("DOWN1", "DOWN3"):
                            hid = (BEFORE[kind], c)
                            n, w = hiddens[hid], wd16 if kind == "DOWN1" else w2_16
                            ps = take_slot(s)
                            pe.wait_ge(lo_done, FB * (n + 1))
                            pe.wait_ge(hi_done, FB * (n + 1))
                            for i in range(TC):
                                rows = slice(i * P, (i + 1) * P)
                                for f in range(FB):
                                    for h in (h_hi, h_lo):
                                        last = nc.tensor.matmul(ps[:, i * D:(i + 1) * D], h[:, n % 2, f, rows], w[:, f, :],
                                                                start=f == 0 and h is h_hi, stop=f == FB - 1 and h is h_lo)
                            last.then_inc(slot_made, 1)
                        elif kind == "BACK":
                            ps = take_slot(s)
                            pe.wait_ge(q_scaled, c // CB + 1)
                            for i in range(TC):
                                for k in range(KC):
                                    last = nc.tensor.transpose(ps[:, i * D + k * P:i * D + (k + 1) * P],
                                                               qt[:, k, (TC * c + i) * P:(TC * c + i + 1) * P], ident[:])
                            last.then_inc(slot_made, 1)

                @block.scalar
                def _(act):
                    for s in ORDER:
                        kind, c = s
                        if kind.startswith("TURN"):
                            act.wait_ge(slot_made, slot_use[s] + 1)
                            if turns[s] >= 2:
                                prev = [p for p in products if turns[(BEFORE[p[0]], p[1])] == turns[s] - 2][0]
                                act.wait_ge(pair_made, pair_use[prev + (NPAIR[prev[0]] - 1,)] + 1)
                            nc.scalar.activation(xt_hi[:, turns[s] % 2].rearrange("p k n -> p (k n)"), slot_of(s)[:],
                                                 ACT.Copy).then_inc(turn_hi, 1)
                        elif kind == "GU":
                            n = hiddens[s]
                            for f in range(FB):
                                u = list_gu.index((c, f))
                                act.wait_ge(pair_made, pair_use[s + (f,)] + 1)
                                if u >= 2:
                                    act.wait_ge(h32_done, hcount[("GU", list_gu[u - 2][0], list_gu[u - 2][1])])
                                nc.scalar.activation(act_out[:, u % 2, :], pair_of(s + (f,))[:, 0, :], ACT.Silu,
                                                     scale=sg_sb[:, f:f + 1]).then_inc(silu_done, 1)
                                if f >= 1:
                                    high_half(act, n, f - 1, s)
                            high_half(act, n, FB - 1, s)
                        elif kind == "UP":
                            for f in range(FB):
                                key, m = s + (f // 2,), hcount[s + (f,)] - 1
                                act.wait_ge(pair_made, pair_use[key] + 1)
                                if m >= 3:
                                    act.wait_ge(lo_done, m - 2)
                                gelu = nc.scalar.activation(h32[:, m % 3, :], pair_of(key)[:, f % 2, :], ACT.Gelu,
                                                            bias=b1_sb[:, f:f + 1], scale=1.0 / XS)
                                gelu.then_inc(h32_done, 1)
                        elif kind == "QKV":
                            sc = 1.0 / (XS * WS)
                            for f in range(2):
                                act.wait_ge(pair_made, pair_use[s + (f,)] + 1)
                                for i in range(2):
                                    bias = bl_sb[:, 2 * f + i:2 * f + i + 1]
                                    src = pair_of(s + (f,))[:, i, :]
                                    if f == 0:
                                        nc.scalar.activation(qt[:, i, c * CH:(c + 1) * CH], src, ACT.Identity, bias=bias, scale=sc)
                                    else:
                                        if c >= 1:
                                            act.wait_ge(kv_done, 2 * (c - 1) + i + 1)
                                        nc.scalar.activation(kt32[:, i, :], src, ACT.Identity, bias=bias, scale=sc).then_inc(k_done, 1)
                                    if 4 * c + 2 * f + i:
                                        act.wait_ge(q_done, 4 * c + 2 * f + i)
                                    nc.scalar.activation(sq_junk[:], src, ACT.Square, bias=bias, scale=sc,
                                                         accum_out=sums[:, f, i, c:c + 1]).then_inc(q_done, 1)

                @block.gpsimd
                def _(pool):
                    def rstd(var, dst, scale, done):
                        then(pool, "pool", nc.gpsimd.tensor_scalar(dst, var, EPS, None, ALU.add))
                        last = nc.gpsimd.tensor_tensor(dst, dst, minus_half[:, 0:TC], ALU.pow)
                        if scale != 1.0:
                            then(pool, "pool", last)
                            last = nc.gpsimd.tensor_scalar(dst, dst, scale, None, ALU.mult)
                        last.then_inc(done, 1)

                    for s in ORDER:
                        kind, c = s
                        if kind.startswith("OUT"):
                            pool.wait_ge(out_stats, outs[s] + 1)
                            rstd(mv_o[:, :, 1], rstd_o[:], 1.0, out_rstd)
                        elif kind.startswith("LN"):
                            pool.wait_ge(x_stats, lns[s] + 1)
                            rstd(mv_x[:, :, 1], rstd_x[:], XS, x_rstd)
                        elif kind in ("GU", "UP"):
                            n = hiddens[s]
                            for f in range(FB):
                                m = hcount[s + (f,)]
                                pool.wait_ge(hi_done, m)
                                if n >= 2 and f == 0:
                                    pool.wait_ge(slot_made, down_slot[n - 2])
                                nc.gpsimd.tensor_tensor(h_lo[:, n % 2, f, :], h32[:, (m - 1) % 3, :], h_hi[:, n % 2, f, :],
                                                        ALU.subtract).then_inc(lo_done, 1)
                        elif kind == "QKV" and c % CB == CB - 1:
                            b = c // CB
                            pool.wait_ge(q_done, 4 * (c + 1))
                            pool.wait_ge(kv_done, 2 * (c + 1))
                            t = tot[:, b]
                            then(pool, "pool", nc.gpsimd.tensor_tensor(t, sums[:, :, :, CB * b], sums[:, :, :, CB * b + 1], ALU.add))
                            half = minus_half[:, 0:2 * KC].rearrange("p (a k) -> p a k", a=2)
                            then(pool, "pool", nc.gpsimd.tensor_tensor(t[:, 0:2], t[:, 0:2], half, ALU.pow))
                            then(pool, "pool", nc.gpsimd.tensor_tensor(t[:, 2], t[:, 2], t[:, 1], ALU.mult))
                            nc.gpsimd.tensor_tensor(t[:, 2], t[:, 2], t[:, 0], ALU.mult).then_inc(factor_done, 1)

                @block.vector
                def _(dve):
                    for s in ORDER:
                        kind, c = s
                        tiles = range(TC * c, TC * (c + 1))
                        if kind.startswith("OUT"):
                            src_stage = (BEFORE[kind], c)
                            ps = slot_of(src_stage)
                            src = ps[:].rearrange("p (i d) -> p i d", d=D)
                            dve.wait_ge(slot_made, slot_use[src_stage] + 1)
                            if outs[s]:
                                dve.wait_ge(x_final, outs[s])
                            if kind == "OUT1":
                                then(dve, "dve", nc.vector.tensor_tensor(y[:], src, sd_b[:].unsqueeze(1).broadcast_to([P, TC, D]), ALU.mult))
                                src = y
                            if kind == "OUT3":
                                then(dve, "dve", nc.vector.tensor_tensor(y[:], src, b2_b[:].unsqueeze(1).broadcast_to([P, TC, D]), ALU.add))
                                src = y
                            ln_rows(dve, None, mv_o, stats, [src[:, i, :] for i in range(TC)]).then_inc(out_stats, 1)
                            dve.wait_ge(out_rstd, outs[s] + 1)
                            dve.wait_ge(out_stats, outs[s] + 1)
                            for i in range(TC):
                                last = nc.vector.tensor_scalar(y[:, i, :], src[:, i, :], mv_o[:, i, 0:1], rstd_o[:, i:i + 1],
                                                               ALU.subtract, ALU.mult)
                            last.then_inc(slot_free, 1)
                            dve.wait_ge(slot_free, freed[src_stage])
                            xs = x[:, TC * c:TC * (c + 1), :]
                            add = nc.vector.tensor_tensor(xs, xs, y[:], ALU.add)
                            add.then_inc(x_final, 1)
                        elif kind.startswith("LN"):
                            dve.wait_ge(x_final, outs[(BEFORE[kind], c)] + 1)
                            ln_rows(dve, None, mv_x, stats, [x[:, t, :] for t in tiles]).then_inc(x_stats, 1)
                            dve.wait_ge(x_rstd, lns[s] + 1)
                            dve.wait_ge(x_stats, lns[s] + 1)
                            if lns[s] >= 2:
                                dve.wait_ge(slot_made, xn_turned[lns[s] - 2])
                            for i, t in enumerate(tiles):
                                last = nc.vector.tensor_scalar(xn[:, lns[s] % 2, i, :], x[:, t, :], mv_x[:, i, 0:1], rstd_x[:, i:i + 1],
                                                               ALU.subtract, ALU.mult)
                            last.then_inc(xn_ready, 1)
                        elif kind.startswith("TURN"):
                            dve.wait_ge(turn_hi, turns[s] + 1)
                            par = turns[s] % 2
                            nc.vector.tensor_tensor(xt_lo[:, par].rearrange("p k n -> p (k n)"), slot_of(s)[:],
                                                    xt_hi[:, par].rearrange("p k n -> p (k n)"), ALU.subtract).then_inc(slot_free, 1)
                        elif kind == "GU":
                            for f in range(FB):
                                m = hcount[s + (f,)]
                                dve.wait_ge(silu_done, list_gu.index((c, f)) + 1)
                                if m >= 4:
                                    dve.wait_ge(lo_done, m - 3)
                                nc.vector.scalar_tensor_tensor(h32[:, (m - 1) % 3, :], pair_of(s + (f,))[:, 1, :], su_sb[:, f:f + 1],
                                                               act_out[:, list_gu.index((c, f)) % 2, :], ALU.mult,
                                                               ALU.mult).then_inc(h32_done, 1)
                        elif kind == "UP":
                            for f in range(FB):
                                high_half(dve, hiddens[s], f, s)
                        elif kind == "QKV":
                            dve.wait_ge(pair_made, pair_use[s + (2,)] + 1)
                            for i in range(2):
                                if c >= 1:
                                    dve.wait_ge(kv_done, 2 * (c - 1) + i + 1)
                                then(dve, "dve", nc.vector.tensor_scalar(vt32[:, i, :], pair_of(s + (2,))[:, i, :], 1.0 / (XS * WS),
                                                                         bl_sb[:, 4 + i:5 + i], ALU.mult, ALU.add))
                                dve.wait_ge(k_done, 2 * c + i + 1)
                                if 2 * c + i:
                                    dve.wait_ge(kv_done, 2 * c + i)
                                nc.vector.tensor_tensor_reduce(kv_junk[:], vt32[:, i, :], kt32[:, i, :], 1.0, 0.0, ALU.mult, ALU.add,
                                                               sums[:, 2, i, c:c + 1]).then_inc(kv_done, 1)
                            if c % CB == CB - 1:
                                b = c // CB
                                dve.wait_ge(factor_done, b + 1)
                                for k in range(KC):
                                    q = qt[:, k, b * S:(b + 1) * S]
                                    last = nc.vector.tensor_scalar(q, q, tot[:, b, 2, k:k + 1], None, ALU.mult)
                                last.then_inc(q_scaled, 1)

                @block.sync
                def _(sp):
                    n = 0
                    for s in ORDER:
                        if s[0] == "OUT3":
                            n += 1
                            sp.wait_ge(x_final, outs[s] + 1)
                            dst = out.rearrange("b (n p) d -> p (b n) d", p=P)[:, TC * s[1]:TC * (s[1] + 1), :]
                            sp.dma_start(dst, x[:, TC * s[1]:TC * (s[1] + 1), :]).then_inc(stored, 16)
                    sp.wait_ge(stored, 16 * n)


def kernel(**inputs):
    import numpy as np
    import concourse.bacc as bacc
    from concourse import mybir as mb
    from concourse.bass_utils import run_bass_kernel_spmd

    a = {k: np.asarray(v) for k, v in inputs.items()}

    def columns(v):
        return np.ascontiguousarray(v.reshape(-1, 128).T)

    def words(v):
        return np.ascontiguousarray(v).view(np.int32)

    arrays = {
        "x": a["L0_attn_X"],
        "wq": a["L0_attn_Wq"].T, "wk": a["L0_attn_Wk"].T, "wv": a["L0_attn_Wv"].T, "wo": a["L0_attn_Wo"].T,
        "bqk": np.concatenate([columns(a["L0_attn_bq"]), columns(a["L0_attn_bk"])], axis=1),
        "bv": a["L0_attn_bv"], "bo": a["L0_attn_bo"].reshape(1, -1),
        "wg": words(a["L0_ffn_w_gate"]), "wu": words(a["L0_ffn_w_up"]), "wd": words(a["L0_ffn_w_down"]),
        "sg": columns(a["L0_ffn_s_gate"]), "su": columns(a["L0_ffn_s_up"]), "sd": a["L0_ffn_s_down"],
        "w2": a["L1_attn_W"], "b2qkv": columns(a["L1_attn_b"]),
        "w1t": a["L1_ffn_w1"].T, "b1": columns(a["L1_ffn_b1"]), "w2t": a["L1_ffn_w2"].T, "b2": a["L1_ffn_b2"],
    }
    nc = bacc.Bacc("TRN2", target_bir_lowering=False, num_devices=1)
    fed, args = {}, []
    for name, v in arrays.items():
        v = np.ascontiguousarray(v)
        fed[f"in_{name}"] = v
        args.append(nc.dram_tensor(f"in_{name}", list(v.shape), mb.dt.from_np(v.dtype), kind="ExternalInput").ap())
    shape = a["L0_attn_X"].shape
    out = nc.dram_tensor("out_x", list(shape), mb.dt.float32, kind="ExternalOutput").ap()
    sandwich(nc, *args, out)
    return run_bass_kernel_spmd(nc, [fed], core_ids=[0]).results[0]["out_x"]
```

```python
from contextlib import ExitStack

import numpy as np
from concourse import mybir

F32 = mybir.dt.float32
F16 = mybir.dt.float16
BF16 = mybir.dt.bfloat16
I8 = mybir.dt.int8
ALU = mybir.AluOpType
ACT = mybir.ActivationFunctionType
AX_X = mybir.AxisListType.X

P = 128
HEADS = 16
QUAD = 4
BANK = 512
EPS = 1e-5
QUANT_EPS = 1e-8
XS = 16.0
WS = 64.0
QS = 16.0
FS = 1.0 / 16.0
BIG = 3.0e38
TWICE_QQ = float(np.array([QS * QS] * 2, np.float16).view(np.float32)[0])


class Tally:

    def __init__(self, sem, step=1):
        self.sem, self.step, self.count, self.value = sem, step, 0, {}

    def mark(self, *key):
        self.count += self.step
        self.value[key] = self.count


def sandwich(nc, x_in, wq, wk, wv, wo, bqk, bv, bo, wg, wu, wd, sg, su, sd, w2, b2qkv, w1t, b1, w2t, b2, out):
    B, S, D = x_in.shape
    TOK = B * S
    NT = TOK // P
    CH = BANK
    TC = CH // P
    NC = TOK // CH
    CB = S // CH
    KC = D // P
    DH = D // HEADS
    INTER = 4 * wg.shape[1]
    FB = INTER // P
    NQ = HEADS // QUAD
    NQUADS = B * NQ
    KT = S // P
    NST = 3
    assert D == KC * P and DH * 8 == P and QUAD * 32 == P and CB == 2 and NC == 4

    whole = ExitStack()
    with whole:
        def sem(name):
            return whole.enter_context(nc.semaphore(name))

        def sb(stack, name, shape, dt):
            return stack.enter_context(nc.sbuf_tensor(name, shape, dt))

        def pb(stack, name, shape, dt):
            return stack.enter_context(nc.psum_tensor(name, shape, dt))

        x = sb(whole, "x", [P, NT, D], F32)
        ident = sb(whole, "ident", [P, P], F32)
        wo_pad = sb(whole, "wo_pad", [P, NQ, D], F32)
        wg16 = sb(whole, "wg16", [P, KC, INTER], F16)
        wu16 = sb(whole, "wu16", [P, KC, INTER], F16)
        wd16 = sb(whole, "wd16", [P, FB, D], F16)
        w1_16 = sb(whole, "w1_16", [P, KC, INTER], F16)
        w2_16 = sb(whole, "w2_16", [P, FB, D], F16)
        wl_hi = sb(whole, "wl_hi", [P, KC, 3 * D], F16)
        wl_lo = sb(whole, "wl_lo", [P, KC, 3 * D], F16)
        sg_sb = sb(whole, "sg_sb", [P, FB], F32)
        su_sb = sb(whole, "su_sb", [P, FB], F32)
        b1_sb = sb(whole, "b1_sb", [P, FB], F32)
        bl_sb = sb(whole, "bl_sb", [P, 3 * KC], F32)
        sd_b = sb(whole, "sd_b", [P, D], F32)
        b2_b = sb(whole, "b2_b", [P, D], F32)
        attn = sb(whole, "attn", [P, NQ, TOK], F32)
        minus_half = sb(whole, "minus_half", [P, 8], F32)
        xn = sb(whole, "xn", [P, 2, TC, D], F32)
        y = sb(whole, "y", [P, TC, D], F32)
        t32 = y[:].rearrange("p i d -> p (i d)").rearrange("p (a c) -> p a c", a=2)
        stats_o = sb(whole, "stats_o", [P, TC, 6], F32)
        stats_x = sb(whole, "stats_x", [P, TC, 6], F32)
        mv_o = sb(whole, "mv_o", [P, TC, 2], F32)
        rstd_o = sb(whole, "rstd_o", [P, TC], F32)
        mv_x = sb(whole, "mv_x", [P, TC, 2], F32)
        rstd_x = sb(whole, "rstd_x", [P, TC], F32)
        scratch = nc.dram_tensor("qk_scratch", [4, D, TOK], F16, kind="Internal")
        den_scr = nc.dram_tensor("den_scratch", [NQUADS, QUAD, S], F32, kind="Internal")
        rec_scr = nc.dram_tensor("rec_scratch", [NQUADS, QUAD, S], F32, kind="Internal")

        x_loaded = [sem(f"x_loaded{c}") for c in range(NC)]
        qkv_w_loaded = sem("qkv_w_loaded")
        wl_loaded = sem("wl_loaded")
        i8_loaded = sem("i8_loaded")
        tern_loaded = sem("tern_loaded")
        wo_zero = sem("wo_zero")
        wo_loaded = sem("wo_loaded")
        small_loaded = sem("small_loaded")
        consts = sem("consts")
        dve_step = sem("dve_step")
        pool_step = sem("pool_step")
        act_step = sem("act_step")
        qk_stored = [sem(f"qk_stored{c}") for c in range(TOK // BANK)]
        steps = {"dve": 0, "pool": 0, "act": 0}
        step_sem = {"dve": dve_step, "pool": pool_step, "act": act_step}

        def then(engine, name, instruction):
            steps[name] += 1
            instruction.then_inc(step_sem[name], 1)
            engine.wait_ge(step_sem[name], steps[name])

        def ln_rows(dve, mv, stats, tiles):
            for i, t in enumerate(tiles):
                last = nc.vector.bn_stats(stats[:, i, :], t)
            then(dve, "dve", last)
            for i in range(len(tiles)):
                last = nc.vector.bn_aggr(mv[:, i, :], stats[:, i, :])
            return last

        life = ExitStack()
        if True:
            VW = DH + 1
            pairs_of_stacks = [(sb(life, f"q_st{i}", [P, QUAD, S], F16), sb(life, f"k_st{i}", [P, QUAD, S], F16)) for i in (0, 2, 1)]
            q_st, k_st = ([pairs_of_stacks[i][n] for i in (0, 2, 1)] for n in range(2))
            v_aug = sb(life, "v_aug", [P, NT, HEADS * VW + 32 - VW], F32)
            mask = sb(life, "mask", [P, BANK], F32)
            junk = sb(life, "junk", [P, 2, CH], BF16)
            parts = sb(life, "parts", [P, 2, QUAD, 12], F32)
            rowmax = sb(life, "rowmax", [P, 2, QUAD, KT], F32)
            max_hi = sb(life, "max_hi", [QUAD * KT, 2, P], F16)
            max_lo = sb(life, "max_lo", [QUAD * KT, 2, P], F16)

            with ExitStack() as ph:
                w0_hi = sb(ph, "w0_hi", [P, KC, 3 * D], F16)
                w0_lo = sb(ph, "w0_lo", [P, KC, 3 * D], F16)
                wlf = sb(ph, "wlf", [P, KC, 3 * D], F32)
                w12f = attn[:, 0:2, :]
                below = attn[:, 2, :]
                w0f = attn[:, 3, 0:KC * 3 * D].rearrange("p (k n) -> p k n", k=KC)
                i8_words = attn[:, 3, 0:3 * 512].bitcast(mybir.dt.int32).rearrange("p (w n) -> p w n", w=3)
                i8 = i8_words.bitcast(I8)
                assert TOK == KC * INTER
                bqk_sb = sb(ph, "bqk_sb", [P, 4], F32)
                bqk16 = sb(ph, "bqk16", [P, 4], F32)
                bv_b = sb(ph, "bv_b", [P, D], F32)
                ones = sb(ph, "ones", [P, P], F32)
                wsum = sb(ph, "wsum", [P, 2], F32)
                thr = sb(ph, "thr", [P, 2, 2], F32)
                stats = sb(ph, "stats", [P, TC, 6], F32)
                mv = sb(ph, "mv", [P, 2, TC, 2], F32)
                rstd = sb(ph, "rstd", [P, 2, TC], F32)
                xt_hi = sb(ph, "xt_hi", [P, 2, KC, CH], F16)
                xt_lo = sb(ph, "xt_lo", [P, 2, KC, CH], F16)
                qk16 = sb(ph, "qk16", [P, 2, 4, KC, CH], F16)
                ps_t = pb(ph, "ps_t", [P, 2, KC, CH], F32)
                ps_v = pb(ph, "ps_v", [P, TC, D], F32)
                ps_q = pb(ph, "ps_q", [P, 2, CH], F32)

                stats_done = sem("p0_stats_done")
                rstd_done = sem("p0_rstd_done")
                xn_done = sem("p0_xn_done")
                turned = sem("p0_turned")
                xt_hi_done = sem("p0_xt_hi_done")
                xt_lo_done = sem("p0_xt_lo_done")
                w0_hi_done = sem("w0_hi_done")
                w0_done = sem("w0_done")
                qk_made = sem("qk_made")
                qk_t32 = sem("qk_t32")
                qk_hi = sem("qk_hi")
                qk_lo = sem("qk_lo")
                v_made = sem("v_made")
                v_done = sem("v_done")
                wsum_done = sem("wsum_done")
                wsum_all = sem("wsum_all")
                wl_hi_done = sem("wl_hi_done")
                bq_done = sem("bq_done")

                with nc.Block() as block:
                    @block.sync
                    def _(sp):
                        def load_x(c):
                            src = x_in.rearrange("b (n p) d -> p (b n) d", p=P)[:, TC * c:TC * (c + 1), :]
                            sp.dma_start(x[:, TC * c:TC * (c + 1), :], src).then_inc(x_loaded[c], 16)
                        load_x(0)
                        for n, w in enumerate((wq, wk, wv)):
                            sp.dma_start(w0f[:, :, n * D:(n + 1) * D],
                                         w.rearrange("(k p) n -> p k n", p=P)).then_inc(qkv_w_loaded, 16)
                        for c in range(1, NC):
                            load_x(c)
                        sp.wait_ge(w0_done, 1)
                        for n, w in enumerate((wg, wu, wd)):
                            sp.dma_start(i8_words[:, n, :].rearrange("p (k n) -> p k n", n=w.shape[1]),
                                          w.rearrange("(k p) n -> p k n", p=P)).then_inc(i8_loaded, 16)
                        for c in range(NC):
                            for a in range(4):
                                for m in range(KC):
                                    sp.wait_ge(qk_lo, 4 * c + 2 * (a // 2) + m + 1)
                                    sp.dma_start(scratch[a, m * P:(m + 1) * P, c * CH:(c + 1) * CH],
                                                 qk16[:, c % 2, a, m, :]).then_inc(qk_stored[c], 16)

                    @block.gpsimd
                    def _(pool):
                        nc.gpsimd.memset(ident[:], 0.0).then_inc(pool_step, 1)
                        steps["pool"] += 1
                        pool.wait_ge(pool_step, steps["pool"])
                        nc.gpsimd.affine_select(out=ident[:], in_=ident[:], compare_op=ALU.not_equal, fill=1.0,
                                                base=0, pattern=[[-1, P]], channel_multiplier=1).then_inc(consts, 1)
                        nc.gpsimd.memset(minus_half[:], -0.5).then_inc(consts, 1)
                        nc.gpsimd.memset(ones[:], 1.0).then_inc(consts, 1)
                        pool.wait_ge(consts, 3)

                        def rstd_of(c):
                            pool.wait_ge(stats_done, c + 1)
                            if c >= 2:
                                pool.wait_ge(xn_done, c - 1)
                            r = rstd[:, c % 2, :]
                            then(pool, "pool", nc.gpsimd.tensor_scalar(r, mv[:, c % 2, :, 1], EPS, None, ALU.add))
                            then(pool, "pool", nc.gpsimd.tensor_tensor(r, r, minus_half[:, 0:TC], ALU.pow))
                            nc.gpsimd.tensor_scalar(r, r, XS, None, ALU.mult).then_inc(rstd_done, 1)

                        rstd_of(0)
                        rstd_of(1)
                        nc.gpsimd.memset(v_aug[:], 1.0).then_inc(consts, 1)
                        for t in (*q_st, *k_st):
                            last = nc.gpsimd.memset(t[:].rearrange("p a b -> p (a b)").bitcast(F32), 0.0)
                        then(pool, "pool", last)
                        for t in k_st:
                            last = nc.gpsimd.memset(t[64:66].rearrange("p a b -> p (a b)").bitcast(F32), TWICE_QQ)
                        then(pool, "pool", last)
                        for c in range(NC):
                            if c + 2 < NC:
                                rstd_of(c + 2)
                            for u in range(4):
                                n = 4 * c + u
                                pool.wait_ge(qk_hi, n + 1)
                                if c >= 2:
                                    pool.wait_ge(qk_stored[c - 2], 16 * 8)
                                nc.gpsimd.tensor_tensor(qk16[:, c % 2, 2 * (u // 2) + 1, u % 2, :], t32[:, n % 2, :],
                                                        qk16[:, c % 2, 2 * (u // 2), u % 2, :],
                                                        ALU.subtract).then_inc(qk_lo, 1)
                        nc.gpsimd.memset(mask[:], 0.0).then_inc(consts, 1)
                        pool.wait_ge(consts, 5)
                        nc.gpsimd.affine_select(out=mask[:, BANK - P:BANK], in_=mask[:, BANK - P:BANK],
                                                compare_op=ALU.is_ge, fill=-BIG, base=0, pattern=[[-1, P]],
                                                channel_multiplier=1).then_inc(consts, 1)

                    @block.scalar
                    def _(act):
                        act.dma_start(bqk_sb[:], bqk).then_inc(small_loaded, 16)
                        act.dma_start(bv_b[:], bv.partition_broadcast(P)).then_inc(small_loaded, 16)
                        for dst, src in ((sg_sb, sg), (su_sb, su), (b1_sb, b1), (bl_sb, b2qkv)):
                            act.dma_start(dst[:], src).then_inc(small_loaded, 16)
                        act.dma_start(sd_b[:], sd.partition_broadcast(P)).then_inc(small_loaded, 16)
                        act.dma_start(b2_b[:], b2.partition_broadcast(P)).then_inc(small_loaded, 16)
                        act.dma_start(wlf[:], w2.rearrange("(k p) n -> p k n", p=P)).then_inc(wl_loaded, 16)
                        act.dma_start(w12f[:, 0, :].rearrange("p (k n) -> p k n", k=KC),
                                      w1t.rearrange("(k p) n -> p k n", p=P)).then_inc(tern_loaded, 16)
                        act.dma_start(w12f[:, 1, :].rearrange("p (k n) -> p k n", k=FB),
                                      w2t.rearrange("(k p) n -> p k n", p=P)).then_inc(tern_loaded, 16)
                        act.wait_ge(wo_zero, 1)
                        for h in range(QUAD):
                            act.dma_start(wo_pad[32 * h:32 * h + DH, :, :],
                                          wo.rearrange("(g h d) n -> h d g n", h=QUAD, d=DH)[h]).then_inc(wo_loaded, 16)
                        act.dma_start(wo_pad[DH:DH + 1, 0, :], bo).then_inc(wo_loaded, 16)

                        act.wait_ge(qkv_w_loaded, 48)
                        nc.scalar.activation(w0_hi[:], w0f, ACT.Copy, scale=WS).then_inc(w0_hi_done, 1)

                        def high(c):
                            act.wait_ge(turned, c + 1)
                            if c >= 2:
                                act.wait_ge(v_made, c - 1)
                            nc.scalar.activation(xt_hi[:, c % 2], ps_t[:, c % 2], ACT.Copy).then_inc(xt_hi_done, 1)

                        high(0)
                        act.wait_ge(bq_done, 1)
                        for c in range(NC):
                            for u in range(4):
                                n = 4 * c + u
                                if u == 1 and c + 1 < NC:
                                    high(c + 1)
                                act.wait_ge(qk_made, n + 1)
                                if n >= 2:
                                    act.wait_ge(qk_lo, n - 1)
                                nc.scalar.activation(t32[:, n % 2, :], ps_q[:, u % 2, :], ACT.Identity, bias=bqk16[:, u:u + 1],
                                                     scale=QS / (XS * WS)).then_inc(qk_t32, 1)
                                act.wait_ge(qk_t32, n + 1)
                                if c >= 2:
                                    act.wait_ge(qk_stored[c - 2], 16 * 8)
                                nc.scalar.activation(qk16[:, c % 2, 2 * (u // 2), u % 2, :], t32[:, n % 2, :],
                                                     ACT.Copy).then_inc(qk_hi, 1)
                            if c == 0:
                                act.wait_ge(wl_loaded, 16)
                                nc.scalar.activation(wl_hi[:], wlf[:], ACT.Copy, scale=WS).then_inc(wl_hi_done, 1)
                            if c == 1:
                                act.wait_ge(tern_loaded, 32)
                                for n in range(2):
                                    then(act, "act", nc.scalar.activation(below, w12f[:, n, :], ACT.Abs,
                                                                          accum_out=wsum[:, n:n + 1]))
                            if c == 2:
                                act.wait_ge(i8_loaded, 48)
                                nc.scalar.activation(wg16[:].rearrange("p a b -> p (a b)"), i8[:, 0, :], ACT.Copy)
                                nc.scalar.activation(wu16[:].rearrange("p a b -> p (a b)"), i8[:, 1, :], ACT.Copy)
                                nc.scalar.activation(wd16[:].rearrange("p a b -> p (a b)"), i8[:, 2, :], ACT.Copy)

                    @block.tensor
                    def _(pe):
                        pe.wait_ge(consts, 3)

                        def turn(c):
                            pe.wait_ge(xn_done, c + 1)
                            if c >= 2:
                                pe.wait_ge(xt_lo_done, c - 1)
                            for i in range(TC):
                                for k in range(KC):
                                    last = nc.tensor.transpose(ps_t[:, c % 2, k, i * P:(i + 1) * P],
                                                               xn[:, c % 2, i, k * P:(k + 1) * P], ident[:])
                            last.then_inc(turned, 1)

                        turn(0)
                        for c in range(NC):
                            if c + 1 < NC:
                                turn(c + 1)
                            if c == 0:
                                pe.wait_ge(w0_done, 1)
                            pe.wait_ge(xt_lo_done, c + 1)
                            hi, lo = xt_hi[:, c % 2], xt_lo[:, c % 2]
                            for u in range(4):
                                n = 4 * c + u
                                if n >= 2:
                                    pe.wait_ge(qk_t32, n - 1)
                                cols = slice(u * P, (u + 1) * P)
                                terms = [(w, r, k) for k in range(KC) for w, r in ((w0_hi, hi), (w0_hi, lo), (w0_lo, hi))]
                                for j, (w, r, k) in enumerate(terms):
                                    last = nc.tensor.matmul(ps_q[:, u % 2, :], w[:, k, cols], r[:, k, :],
                                                            start=j == 0, stop=j == len(terms) - 1)
                                last.then_inc(qk_made, 1)
                            if c >= 1:
                                pe.wait_ge(v_done, c)
                            for i in range(TC):
                                rows = slice(i * P, (i + 1) * P)
                                terms = [(r, w, k) for k in range(KC) for r, w in ((hi, w0_hi), (hi, w0_lo), (lo, w0_hi))]
                                for j, (r, w, k) in enumerate(terms):
                                    last = nc.tensor.matmul(ps_v[:, i, :], r[:, k, rows], w[:, k, 2 * D:3 * D],
                                                            start=j == 0, stop=j == len(terms) - 1)
                            last.then_inc(v_made, 1)
                            if c == NC - 2:
                                pe.wait_ge(act_step, 2)
                                nc.tensor.matmul(ps_t[:, c % 2, 0, 0:2], ones[:], wsum[:], start=True,
                                                 stop=True).then_inc(wsum_all, 1)

                    @block.vector
                    def _(dve):
                        def ln(c):
                            dve.wait_ge(x_loaded[c], 16)
                            if c >= 2:
                                dve.wait_ge(rstd_done, c - 1)
                            ln_rows(dve, mv[:, c % 2], stats,
                                    [x[:, TC * c + i, :] for i in range(TC)]).then_inc(stats_done, 1)

                        def normalise(c):
                            dve.wait_ge(rstd_done, c + 1)
                            dve.wait_ge(stats_done, c + 1)
                            if c >= 2:
                                dve.wait_ge(turned, c - 1)
                            for i in range(TC):
                                last = nc.vector.tensor_scalar(xn[:, c % 2, i, :], x[:, TC * c + i, :], mv[:, c % 2, i, 0:1],
                                                               rstd[:, c % 2, i:i + 1], ALU.subtract, ALU.mult)
                            last.then_inc(xn_done, 1)

                        ln(0)
                        nc.vector.memset(wo_pad[:], 0.0).then_inc(wo_zero, 1)
                        dve.wait_ge(small_loaded, 128)
                        nc.vector.tensor_scalar(bqk16[:], bqk_sb[:], QS, None, ALU.mult).then_inc(bq_done, 1)
                        normalise(0)
                        ln(1)
                        dve.wait_ge(w0_hi_done, 1)
                        nc.vector.scalar_tensor_tensor(w0_lo[:].rearrange("p a b -> p (a b)"), w0f.rearrange("p a b -> p (a b)"),
                                                       WS, w0_hi[:].rearrange("p a b -> p (a b)"),
                                                       ALU.mult, ALU.subtract).then_inc(w0_done, 1)
                        normalise(1)

                        def low(c):
                            dve.wait_ge(xt_hi_done, c + 1)
                            if c >= 2:
                                dve.wait_ge(v_made, c - 1)
                            nc.vector.tensor_tensor(xt_lo[:, c % 2], ps_t[:, c % 2], xt_hi[:, c % 2], ALU.subtract).then_inc(xt_lo_done, 1)

                        low(0)
                        for c in range(NC):
                            if c + 2 < NC:
                                ln(c + 2)
                            if c + 1 < NC:
                                low(c + 1)
                            if c + 2 < NC:
                                normalise(c + 2)
                            dve.wait_ge(v_made, c + 1)
                            if c == 0:
                                dve.wait_ge(consts, 4)
                            for i in range(TC):
                                last = nc.vector.scalar_tensor_tensor(
                                    v_aug[:, TC * c + i, 0:HEADS * VW].rearrange("p (h e) -> p h e", e=VW)[:, :, 0:DH],
                                    ps_v[:, i, :].rearrange("p (h d) -> p h d", d=DH),
                                    1.0 / (XS * WS), bv_b[:].rearrange("p (h d) -> p h d", d=DH), ALU.mult, ALU.add)
                            last.then_inc(v_done, 1)
                            if c == 0:
                                dve.wait_ge(wl_hi_done, 1)
                                nc.vector.scalar_tensor_tensor(wl_lo[:].rearrange("p a b -> p (a b)"), wlf[:].rearrange("p a b -> p (a b)"),
                                                               WS, wl_hi[:].rearrange("p a b -> p (a b)"), ALU.mult, ALU.subtract)
                            if c == NC - 2:
                                dve.wait_ge(wsum_all, 1)
                                then(dve, "dve", nc.vector.tensor_scalar(thr[:, 0, :], ps_t[:, (NC - 2) % 2, 0, 0:2], 1.0 / (D * INTER), QUANT_EPS,
                                                                         ALU.mult, ALU.max))
                                then(dve, "dve", nc.vector.tensor_scalar(thr[:, 1, :], thr[:, 0, :], -0.5, None, ALU.mult))
                                nc.vector.tensor_scalar(thr[:, 0, :], thr[:, 0, :], 0.5, None, ALU.mult).then_inc(wsum_done, 1)
                                dve.wait_ge(wsum_done, 1)
                                dve.wait_ge(act_step, 2)
                                for n, dst in enumerate((w1_16, w2_16)):
                                    then(dve, "dve", nc.vector.tensor_scalar(below, w12f[:, n, :], thr[:, 1, n:n + 1], None, ALU.is_lt))
                                    then(dve, "dve", nc.vector.scalar_tensor_tensor(
                                        dst[:].rearrange("p a b -> p (a b)"), w12f[:, n, :], thr[:, 0, n:n + 1], below,
                                        ALU.is_gt, ALU.subtract))
                        nc.vector.tensor_scalar(sg_sb[:], sg_sb[:], 1.0 / XS, None, ALU.mult)
                        nc.vector.tensor_scalar(su_sb[:], su_sb[:], FS / XS, None, ALU.mult)
                        nc.vector.tensor_scalar(sd_b[:], sd_b[:], 1.0 / FS, None, ALU.mult)


        ps = pb(whole, "ps", [P, 8, BANK], F32)

        ph = ExitStack()
        probs = sb(ph, "probs", [P, 3, QUAD, CH], F32)
        o_sb = sb(ph, "o_sb", [P, 2, S], F32)
        den = sb(ph, "den", [P, 2, 32], F32)
        rec_b = sb(ph, "rec_b", [P, 2, S], F32)
        ps_s = ps[:, 0:4, :].rearrange("p (a b) n -> p a b n", a=2)
        ps_m = ps[:, 4:7, :]
        ps_o = ps[:, 7, :]

        PIECES = [(t, p) for t in range(KT) for p in range(t // TC + 1)]
        NP = len(PIECES)
        MAXES = QUAD * NP
        UNITS = [(c, j) for c in range(CB) for j in range(TC * (c + 1))]
        NU = len(UNITS)
        DIAGS = [u for u, (c, j) in enumerate(UNITS) if j >= TC * c]
        LEAD = 3
        LAG = 2

        stacks_in = [sem(f"stacks_in{i}") for i in range(NST)]
        max_made = sem("max_made")
        max_read = sem("max_read")
        max_full = sem("max_full")
        max_turned = sem("max_turned")
        max_split = sem("max_split")
        max_rows_in = [sem(f"max_rows_in{i}") for i in range(2)]
        scores_made = sem("scores_made")
        exp_done = sem("exp_done")
        masked = sem("masked")
        pv_done = sem("pv_done")
        o_copied = sem("o_copied")
        den_out = sem("den_out")
        den_in = sem("den_in")
        rec_done = sem("rec_done")
        rec_out = sem("rec_out")
        rec_in = [sem(f"rec_in{i}") for i in range(2)]
        attn_done = sem("attn_done")

        def width(u):
            c, j = UNITS[u]
            first = max(CH * c, P * j)
            return first, CH * (c + 1) - first

        def max_slot(i, n):
            return (i * (MAXES + 1) + n) % 3

        ph.close()
        life.close()
        ph = whole
        NH, NA = 6, 4
        xt_hi = sb(ph, "xt_hi2", [P, 2, KC, CH], F16)
        xt_lo = sb(ph, "xt_lo2", [P, 2, KC, CH], F16)
        act_out = sb(ph, "act_out", [P, NA, CH], F32)
        h32 = sb(ph, "h32", [P, NH, CH], F32)
        h_hi = sb(ph, "h_hi", [P, 2, FB, CH], F16)
        h_lo = sb(ph, "h_lo", [P, 2, FB, CH], F16)
        qt = sb(ph, "qt", [P, KC, TOK], F32)
        kt32 = sb(ph, "kt32", [P, 2, CH], F32)
        vt32 = sb(ph, "vt32", [P, 2, CH], F32)
        sums = sb(ph, "sums", [P, 3, KC, NC], F32)
        tot = sb(ph, "tot", [P, B, 3, KC], F32)
        sq_junk = sb(ph, "sq_junk", [P, CH], BF16)
        kv_junk = sb(ph, "kv_junk", [P, CH], BF16)
        ps_slot = [ps[:, 4 + 2 * i:6 + 2 * i, :].rearrange("p a n -> p (a n)") for i in range(2)]
        ps_blk = [ps[:, 2 * i:2 * i + 2, :] for i in range(2)]

        ORDER = []
        for word in (
                "WO:0.0 WO:0.1 WO:0.2 WO:0.3 STAT0:0 ADD0:0 LNS1:0 LNN1:0 TURN1:0 WO:1.0 WO:1.1 RECIP:7 WO:1.2 STAT0:1 "
                "WO:1.3 GU:0.0 GU:0.1 NORM:7 ADD0:1 GU:0.2 GU:0.3 WO:2.0 LNS1:1 WO:2.1 LNN1:1 GU:0.4 WO:2.2 GU:0.5 "
                "STAT0:2 WO:2.3 TURN1:1 GU:0.6 GU:0.7 ADD0:2 GU:1.0 GU:1.1 DOWN1:0.0 GU:1.2 WO:3.0 GU:1.3 DOWN1:0.1 "
                "LNS1:2 STAT1:0 DOWN1:0.2 DOWN1:0.3 LNN1:2 WO:3.1 ADD1:0 WO:3.2 GU:1.4 STAT0:3 WO:3.3 GU:1.5 TURN1:2 "
                "GU:1.6 GU:1.7 GU:2.0 GU:2.1 ADD0:3 LNS1:3 GU:2.2 GU:2.3 DOWN1:1.0 DOWN1:1.1 DOWN1:1.2 LNN1:3 DOWN1:1.3 "
                "LNS2:0 STAT1:1 GU:2.4 LNN2:0 GU:2.5 TURN1:3 GU:2.6 GU:2.7 GU:3.0 ADD1:1 GU:3.1 GU:3.2 TURN2:0 GU:3.3 "
                "GU:3.4 LNS2:1 DOWN1:2.0 GU:3.5 GU:3.6 GU:3.7 DOWN1:2.1 DOWN1:2.2 DOWN1:2.3 DOWN1:3.0 QKV:0.0 LNN2:1 "
                "DOWN1:3.1 STAT1:2 DOWN1:3.2 QKV:0.1 ADD1:2 DOWN1:3.3 LNS2:2 STAT1:3 TURN2:1 QKV:0.2 QKV:1.0 QKV:1.1 "
                "ADD1:3 LNN2:2 LNS2:3 QKV:1.2 LNN2:3 TURN2:2 FACTOR:0 STAT2:0 TURN2:3 BACK:0 ADD2:0 QKV:2.0 BACK:1 LNS3:0 "
                "STAT2:1 LNN3:0 QKV:2.1 QKV:2.2 ADD2:1 QKV:3.0 TURN3:0 QKV:3.1 LNS3:1 QKV:3.2 UP:0.0 LNN3:1 FACTOR:1 "
                "UP:0.1 STAT2:2 UP:0.2 BACK:2 TURN3:1 UP:0.3 ADD2:2 UP:1.0 LNS3:2 STAT2:3 UP:1.1 LNN3:2 BACK:3 ADD2:3 "
                "UP:1.2 DOWN3:0.0 UP:1.3 DOWN3:0.1 TURN3:2 LNS3:3 STAT3:0 DOWN3:0.2 LNN3:3 DOWN3:0.3 UP:2.0 ADD3:0 UP:2.1 "
                "UP:2.2 UP:2.3 TURN3:3 DOWN3:1.0 DOWN3:1.1 DOWN3:1.2 UP:3.0 DOWN3:1.3 UP:3.1 STAT3:1 UP:3.2 UP:3.3 "
                "DOWN3:2.0 ADD3:1 DOWN3:2.1 DOWN3:2.2 DOWN3:2.3 DOWN3:3.0 STAT3:2 ADD3:2 STAT3:3 DOWN3:3.1 DOWN3:3.2 "
                "ADD3:3 DOWN3:3.3 ").split():
            kind, at = word.split(":")
            ORDER.append((kind, *(int(n) for n in at.split("."))))
        LAST = NU * (NQUADS - 1)
        EARLY_TILE = {LAST + u: i for i, u in enumerate((0, 1, 2, 3))}
        EARLY_TURN = LAST + 9
        FIRST, LATE = ORDER[:TC + 5], ORDER[TC + 5:]
        assert FIRST[0][0] == "WO" and FIRST[-1][0] == "TURN1"
        SLOTTED = ("WO", "TURN1", "DOWN1", "TURN2", "BACK", "TURN3", "DOWN3")
        TILED = ("WO", "DOWN1", "DOWN3")
        slot_use = {s[0:2]: n for n, s in enumerate(s for s in ORDER if s[0] in SLOTTED and s[2:] in ((), (0,)))}
        filled = {s[0:2]: n + 1 for n, s in enumerate(
            s for s in ORDER if s[0] in SLOTTED and s[2:] == ((TC - 1,) if s[0] in TILED else ()))}
        NPAIR = {"GU": FB, "QKV": 3, "UP": FB // 2}
        BLOCKED = [s for s in ORDER if s[0] in NPAIR]
        pair_use = {s: n for n, s in enumerate(BLOCKED)}

        def numbered(*kinds):
            return {s: n for n, s in enumerate(s for s in ORDER if s[0].rstrip("0123") in kinds)}

        outs, lns, turns = numbered("STAT"), numbered("LNN"), numbered("TURN")
        adds = {("STAT" + s[0][-1], s[1]): n + 1 for s, n in numbered("ADD").items()}
        HIDDEN = [(s[0], s[1], f) for s in BLOCKED if s[0] != "QKV"
                  for f in ((s[2],) if s[0] == "GU" else (2 * s[2], 2 * s[2] + 1))]
        hidden = {key: m for m, key in enumerate(HIDDEN)}
        hiddens = {s: n for n, s in enumerate(dict.fromkeys(key[0:2] for key in HIDDEN))}
        BEFORE = {"LNS1": "STAT0", "LNS2": "STAT1", "LNS3": "STAT2", "GU": "TURN1", "QKV": "TURN2", "UP": "TURN3",
                  "STAT0": "WO", "STAT1": "DOWN1", "STAT2": "BACK", "STAT3": "DOWN3", "DOWN1": "GU", "DOWN3": "UP"}
        used = {n: s for s, n in slot_use.items()}
        freed = {}
        for s in ORDER:
            if s[0].startswith("ADD"):
                freed[(BEFORE["STAT" + s[0][-1]], s[1])] = len(freed) + 1
            elif s[0].startswith("TURN"):
                freed[s] = len(freed) + 1
        down_made = {hiddens[(BEFORE[kind], c)]: made for (kind, c), made in filled.items() if kind.startswith("DOWN")}

        def with_lag(kind, lag):
            mine = [m for m, key in enumerate(HIDDEN) if key[0] == kind]
            due, n = {}, 0
            for s in ORDER:
                if s[0] == kind:
                    upto = hidden[(kind, s[1], s[2] if kind == "GU" else 2 * s[2] + 1)] - lag
                elif s[0].startswith("DOWN") and BEFORE[s[0]] == kind and s[2] == 0:
                    upto = hidden[(kind, s[1], FB - 1)]
                else:
                    continue
                due[s] = [m for m in mine[n:] if m <= upto]
                n += len(due[s])
            return due

        GATED = with_lag("GU", 0)
        HIGH = with_lag("GU", 1) | with_lag("UP", 2)
        LOW = with_lag("GU", 2) | with_lag("UP", 2)
        xn_turned = [filled[t] for t in turns]

        def high_half(engine, m):
            n = hiddens[HIDDEN[m][0:2]]
            engine.wait_ge(h32_done, m + 1)
            if n >= 2 and HIDDEN[m][2] == 0:
                engine.wait_ge(slot_made, down_made[n - 2])
            src, dst = h32[:, m % NH, :], h_hi[:, n % 2, HIDDEN[m][2], :]
            if HIDDEN[m][0] == "GU":
                nc.scalar.activation(dst, src, ACT.Copy).then_inc(hi_done, 1)
            else:
                nc.vector.tensor_copy(dst, src).then_inc(hi_done, 1)

        slot_made = sem("slot_made")
        slot_free = sem("slot_free")
        pair_made = sem("pair_made")
        out_stats = sem("out_stats")
        out_rstd = sem("out_rstd")
        x_stats = sem("x_stats")
        x_rstd = sem("x_rstd")
        xn_ready = sem("xn_ready")
        turn_hi = sem("turn_hi")
        product_done = sem("product_done")
        silu_done = sem("silu_done")
        h32_done = sem("h32_done")
        hi_done = sem("hi_done")
        lo_done = sem("lo_done")
        down_done = sem("down_done")
        k_done = sem("k_done")
        q_done = sem("q_done")
        kv_done = sem("kv_done")
        factor_done = sem("factor_done")
        q_scaled = sem("q_scaled")
        x_final = sem("x_final")
        stored = sem("stored")

        pair_freed = {}
        for key, n in pair_use.items():
            kind, c, f = key
            if kind == "GU":
                pair_freed[n] = (h32_done, hidden[key] + 1)
            elif kind == "UP":
                pair_freed[n] = (h32_done, hidden[(kind, c, 2 * f + 1)] + 1)
            elif f < 2:
                pair_freed[n] = (q_done, 4 * c + 2 * f + 2)
            else:
                pair_freed[n] = (kv_done, 2 * (c + 1))

        def slot_index(n):
            return 0 if n < 2 else n % 2

        def slot_of(s):
            return ps_slot[slot_index(slot_use[s[0:2]])]

        def pair_of(key):
            return ps_blk[pair_use[key] % 2]

        with nc.Block() as block:
            @block.sync
            def _(sp):
                def stacks(i):
                    b, g = i // NQ, i % NQ
                    if i % NQ == 0:
                        for c in range(CB * b, CB * (b + 1)):
                            sp.wait_ge(qk_stored[c], 16 * 8)
                    if i >= NST:
                        sp.wait_ge(scores_made, 2 * NU * (i - NST + 1))
                    rows = scratch[:, g * QUAD * DH:(g + 1) * QUAD * DH, b * S:(b + 1) * S]\
                        .rearrange("a (h d) t -> a d h t", d=DH)
                    for r, (a_q, a_k) in enumerate(((0, 2), (0, 3), (1, 2), (1, 3))):
                        for st, a in ((q_st, a_q), (k_st, a_k)):
                            sp.dma_start(st[i % NST][r * DH:(r + 1) * DH], rows[a]).then_inc(stacks_in[i % NST], 16)

                def max_rows(i):
                    sp.wait_ge(max_split, i + 1)
                    for r, part in enumerate((max_hi, max_lo)):
                        sp.dma_start(q_st[i % NST][64 + r:65 + r].rearrange("o h (t n) -> o (h t) n", n=P),
                                     part[:, i % 2, :]).then_inc(max_rows_in[i % 2], 16)

                def denominators(i):
                    sp.wait_ge(o_copied, CB * (i + 1))
                    for h in range(QUAD):
                        sp.dma_start(den_scr[i, h:h + 1, :], o_sb[32 * h + DH:32 * h + DH + 1, i % 2, :])\
                            .then_inc(den_out, 16)
                    sp.wait_ge(den_out, 16 * QUAD * (i + 1))
                    sp.dma_start(den[:, i % 2, :], den_scr[i].rearrange("h (a b) -> (h a) b", b=32)).then_inc(den_in, 16)
                    sp.wait_ge(rec_done, i + 1)
                    sp.dma_start(rec_scr[i].rearrange("h (a b) -> (h a) b", b=32), den[:, i % 2, :]).then_inc(rec_out, 16)
                    sp.wait_ge(rec_out, 16 * (i + 1))
                    if i >= 2:
                        sp.wait_ge(attn_done, i - 1)
                    for h in range(QUAD):
                        sp.dma_start(rec_b[32 * h:32 * h + 32, i % 2, :],
                                     rec_scr[i, h, :].partition_broadcast(32)).then_inc(rec_in[i % 2], 16)

                for i in range(NST):
                    stacks(i)
                max_rows(0)
                for i in range(NQUADS):
                    if i >= 1 and i + NST - 1 < NQUADS:
                        stacks(i + NST - 1)
                    if i >= 1:
                        denominators(i - 1)
                    if i + 1 < NQUADS:
                        max_rows(i + 1)
                denominators(NQUADS - 1)
                n = 0
                for s in ORDER:
                    if s[0] == "ADD3":
                        n += 1
                        sp.wait_ge(x_final, adds[("STAT3", s[1])])
                        dst = out.rearrange("b (n p) d -> p (b n) d", p=P)[:, TC * s[1]:TC * (s[1] + 1), :]
                        sp.dma_start(dst, x[:, TC * s[1]:TC * (s[1] + 1), :]).then_inc(stored, 16)
                sp.wait_ge(stored, 16 * n)

            @block.tensor
            def _(pe):
                def take_slot(s):
                    n = slot_use[s[0:2]]
                    if n == 0:
                        pe.wait_ge(max_split, NQUADS)
                    elif n == 3:
                        pe.wait_ge(o_copied, CB * NQUADS)
                    else:
                        pe.wait_ge(slot_free, freed[used[n - 1 if n <= 2 else n - 2]])
                    return slot_of(s)

                def take_pair(key):
                    if pair_use[key] >= 2:
                        pe.wait_ge(*pair_freed[pair_use[key] - 2])
                    elif pair_use[key] == 0:
                        pe.wait_ge(exp_done, 2 * NU * NQUADS)
                    return pair_of(key)

                def blocks(s, halves):
                    par = turns[(BEFORE[s[0]], s[1])] % 2
                    ps = take_pair(s)
                    for i, (terms, col) in enumerate(halves):
                        cols = slice(col * P, (col + 1) * P)
                        jobs = [(w, r, k) for k in range(KC) for w, r in terms]
                        for j, (w, r, k) in enumerate(jobs):
                            last = nc.tensor.matmul(ps[:, i, :], w[:, k, cols], r[:, par, k, :],
                                                    start=j == 0, stop=j == len(jobs) - 1)
                    last.then_inc(pair_made, 1)

                def project(s):
                    c, i = s[1:3]
                    if i == 0:
                        pe.wait_ge(wo_loaded, 16 * (QUAD + 1))
                        pe.wait_ge(attn_done, NQ * (c // CB + 1))
                        take_slot(s)
                    rows = slice((TC * c + i) * P, (TC * c + i + 1) * P)
                    for g in range(NQ):
                        last = nc.tensor.matmul(slot_of(s)[:, i * D:(i + 1) * D], attn[:, g, rows], wo_pad[:, g, :],
                                                start=g == 0, stop=g == NQ - 1)
                    if i == TC - 1:
                        last.then_inc(slot_made, 1)

                def stage(s):
                    kind, c = s[0:2]
                    if kind == "WO":
                        project(s)
                    elif kind.startswith("TURN"):
                        ps = take_slot(s)
                        pe.wait_ge(xn_ready, turns[s] + 1)
                        for i in range(TC):
                            for k in range(KC):
                                last = nc.tensor.transpose(ps[:, k * CH + i * P:k * CH + (i + 1) * P],
                                                           xn[:, turns[s] % 2, i, k * P:(k + 1) * P], ident[:])
                        last.then_inc(slot_made, 1)
                    elif kind in ("GU", "UP", "QKV"):
                        f = s[2]
                        if f == 0:
                            pe.wait_ge(slot_free, freed[(BEFORE[kind], c)])
                        if kind == "GU":
                            blocks(s, [([(w, xt_hi), (w, xt_lo)], f) for w in (wg16, wu16)])
                        elif kind == "UP":
                            blocks(s, [([(w1_16, xt_hi), (w1_16, xt_lo)], 2 * f + i) for i in range(2)])
                        else:
                            blocks(s, [([(wl_hi, xt_hi), (wl_hi, xt_lo), (wl_lo, xt_hi)], 2 * f + i) for i in range(2)])
                    elif kind in ("DOWN1", "DOWN3"):
                        n, w = hiddens[(BEFORE[kind], c)], wd16 if kind == "DOWN1" else w2_16
                        if s[2] == 0:
                            take_slot(s)
                            pe.wait_ge(lo_done, FB * (n + 1))
                            pe.wait_ge(hi_done, FB * (n + 1))
                        i = s[2]
                        for f in range(FB):
                            for h in (h_hi, h_lo):
                                last = nc.tensor.matmul(slot_of(s)[:, i * D:(i + 1) * D], h[:, n % 2, f, i * P:(i + 1) * P],
                                                        w[:, f, :], start=f == 0 and h is h_hi,
                                                        stop=f == FB - 1 and h is h_lo)
                        if i == TC - 1:
                            last.then_inc(slot_made, 1)
                    elif kind == "BACK":
                        ps = take_slot(s)
                        pe.wait_ge(q_scaled, c // CB + 1)
                        for i in range(TC):
                            for k in range(KC):
                                last = nc.tensor.transpose(ps[:, i * D + k * P:i * D + (k + 1) * P],
                                                           qt[:, k, (TC * c + i) * P:(TC * c + i + 1) * P], ident[:])
                        last.then_inc(slot_made, 1)

                def piece(i, n):
                    h, (t, p) = n // NP, PIECES[n % NP]
                    if n == 0:
                        pe.wait_ge(stacks_in[i % NST], 16 * 8 * (i // NST + 1))
                    if n == 2 and i:
                        pe.wait_ge(max_split, i)
                    elif i or n >= 3:
                        pe.wait_ge(max_read, i * MAXES + n - 2 + (1 if n < 2 else 0))
                    keys = slice(CH * p, min(CH * (p + 1), P * (t + 1)))
                    nc.tensor.matmul(ps_m[:, max_slot(i, n), 0:keys.stop - keys.start],
                                     q_st[i % NST][0:64, h, t * P:(t + 1) * P], k_st[i % NST][0:64, h, keys],
                                     start=True, stop=True).then_inc(max_made, 1)

                def turn_max(i):
                    pe.wait_ge(max_full, i + 1)
                    nc.tensor.transpose(ps_m[0:QUAD * KT, max_slot(i, MAXES), 0:P],
                                        rowmax[:, i % 2].rearrange("p h t -> p (h t)"), ident[:]).then_inc(max_turned, 1)

                def scores(i, u, pair):
                    c, j = UNITS[u]
                    first, w = width(u)
                    if u == 0 and pair == 0:
                        pe.wait_ge(max_rows_in[i % 2], 32 * (i // 2 + 1))
                    n = 2 * (i * NU + u) + pair
                    if n >= 2:
                        pe.wait_ge(exp_done, n - 1)
                    for h in range(2):
                        last = nc.tensor.matmul(ps_s[:, pair, h, 0:w], k_st[i % NST][:, 2 * pair + h, j * P:(j + 1) * P],
                                                q_st[i % NST][:, 2 * pair + h, first:first + w], start=True, stop=True)
                    last.then_inc(scores_made, 1)

                def product(i, u):
                    c, j = UNITS[u]
                    first, w = width(u)
                    n = i * NU + u
                    pe.wait_ge(exp_done, 2 * n + 2)
                    if u in DIAGS:
                        pe.wait_ge(masked, i * len(DIAGS) + DIAGS.index(u) + 1)
                    if j == 0 and i * CB + c >= 1:
                        pe.wait_ge(o_copied, i * CB + c)
                    at = first - CH * c
                    tile = (i // NQ) * KT + j
                    for h in range(QUAD):
                        head = QUAD * (i % NQ) + h
                        last = nc.tensor.matmul(ps_o[32 * h:32 * h + 32, at:at + w],
                                                v_aug[:, tile, VW * head:VW * head + 32], probs[:, n % 3, h, 0:w],
                                                start=j == 0, stop=j == TC * (c + 1) - 1)
                    last.then_inc(pv_done, 1)

                def pieces(start, stop):
                    for m in range(start, min(stop, NQUADS * MAXES)):
                        i, k = divmod(m, MAXES)
                        piece(i, k)
                        if k == 1 and i:
                            turn_max(i - 1)
                    if start < NQUADS * MAXES <= stop:
                        turn_max(NQUADS - 1)

                PER = MAXES // NU
                pieces(0, PER * (NU + LEAD))
                assert PER == 4
                for n in range(NQUADS * NU):
                    ahead = PER * (n + NU + LEAD)
                    for pair in range(2):
                        scores(*divmod(n, NU), pair)
                        pieces(ahead + pair, ahead + pair + 1)
                    if n >= LAG:
                        product(*divmod(n - LAG, NU))
                    pieces(ahead + 2, ahead + 4)
                    if n in EARLY_TILE:
                        stage(FIRST[EARLY_TILE[n]])
                    elif n == EARLY_TURN:
                        stage(FIRST[-1])
                for u in range(NU - LAG, NU):
                    product(NQUADS - 1, u)

                for s in LATE:
                    stage(s)

            @block.scalar
            def _(act):
                sc = 1.0 / (XS * WS)
                def stage(s):
                    kind, c = s[0:2]
                    if kind.startswith("TURN"):
                        act.wait_ge(slot_made, filled[s])
                        if turns[s] >= 2:
                            before = max(n for b, n in pair_use.items() if turns[(BEFORE[b[0]], b[1])] == turns[s] - 2)
                            act.wait_ge(pair_made, before + 1)
                        nc.scalar.activation(xt_hi[:, turns[s] % 2].rearrange("p k n -> p (k n)"), slot_of(s),
                                             ACT.Copy).then_inc(turn_hi, 1)
                    elif kind == "GU":
                        f, m = s[2], hidden[s]
                        if m == 0:
                            act.wait_ge(pv_done, NU * NQUADS)
                        act.wait_ge(pair_made, pair_use[s] + 1)
                        if m >= NA:
                            act.wait_ge(h32_done, m - NA + 1)
                        nc.scalar.activation(act_out[:, m % NA, :], pair_of(s)[:, 0, :], ACT.Silu,
                                             scale=sg_sb[:, f:f + 1]).then_inc(silu_done, 1)
                    elif kind == "UP":
                        act.wait_ge(pair_made, pair_use[s] + 1)
                        for f in (2 * s[2], 2 * s[2] + 1):
                            m = hidden[(kind, c, f)]
                            act.wait_ge(lo_done, m - NH + 1)
                            nc.scalar.activation(h32[:, m % NH, :], pair_of(s)[:, f % 2, :], ACT.Gelu,
                                                 bias=b1_sb[:, f:f + 1], scale=1.0 / XS).then_inc(h32_done, 1)
                    elif kind == "QKV" and s[2] < 2:
                        f = s[2]
                        act.wait_ge(pair_made, pair_use[s] + 1)
                        for i in range(2):
                            bias = bl_sb[:, 2 * f + i:2 * f + i + 1]
                            src = pair_of(s)[:, i, :]
                            if f == 0:
                                nc.scalar.activation(qt[:, i, c * CH:(c + 1) * CH], src, ACT.Identity, bias=bias, scale=sc)
                            else:
                                if c >= 1:
                                    act.wait_ge(kv_done, 2 * (c - 1) + i + 1)
                                nc.scalar.activation(kt32[:, i, :], src, ACT.Identity, bias=bias, scale=sc).then_inc(k_done, 1)
                            if 4 * c + 2 * f + i:
                                act.wait_ge(q_done, 4 * c + 2 * f + i)
                            nc.scalar.activation(sq_junk[:], src, ACT.Square, bias=bias, scale=sc,
                                                 accum_out=sums[:, f, i, c:c + 1]).then_inc(q_done, 1)
                    if kind in ("GU", "DOWN1"):
                        for m in HIGH.get(s, ()):
                            high_half(act, m)

                def copy_out(n):
                    i, c = divmod(n, CB)
                    act.wait_ge(pv_done, i * NU + (TC if c == 0 else NU))
                    if i >= 2 and c == 0:
                        act.wait_ge(attn_done, i - 1)
                    nc.scalar.activation(o_sb[:, i % 2, c * CH:(c + 1) * CH], ps_o, ACT.Copy).then_inc(o_copied, 1)

                copied = 0
                for i in range(NQUADS):
                    for u in range(NU):
                        n = i * NU + u
                        first, w = width(u)
                        if n >= 3:
                            act.wait_ge(pv_done, n - 2)
                        for pair in range(2):
                            act.wait_ge(scores_made, 2 * n + pair + 1)
                            nc.scalar.activation(probs[:, n % 3, 2 * pair:2 * pair + 2, 0:w], ps_s[:, pair, :, 0:w],
                                                 ACT.Exp, scale=0.25 / (QS * QS)).then_inc(exp_done, 1)
                        if n == EARLY_TURN:
                            stage(FIRST[-1])
                        if (u == TC - 1 + LAG) or (u == LAG - 1 and i):
                            copy_out(copied)
                            copied += 1
                copy_out(copied)

                for s in LATE:
                    stage(s)

            @block.gpsimd
            def _(pool):
                def rstd(var, dst, scale, done):
                    then(pool, "pool", nc.gpsimd.tensor_scalar(dst, var, EPS, None, ALU.add))
                    last = nc.gpsimd.tensor_tensor(dst, dst, minus_half[:, 0:TC], ALU.pow)
                    if scale != 1.0:
                        then(pool, "pool", last)
                        last = nc.gpsimd.tensor_scalar(dst, dst, scale, None, ALU.mult)
                    last.then_inc(done, 1)

                def stage(s):
                    kind, c = s[0:2]
                    if kind == "NORM":
                        normalise(NQUADS - 1)
                    elif kind.startswith("STAT"):
                        pool.wait_ge(out_stats, outs[s] + 1)
                        rstd(mv_o[:, :, 1], rstd_o[:], 1.0, out_rstd)
                    elif kind.startswith("LNS"):
                        pool.wait_ge(x_stats, lns[("LNN" + kind[-1], c)] + 1)
                        rstd(mv_x[:, :, 1], rstd_x[:], XS, x_rstd)
                    elif kind == "FACTOR":
                        b = c
                        pool.wait_ge(q_done, 4 * CB * (b + 1))
                        pool.wait_ge(kv_done, 2 * CB * (b + 1))
                        t = tot[:, b]
                        then(pool, "pool", nc.gpsimd.tensor_tensor(t, sums[:, :, :, CB * b], sums[:, :, :, CB * b + 1], ALU.add))
                        half = minus_half[:, 0:2 * KC].rearrange("p (a k) -> p a k", a=2)
                        then(pool, "pool", nc.gpsimd.tensor_tensor(t[:, 0:2], t[:, 0:2], half, ALU.pow))
                        then(pool, "pool", nc.gpsimd.tensor_tensor(t[:, 2], t[:, 2], t[:, 1], ALU.mult))
                        nc.gpsimd.tensor_tensor(t[:, 2], t[:, 2], t[:, 0], ALU.mult).then_inc(factor_done, 1)
                    for m in LOW.get(s, ()):
                        n, f = hiddens[HIDDEN[m][0:2]], HIDDEN[m][2]
                        pool.wait_ge(hi_done, m + 1)
                        if n >= 2 and f == 0:
                            pool.wait_ge(slot_made, down_made[n - 2])
                        nc.gpsimd.tensor_tensor(h_lo[:, n % 2, f, :], h32[:, m % NH, :], h_hi[:, n % 2, f, :],
                                                ALU.subtract).then_inc(lo_done, 1)

                def normalise(i):
                    pool.wait_ge(rec_in[i % 2], 16 * QUAD * (i // 2 + 1))
                    pool.wait_ge(o_copied, CB * (i + 1))
                    b, g = i // NQ, i % NQ
                    nc.gpsimd.tensor_tensor(attn[:, g, b * S:(b + 1) * S], o_sb[:, i % 2, :], rec_b[:, i % 2, :],
                                            ALU.mult).then_inc(attn_done, 1)

                for i in range(NQUADS):
                    for k, u in enumerate(DIAGS):
                        n = i * NU + u
                        if i == NQUADS - 1 and k == TC:
                            for s in FIRST:
                                stage(s)
                        pool.wait_ge(exp_done, 2 * n + 2)
                        tri = probs[:, n % 3, :, 0:P]
                        nc.gpsimd.affine_select(out=tri, in_=tri, compare_op=ALU.is_ge, fill=0.0, base=0,
                                                pattern=[[0, QUAD], [1, P]], channel_multiplier=-1).then_inc(masked, 1)
                        if k == len(DIAGS) - 1 and i >= 1:
                            normalise(i - 1)

                for s in LATE:
                    stage(s)

            @block.vector
            def _(dve):
                def stage(s):
                    kind, c = s[0:2]
                    tiles = range(TC * c, TC * (c + 1))
                    if kind == "RECIP":
                        reciprocals(NQUADS - 1)
                    elif kind.startswith("STAT"):
                        source = (BEFORE[kind], c)
                        src = slot_of(source).rearrange("p (i d) -> p i d", d=D)
                        dve.wait_ge(slot_made, filled[source])
                        if outs[s]:
                            dve.wait_ge(x_final, outs[s])
                        if kind == "STAT1":
                            then(dve, "dve", nc.vector.tensor_tensor(y[:], src, sd_b[:].unsqueeze(1).broadcast_to([P, TC, D]), ALU.mult))
                            src = y
                        if kind == "STAT3":
                            then(dve, "dve", nc.vector.tensor_tensor(y[:], src, b2_b[:].unsqueeze(1).broadcast_to([P, TC, D]), ALU.add))
                            src = y
                        ln_rows(dve, mv_o, stats_o, [src[:, i, :] for i in range(TC)]).then_inc(out_stats, 1)
                    elif kind.startswith("ADD"):
                        stat = ("STAT" + kind[-1], c)
                        source = (BEFORE[stat[0]], c)
                        src = y if kind[-1] in "13" else slot_of(source).rearrange("p (i d) -> p i d", d=D)
                        dve.wait_ge(out_rstd, outs[stat] + 1)
                        dve.wait_ge(out_stats, outs[stat] + 1)
                        for i in range(TC):
                            last = nc.vector.tensor_scalar(y[:, i, :], src[:, i, :], mv_o[:, i, 0:1], rstd_o[:, i:i + 1],
                                                           ALU.subtract, ALU.mult)
                        last.then_inc(slot_free, 1)
                        dve.wait_ge(slot_free, freed[source])
                        xs = x[:, TC * c:TC * (c + 1), :]
                        nc.vector.tensor_tensor(xs, xs, y[:], ALU.add).then_inc(x_final, 1)
                    elif kind.startswith("LNS"):
                        dve.wait_ge(x_final, adds[(BEFORE[kind], c)])
                        ln_rows(dve, mv_x, stats_x, [x[:, t, :] for t in tiles]).then_inc(x_stats, 1)
                    elif kind.startswith("LNN"):
                        dve.wait_ge(x_rstd, lns[s] + 1)
                        dve.wait_ge(x_stats, lns[s] + 1)
                        if lns[s] >= 2:
                            dve.wait_ge(slot_made, xn_turned[lns[s] - 2])
                        for i, t in enumerate(tiles):
                            last = nc.vector.tensor_scalar(xn[:, lns[s] % 2, i, :], x[:, t, :], mv_x[:, i, 0:1],
                                                           rstd_x[:, i:i + 1], ALU.subtract, ALU.mult)
                        last.then_inc(xn_ready, 1)
                    elif kind.startswith("TURN"):
                        dve.wait_ge(turn_hi, turns[s] + 1)
                        par = turns[s] % 2
                        nc.vector.tensor_tensor(xt_lo[:, par].rearrange("p k n -> p (k n)"), slot_of(s),
                                                xt_hi[:, par].rearrange("p k n -> p (k n)"), ALU.subtract).then_inc(slot_free, 1)
                    elif kind == "QKV" and s[2] == 2:
                        dve.wait_ge(pair_made, pair_use[s] + 1)
                        for i in range(2):
                            if c >= 1:
                                dve.wait_ge(kv_done, 2 * (c - 1) + i + 1)
                            then(dve, "dve", nc.vector.tensor_scalar(vt32[:, i, :], pair_of(s)[:, i, :], 1.0 / (XS * WS),
                                                                     bl_sb[:, 4 + i:5 + i], ALU.mult, ALU.add))
                            dve.wait_ge(k_done, 2 * c + i + 1)
                            if 2 * c + i:
                                dve.wait_ge(kv_done, 2 * c + i)
                            nc.vector.tensor_tensor_reduce(kv_junk[:], vt32[:, i, :], kt32[:, i, :], 1.0, 0.0, ALU.mult, ALU.add,
                                                           sums[:, 2, i, c:c + 1]).then_inc(kv_done, 1)
                    elif kind == "FACTOR":
                        dve.wait_ge(factor_done, c + 1)
                        for k in range(KC):
                            q = qt[:, k, c * S:(c + 1) * S]
                            last = nc.vector.tensor_scalar(q, q, tot[:, c, 2, k:k + 1], None, ALU.mult)
                        last.then_inc(q_scaled, 1)
                    for m in GATED.get(s, ()):
                        f = HIDDEN[m][2]
                        if m == 0:
                            dve.wait_ge(pv_done, NU * NQUADS)
                        dve.wait_ge(silu_done, m + 1)
                        if m >= NH:
                            dve.wait_ge(lo_done, m - NH + 1)
                        nc.vector.scalar_tensor_tensor(h32[:, m % NH, :], pair_of(HIDDEN[m])[:, 1, :], su_sb[:, f:f + 1],
                                                       act_out[:, m % NA, :], ALU.mult, ALU.mult).then_inc(h32_done, 1)
                    if kind in ("UP", "DOWN3"):
                        for m in HIGH.get(s, ()):
                            high_half(dve, m)

                def maxima(i, n):
                    h, (t, p) = n // NP, PIECES[n % NP]
                    w = min(CH, P * (t + 1) - CH * p)
                    dve.wait_ge(max_made, i * MAXES + n + 1)
                    src, dst = ps_m[:, max_slot(i, n), 0:w], parts[:, i % 2, h, n % NP:n % NP + 1]
                    m = i * MAXES + n
                    if p == t // TC:
                        if m >= 2:
                            dve.wait_ge(max_read, m - 1)
                        nc.vector.tensor_tensor_reduce(junk[:, m % 2, 0:w], src, mask[:, CH - w:CH], 1.0, -BIG, ALU.add,
                                                       ALU.max, dst).then_inc(max_read, 1)
                    else:
                        nc.vector.tensor_reduce(dst, src, axis=AX_X, op=ALU.max).then_inc(max_read, 1)

                def finish_max(i):
                    pi, mi = parts[:, i % 2], rowmax[:, i % 2]
                    dve.wait_ge(max_read, MAXES * (i + 1))
                    nc.vector.tensor_copy(mi[:, :, 0:TC], pi[:, :, 0:TC])
                    two = pi[:, :, TC:NP].rearrange("p h (t c) -> p h t c", c=2)
                    nc.vector.tensor_tensor(mi[:, :, TC:KT], two[:, :, :, 0], two[:, :, :, 1], ALU.max).then_inc(max_full, 1)

                def split_max(i):
                    dve.wait_ge(max_turned, i + 1)
                    if i >= 2:
                        dve.wait_ge(max_rows_in[i % 2], 32 * (i // 2))
                    src = ps_m[0:QUAD * KT, max_slot(i, MAXES), 0:P]
                    then(dve, "dve", nc.vector.tensor_scalar(max_hi[:, i % 2, :], src, -1.0 / (QS * QS), None, ALU.mult))
                    nc.vector.scalar_tensor_tensor(max_lo[:, i % 2, :], src, -1.0 / (QS * QS), max_hi[:, i % 2, :],
                                                   ALU.mult, ALU.subtract).then_inc(max_split, 1)

                def reciprocals(i):
                    dve.wait_ge(den_in, 16 * (i + 1))
                    nc.vector.reciprocal(den[:, i % 2, :], den[:, i % 2, :]).then_inc(rec_done, 1)

                for i in range(NQUADS):
                    for n in range(MAXES):
                        maxima(i, n)
                        if n == 1 and i:
                            split_max(i - 1)
                        if n == 3 * NP and i >= 2:
                            reciprocals(i - 2)
                    finish_max(i)
                split_max(NQUADS - 1)
                for s in FIRST:
                    if s[0] == "LNN1":
                        reciprocals(NQUADS - 2)
                    stage(s)

                for s in LATE:
                    stage(s)





def kernel(**inputs):
    import numpy as np
    import concourse.bacc as bacc
    from concourse import mybir as mb
    from concourse.bass_utils import run_bass_kernel_spmd

    a = {k: np.asarray(v) for k, v in inputs.items()}

    def columns(v):
        return np.ascontiguousarray(v.reshape(-1, 128).T)

    def words(v):
        return np.ascontiguousarray(v).view(np.int32)

    arrays = {
        "x": a["L0_attn_X"],
        "wq": a["L0_attn_Wq"].T, "wk": a["L0_attn_Wk"].T, "wv": a["L0_attn_Wv"].T, "wo": a["L0_attn_Wo"].T,
        "bqk": np.concatenate([columns(a["L0_attn_bq"]), columns(a["L0_attn_bk"])], axis=1),
        "bv": a["L0_attn_bv"], "bo": a["L0_attn_bo"].reshape(1, -1),
        "wg": words(a["L0_ffn_w_gate"]), "wu": words(a["L0_ffn_w_up"]), "wd": words(a["L0_ffn_w_down"]),
        "sg": columns(a["L0_ffn_s_gate"]), "su": columns(a["L0_ffn_s_up"]), "sd": a["L0_ffn_s_down"],
        "w2": a["L1_attn_W"], "b2qkv": columns(a["L1_attn_b"]),
        "w1t": a["L1_ffn_w1"].T, "b1": columns(a["L1_ffn_b1"]), "w2t": a["L1_ffn_w2"].T, "b2": a["L1_ffn_b2"],
    }
    nc = bacc.Bacc("TRN2", target_bir_lowering=False, num_devices=1)
    fed, args = {}, []
    for name, v in arrays.items():
        v = np.ascontiguousarray(v)
        fed[f"in_{name}"] = v
        args.append(nc.dram_tensor(f"in_{name}", list(v.shape), mb.dt.from_np(v.dtype), kind="ExternalInput").ap())
    shape = a["L0_attn_X"].shape
    out = nc.dram_tensor("out_x", list(shape), mb.dt.float32, kind="ExternalOutput").ap()
    sandwich(nc, *args, out)
    return run_bass_kernel_spmd(nc, [fed], core_ids=[0]).results[0]["out_x"]
```

```python
from contextlib import ExitStack

import numpy as np
from concourse import mybir

F32 = mybir.dt.float32
F16 = mybir.dt.float16
BF16 = mybir.dt.bfloat16
I8 = mybir.dt.int8
ALU = mybir.AluOpType
ACT = mybir.ActivationFunctionType
AX_X = mybir.AxisListType.X

P = 128
HEADS = 16
QUAD = 4
BANK = 512
EPS = 1e-5
QUANT_EPS = 1e-8
XS = 16.0
WS = 64.0
QS = 16.0
FS = 1.0 / 16.0
BIG = 3.0e38
TWICE_QQ = float(np.array([QS * QS] * 2, np.float16).view(np.float32)[0])


class Tally:

    def __init__(self, sem, step=1):
        self.sem, self.step, self.count, self.value = sem, step, 0, {}

    def mark(self, *key):
        self.count += self.step
        self.value[key] = self.count


def sandwich(nc, x_in, wq, wk, wv, wo, bqk, bv, bo, wg, wu, wd, sg, su, sd, w2, b2qkv, w1t, b1, w2t, b2, out):
    B, S, D = x_in.shape
    TOK = B * S
    NT = TOK // P
    CH = BANK
    TC = CH // P
    NC = TOK // CH
    CB = S // CH
    KC = D // P
    DH = D // HEADS
    INTER = 4 * wg.shape[1]
    FB = INTER // P
    NQ = HEADS // QUAD
    NQUADS = B * NQ
    KT = S // P
    NST = 3
    assert D == KC * P and DH * 8 == P and QUAD * 32 == P and CB == 2 and NC == 4

    whole = ExitStack()
    with whole:
        def sem(name):
            return whole.enter_context(nc.semaphore(name))

        def sb(stack, name, shape, dt):
            return stack.enter_context(nc.sbuf_tensor(name, shape, dt))

        def pb(stack, name, shape, dt):
            return stack.enter_context(nc.psum_tensor(name, shape, dt))

        x = sb(whole, "x", [P, NT, D], F32)
        ident = sb(whole, "ident", [P, P], F32)
        wo_sb = sb(whole, "wo_sb", [P, KC, D], F32)
        bo_b = sb(whole, "bo_b", [P, D], F32)
        wg16 = sb(whole, "wg16", [P, KC, INTER], F16)
        wu16 = sb(whole, "wu16", [P, KC, INTER], F16)
        wd16 = sb(whole, "wd16", [P, FB, D], F16)
        w1_16 = sb(whole, "w1_16", [P, KC, INTER], F16)
        w2_16 = sb(whole, "w2_16", [P, FB, D], F16)
        wl_hi = sb(whole, "wl_hi", [P, KC, 3 * D], F16)
        wl_lo = sb(whole, "wl_lo", [P, KC, 3 * D], F16)
        sg_sb = sb(whole, "sg_sb", [P, FB], F32)
        su_sb = sb(whole, "su_sb", [P, FB], F32)
        b1_sb = sb(whole, "b1_sb", [P, FB], F32)
        bl_sb = sb(whole, "bl_sb", [P, 3 * KC], F32)
        sd_b = sb(whole, "sd_b", [P, D], F32)
        b2_b = sb(whole, "b2_b", [P, D], F32)
        attn = sb(whole, "attn", [P, KC, TOK], F32)
        thr = sb(whole, "thr", [P, 2, 2], F32)
        minus_half = sb(whole, "minus_half", [P, 8], F32)
        xn = sb(whole, "xn", [P, 2, TC, D], F32)
        y = sb(whole, "y", [P, TC, D], F32)
        t32 = y[:].rearrange("p i d -> p (i d)").rearrange("p (a c) -> p a c", a=2)
        stats_o = sb(whole, "stats_o", [P, TC, 6], F32)
        stats_x = sb(whole, "stats_x", [P, TC, 6], F32)
        mv_o = sb(whole, "mv_o", [P, TC, 2], F32)
        rstd_o = sb(whole, "rstd_o", [P, TC], F32)
        mv_x = sb(whole, "mv_x", [P, TC, 2], F32)
        rstd_x = sb(whole, "rstd_x", [P, TC], F32)
        scratch = nc.dram_tensor("qk_scratch", [4, D, TOK], F16, kind="Internal")
        den_scr = nc.dram_tensor("den_scratch", [NQUADS, QUAD, S], F32, kind="Internal")
        rec_scr = nc.dram_tensor("rec_scratch", [NQUADS, QUAD, S], F32, kind="Internal")

        x_loaded = [sem(f"x_loaded{c}") for c in range(NC)]
        qkv_w_loaded = sem("qkv_w_loaded")
        bqk_loaded = sem("bqk_loaded")
        wl_loaded = sem("wl_loaded")
        i8_loaded = sem("i8_loaded")
        tern_loaded = sem("tern_loaded")
        wo_loaded = sem("wo_loaded")
        small_loaded = sem("small_loaded")
        consts = sem("consts")
        dve_step = sem("dve_step")
        pool_step = sem("pool_step")
        act_step = sem("act_step")
        v_ones = sem("v_ones")
        stack_rows = sem("stack_rows")
        mask_made = sem("mask_made")
        qk_stored = [[sem(f"qk_stored{c}_{m}") for m in range(D // P)] for c in range(NC)]
        steps = {"dve": 0, "pool": 0, "act": 0}
        step_sem = {"dve": dve_step, "pool": pool_step, "act": act_step}

        def then(engine, name, instruction):
            steps[name] += 1
            instruction.then_inc(step_sem[name], 1)
            engine.wait_ge(step_sem[name], steps[name])

        def ln_rows(dve, mv, stats, tiles):
            for i, t in enumerate(tiles):
                last = nc.vector.bn_stats(stats[:, i, :], t)
            then(dve, "dve", last)
            for i in range(len(tiles)):
                last = nc.vector.bn_aggr(mv[:, i, :], stats[:, i, :])
            return last

        life = ExitStack()
        VW = DH + 1
        assert (NQUADS - 1) % NST == 1
        stacks_of = {i: (sb(life, f"q_st{i}", [P, QUAD, S], F16), sb(life, f"k_st{i}", [P, QUAD, S], F16)) for i in (0, 2, 1)}
        q_st, k_st = ([stacks_of[i][n] for i in range(NST)] for n in range(2))
        v_aug = sb(life, "v_aug", [P, NT, HEADS * VW + 32 - VW], F32)
        mask = sb(life, "mask", [P, BANK], F32)
        junk = sb(life, "junk", [P, 2, CH], BF16)
        parts = sb(life, "parts", [P, 2, QUAD, 12], F32)
        rowmax = sb(life, "rowmax", [P, 2, QUAD, KT], F32)
        max_hi = sb(life, "max_hi", [QUAD * KT, 2, P], F16)
        max_lo = sb(life, "max_lo", [QUAD * KT, 2, P], F16)
        w12f = sb(life, "w12f", [P, 2, KC * INTER], F32)
        below = sb(life, "below", [P, KC * INTER], F16)

        ps = pb(whole, "ps", [P, 8, BANK], F32)

        ph = ExitStack()
        w0_hi = sb(ph, "w0_hi", [P, KC, 3 * D], F16)
        w0_lo = sb(ph, "w0_lo", [P, KC, 3 * D], F16)
        wlf = sb(ph, "wlf", [P, KC, 3 * D], F32)
        w0f = attn[:, 0, 0:KC * 3 * D].rearrange("p (k n) -> p k n", k=KC)
        i8_words = attn[:, 0, 0:3 * 512].bitcast(mybir.dt.int32).rearrange("p (w n) -> p w n", w=3)
        i8 = i8_words.bitcast(I8)
        assert TOK == KC * INTER
        bqk_sb = sb(ph, "bqk_sb", [P, 4], F32)
        bqk16 = sb(ph, "bqk16", [P, 4], F32)
        bv_b = sb(ph, "bv_b", [P, D], F32)
        ones = sb(ph, "ones", [P, P], F32)
        wsum = sb(ph, "wsum", [P, 2], F32)
        stats0 = sb(ph, "stats0", [P, TC, 6], F32)
        mv0 = sb(ph, "mv0", [P, 2, TC, 2], F32)
        rstd0 = sb(ph, "rstd0", [P, 2, TC], F32)
        xt_hi0 = sb(ph, "xt_hi0", [P, 2, KC, CH], F16)
        xt_lo0 = sb(ph, "xt_lo0", [P, 2, KC, CH], F16)
        qk16 = sb(ph, "qk16", [P, 2, 4, KC, CH], F16)
        ps_t = ps[:, 0:KC, :]
        ps_v = ps[:, 2, :].rearrange("p (i d) -> p i d", i=2)
        ps_q = (ps[:, 3, :], ps[:, 7, :])
        ps_w = ps[:, 6, 0:2]

        stats_done = sem("p0_stats_done")
        rstd_done = sem("p0_rstd_done")
        xn_done = sem("p0_xn_done")
        turned = sem("p0_turned")
        xt_hi_done = sem("p0_xt_hi_done")
        xt_lo_done = sem("p0_xt_lo_done")
        w0_hi_done = sem("w0_hi_done")
        w0_done = sem("w0_done")
        qk_made = sem("qk_made")
        qk_t32 = sem("qk_t32")
        qk_hi = sem("qk_hi")
        qk_lo = sem("qk_lo")
        v_made = sem("v_made")
        v_done = sem("v_done")
        wsum_done = sem("wsum_done")
        wsum_all = sem("wsum_all")
        wl_hi_done = sem("wl_hi_done")
        i8_cast = sem("i8_cast")
        bq_done = sem("bq_done")

        ph.close()
        ph = ExitStack()
        probs = sb(ph, "probs", [P, 3, QUAD, CH], F32)
        o_sb = sb(ph, "o_sb", [P, 2, S], F32)
        den = sb(ph, "den", [P, 2, 32], F32)
        rec_b = sb(ph, "rec_b", [P, 2, S], F32)
        ps_s = ps[:, 0:4, :].rearrange("p (a b) n -> p a b n", a=2)
        ps_m = ps[:, 4:7, :]
        ps_o = ps[:, 7, :]

        PIECES = [(t, p) for t in range(KT) for p in range(t // TC + 1)]
        NP = len(PIECES)
        MAXES = QUAD * NP
        UNITS = [(c, j) for c in range(CB) for j in range(TC * (c + 1))]
        NU = len(UNITS)
        DIAGS = [u for u, (c, j) in enumerate(UNITS) if j >= TC * c]
        PIECES_AT = {(c, u): (0, 0) for c in range(NC) for u in range(4)}
        begun = 0
        for at, upto in (((2, 1), 0), ((2, 2), 6), ((2, 3), 13), ((3, 0), 17), ((3, 1), 23), ((3, 2), 29), ((3, 3), 36)):
            PIECES_AT[at] = (begun, upto)
            begun = upto
        PLAN = ((2, 0, 2), (1, 1, 2), (2, 1, 1), (1, 1, 2), (1, 0, 3), (1, 1, 2),
                (1, 1, 2), (1, 1, 2), (1, 2, 2), (0, 1, 2), (1, 1, 3), (1, 1, 1))
        assert sum(map(sum, PLAN)) == MAXES

        def pieces_by(n, slot):
            i, u = divmod(n, NU)
            return (i + 1) * MAXES + LEAD + sum(map(sum, PLAN[:u])) + sum(PLAN[u][:slot])

        LEAD = 12
        LAG = 2

        stacks_in = [sem(f"stacks_in{i}") for i in range(NST)]
        max_made = sem("max_made")
        max_read = sem("max_read")
        max_full = sem("max_full")
        max_turned = sem("max_turned")
        max_split = sem("max_split")
        max_rows_in = [sem(f"max_rows_in{i}") for i in range(2)]
        scores_made = sem("scores_made")
        exp_done = sem("exp_done")
        masked = sem("masked")
        pv_done = sem("pv_done")
        o_copied = sem("o_copied")
        den_out = sem("den_out")
        den_in = sem("den_in")
        rec_done = sem("rec_done")
        rec_out = sem("rec_out")
        rec_in = [sem(f"rec_in{i}") for i in range(2)]
        attn_done = sem("attn_done")
        attn_in = [sem(f"attn_in{i}") for i in range(2)]

        def width(u):
            c, j = UNITS[u]
            first = max(CH * c, P * j)
            return first, CH * (c + 1) - first

        def max_slot(i, n):
            return (i * (MAXES + 1) + n) % 3

        ph.close()
        life.close()
        ph = whole
        NH, NA = 6, 4
        xt_hi = sb(ph, "xt_hi2", [P, 2, KC, CH], F16)
        xt_lo = sb(ph, "xt_lo2", [P, 2, KC, CH], F16)
        h_lo = sb(ph, "h_lo", [P, 2, FB, CH], F16)
        h_hi = sb(ph, "h_hi", [P, 2, FB, CH], F16)
        act_out = sb(ph, "act_out", [P, NA, CH], F32)
        h32 = sb(ph, "h32", [P, NH, CH], F32)
        qt = sb(ph, "qt", [P, KC, TOK], F32)
        kt32 = sb(ph, "kt32", [P, 2, CH], F32)
        vt32 = sb(ph, "vt32", [P, 2, CH], F32)
        sums = sb(ph, "sums", [P, 3, KC, NC], F32)
        tot = sb(ph, "tot", [P, B, 3, KC], F32)
        sq_junk = sb(ph, "sq_junk", [P, CH], BF16)
        kv_junk = sb(ph, "kv_junk", [P, CH], BF16)
        ps_slot = [ps[:, 4 + 2 * i:6 + 2 * i, :].rearrange("p a n -> p (a n)") for i in range(2)]
        ps_blk = [ps[:, 2 * i:2 * i + 2, :] for i in range(2)]

        ORDER = []
        for word in (
                "WO:0.0 WO:0.1 WO:0.2 WO:0.3 STAT0:0 ADD0:0 LNS1:0 LNN1:0 TURN1:0 LOW1:0 WO:1.0 GU:0.0 WO:1.1 GU:0.1 "
                "WO:1.2 WO:1.3 GU:0.2 RECIP:7 STAT0:1 GU:0.3 GU:0.4 ADD0:1 NORM:7 GU:0.5 LNS1:1 GU:0.6 GU:0.7 TURN1:1 "
                "WO:2.0 WO:2.1 LNN1:1 WO:2.2 LOW1:1 GU:1.0 WO:2.3 GU:1.1 DOWN1:0.0 STAT0:2 GU:1.2 DOWN1:0.1 DOWN1:0.2 "
                "DOWN1:0.3 ADD0:2 GU:1.3 LNS1:2 STAT1:0 WO:3.0 GU:1.4 WO:3.1 WO:3.2 LNN1:2 WO:3.3 ADD1:0 TURN1:2 GU:1.5 "
                "STAT0:3 GU:1.6 LOW1:2 GU:1.7 GU:2.0 GU:2.1 GU:2.2 ADD0:3 GU:2.3 DOWN1:1.0 GU:2.4 DOWN1:1.1 LNS1:3 GU:2.5 "
                "LNN1:3 GU:2.6 TURN1:3 LNS2:0 DOWN1:1.2 GU:2.7 LOW1:3 DOWN1:1.3 LNN2:0 GU:3.0 STAT1:1 GU:3.1 GU:3.2 "
                "ADD1:1 GU:3.3 LNS2:1 TURN2:0 GU:3.4 GU:3.5 DOWN1:2.0 GU:3.6 GU:3.7 DOWN1:2.1 DOWN1:2.2 DOWN1:2.3 LOW2:0 "
                "LNN2:1 DOWN1:3.0 STAT1:2 DOWN1:3.1 ADD1:2 LNS2:2 STAT1:3 LOW2:1 DOWN1:3.2 KV:0 QKV:0.0 QKV:0.1 ADD1:3 "
                "DOWN1:3.3 TURN2:1 QKV:0.2 QKV:1.0 QKV:1.1 QKV:1.2 LNN2:2 TURN2:2 LNS2:3 KV:1 LOW2:2 LNN2:3 QKV:2.0 "
                "BACK:0 FACTOR:0 STAT2:0 TURN2:3 LOW2:3 QKV:2.1 QKV:2.2 ADD2:0 QKV:3.0 KV:2 LNS3:0 BACK:1 STAT2:1 LNN3:0 "
                "QKV:3.1 KV:3 LOW3:0 ADD2:1 QKV:3.2 FACTOR:1 LNS3:1 TURN3:0 STAT2:2 UP:0.0 UP:0.1 LNN3:1 BACK:2 ADD2:2 "
                "UP:0.2 TURN3:1 LOW3:1 UP:0.3 BACK:3 LNS3:2 STAT2:3 UP:1.0 LNN3:2 UP:1.1 ADD2:3 UP:1.2 LNS3:3 LOW3:2 "
                "UP:1.3 TURN3:2 DOWN3:0.0 DOWN3:0.1 DOWN3:0.2 UP:2.0 DOWN3:0.3 LNN3:3 STAT3:0 ADD3:0 UP:2.1 TURN3:3 "
                "UP:2.2 UP:2.3 DOWN3:1.0 DOWN3:1.1 LOW3:3 DOWN3:1.2 UP:3.0 DOWN3:1.3 UP:3.1 DOWN3:2.0 STAT3:1 UP:3.2 "
                "UP:3.3 ADD3:1 DOWN3:2.1 DOWN3:2.2 DOWN3:2.3 DOWN3:3.0 STAT3:2 DOWN3:3.1 ADD3:2 DOWN3:3.2 "
                "DOWN3:3.3 STAT3:3.0 STAT3:3.1 ADD3:3.0 ADD3:3.1 ").split():
            kind, at = word.split(":")
            ORDER.append((kind, *(int(n) for n in at.split("."))))
        LAST = NU * (NQUADS - 1)
        EARLY_TILE = {LAST + u: i for i, u in enumerate((0, 1, 2, 3))}
        EARLY_TURN = LAST + 10
        FIRST, LATE = ORDER[:TC + 6], ORDER[TC + 6:]
        assert FIRST[0][0] == "WO" and FIRST[-2][0] == "TURN1"
        SLOTTED = ("WO", "TURN1", "DOWN1", "TURN2", "BACK", "TURN3", "DOWN3")
        TILED = ("WO", "DOWN1", "DOWN3")
        slot_use = {s[0:2]: n for n, s in enumerate(s for s in ORDER if s[0] in SLOTTED and s[2:] in ((), (0,)))}
        filled = {s[0:2]: n + 1 for n, s in enumerate(
            s for s in ORDER if s[0] in SLOTTED and s[2:] == ((TC - 1,) if s[0] in TILED else ()))}
        NPAIR = {"GU": FB, "QKV": 3, "UP": FB // 2}
        BLOCKED = [s for s in ORDER if s[0] in NPAIR]
        pair_use = {s: n for n, s in enumerate(BLOCKED)}

        def numbered(*kinds):
            return {s: n for n, s in enumerate(s for s in ORDER if s[0].rstrip("0123") in kinds)}

        outs, lns, turns = numbered("STAT"), numbered("LNN"), numbered("TURN")
        adds = {("STAT" + s[0][-1], *s[1:]): n + 1 for s, n in numbered("ADD").items()}

        def part_of(s):
            return slice(0, TC) if len(s) == 2 else slice(TC // 2 * s[2], TC // 2 * (s[2] + 1))

        HIDDEN = [(s[0], s[1], f) for s in BLOCKED if s[0] != "QKV"
                  for f in ((s[2],) if s[0] == "GU" else (2 * s[2], 2 * s[2] + 1))]
        hidden = {key: m for m, key in enumerate(HIDDEN)}
        hiddens = {s: n for n, s in enumerate(dict.fromkeys(key[0:2] for key in HIDDEN))}
        BEFORE = {"LNS1": "STAT0", "LNS2": "STAT1", "LNS3": "STAT2", "GU": "TURN1", "QKV": "TURN2", "UP": "TURN3",
                  "STAT0": "WO", "STAT1": "DOWN1", "STAT2": "BACK", "STAT3": "DOWN3", "DOWN1": "GU", "DOWN3": "UP"}
        used = {n: s for s, n in slot_use.items()}
        freed = {}
        for s in ORDER:
            if s[0].startswith("ADD"):
                freed[(BEFORE["STAT" + s[0][-1]], *s[1:])] = len(freed) + 1
            elif s[0].startswith("LOW"):
                freed[("TURN" + s[0][-1], s[1])] = len(freed) + 1
        down_made = {hiddens[(BEFORE[kind], c)]: made for (kind, c), made in filled.items() if kind.startswith("DOWN")}

        def with_lag(kind, lag):
            mine = [m for m, key in enumerate(HIDDEN) if key[0] == kind]
            due, n = {}, 0
            for s in ORDER:
                if s[0] == kind:
                    upto = hidden[(kind, s[1], s[2] if kind == "GU" else 2 * s[2] + 1)] - lag
                elif s[0].startswith("DOWN") and BEFORE[s[0]] == kind and s[2] == 0:
                    upto = hidden[(kind, s[1], FB - 1)]
                else:
                    continue
                due[s] = [m for m in mine[n:] if m <= upto]
                n += len(due[s])
            return due

        GATED = with_lag("GU", 1)
        HIGH = with_lag("GU", 1) | with_lag("UP", 2)
        LOW = with_lag("GU", 4) | with_lag("UP", 2)
        xn_turned = [filled[t] for t in turns]

        def high_half(engine, m):
            n = hiddens[HIDDEN[m][0:2]]
            engine.wait_ge(h32_done, m + 1)
            if n >= 2 and HIDDEN[m][2] == 0:
                engine.wait_ge(slot_made, down_made[n - 2])
            src, dst = h32[:, m % NH, :], h_hi[:, n % 2, HIDDEN[m][2], :]
            if HIDDEN[m][0] == "GU":
                nc.scalar.activation(dst, src, ACT.Copy).then_inc(hi_done, 1)
            else:
                nc.vector.tensor_copy(dst, src).then_inc(hi_done, 1)

        slot_made = sem("slot_made")
        slot_free = sem("slot_free")
        pair_made = sem("pair_made")
        out_stats = sem("out_stats")
        out_rstd = sem("out_rstd")
        x_stats = sem("x_stats")
        x_rstd = sem("x_rstd")
        xn_ready = sem("xn_ready")
        turn_hi = sem("turn_hi")
        silu_done = sem("silu_done")
        h32_done = sem("h32_done")
        hi_done = sem("hi_done")
        lo_done = sem("lo_done")
        k_done = sem("k_done")
        q_done = sem("q_done")
        kv_done = sem("kv_done")
        factor_done = sem("factor_done")
        q_scaled = sem("q_scaled")
        half_made = sem("half_made")
        x_final = sem("x_final")
        stored = sem("stored")

        pair_freed = {}
        for key, n in pair_use.items():
            kind, c, f = key
            if kind == "GU":
                pair_freed[n] = (h32_done, hidden[key] + 1)
            elif kind == "UP":
                pair_freed[n] = (h32_done, hidden[(kind, c, 2 * f + 1)] + 1)
            elif f < 2:
                pair_freed[n] = (q_done, 4 * c + 2 * f + 2)
            else:
                pair_freed[n] = (kv_done, 2 * (c + 1))

        def slot_index(n):
            return 0 if n < 2 else n % 2

        def slot_of(s):
            return ps_slot[slot_index(slot_use[s[0:2]])]

        def pair_of(key):
            return ps_blk[pair_use[key] % 2]

        with nc.Block() as block:
            @block.sync
            def _(sp):
                def stacks(i):
                    b, g = i // NQ, i % NQ
                    m = g * QUAD * DH // P
                    if i % NQ == m * P // (QUAD * DH):
                        for c in range(CB * b, CB * (b + 1)):
                            sp.wait_ge(qk_stored[c][m], 16 * 2)
                    if i >= NST:
                        sp.wait_ge(scores_made, 2 * NU * (i - NST + 1))
                    rows = scratch[:, g * QUAD * DH:(g + 1) * QUAD * DH, b * S:(b + 1) * S]\
                        .rearrange("a (h d) t -> a d h t", d=DH)
                    for r, (a_q, a_k) in enumerate(((0, 2), (0, 3), (1, 2), (1, 3))):
                        for st, a in ((q_st, a_q), (k_st, a_k)):
                            sp.dma_start(st[i % NST][r * DH:(r + 1) * DH], rows[a]).then_inc(stacks_in[i % NST], 16)

                def max_rows(i):
                    sp.wait_ge(max_split, i + 1)
                    for r, part in enumerate((max_hi, max_lo)):
                        sp.dma_start(q_st[i % NST][64 + r:65 + r].rearrange("o h (t n) -> o (h t) n", n=P),
                                     part[:, i % 2, :]).then_inc(max_rows_in[i % 2], 16)

                def denominators(i):
                    sp.wait_ge(o_copied, CB * (i + 1))
                    sp.dma_start(den_scr[i], o_sb[DH:P:32, i % 2, :]).then_inc(den_out, 16)
                    if i == NQUADS - 1:
                        gather(i - 1)
                    sp.wait_ge(den_out, 16 * (i + 1))
                    sp.dma_start(den[:, i % 2, :], den_scr[i].rearrange("h (a b) -> (h a) b", b=32)).then_inc(den_in, 16)
                    sp.wait_ge(rec_done, i + 1)
                    sp.dma_start(rec_scr[i].rearrange("h (a b) -> (h a) b", b=32), den[:, i % 2, :]).then_inc(rec_out, 16)
                    sp.wait_ge(rec_out, 16 * (i + 1))
                    if i >= 2:
                        sp.wait_ge(attn_done, i - 1)
                    for h in range(QUAD):
                        sp.dma_start(rec_b[32 * h:32 * h + 32, i % 2, :],
                                     rec_scr[i, h, :].partition_broadcast(32)).then_inc(rec_in[i % 2], 16)

                def gather(i):
                    sp.wait_ge(attn_done, i + 1)
                    b, g = divmod(i, NQ)
                    for h in range(QUAD):
                        k, row = divmod((QUAD * g + h) * DH, P)
                        sp.dma_start(attn[row:row + DH, k, b * S:(b + 1) * S], o_sb[32 * h:32 * h + DH, i % 2, :])\
                            .then_inc(attn_in[i % 2], 16)

                def load_x(c):
                    src = x_in.rearrange("b (n p) d -> p (b n) d", p=P)[:, TC * c:TC * (c + 1), :]
                    sp.dma_start(x[:, TC * c:TC * (c + 1), :], src).then_inc(x_loaded[c], 16)

                def store_qk(c, blocks):
                    for u in blocks:
                        a, m = u % 2, u // 2
                        sp.wait_ge(qk_lo, 4 * c + u + 1)
                        sp.dma_start(scratch[2 * a:2 * a + 2, m * P:(m + 1) * P, c * CH:(c + 1) * CH].rearrange("a p n -> p a n"),
                                     qk16[:, c % 2, 2 * a:2 * a + 2, m, :]).then_inc(qk_stored[c][m], 16)

                for c in range(NC):
                    load_x(c)
                for n, (w, blocks) in enumerate(((w1t, KC), (w2t, FB))):
                    sp.dma_start(w12f[:, n, :].rearrange("p (k n) -> p k n", k=blocks),
                                 w.rearrange("(k p) n -> p k n", p=P)).then_inc(tern_loaded, 16)
                sp.dma_start(wlf[:], w2.rearrange("(k p) n -> p k n", p=P)).then_inc(wl_loaded, 16)
                for dst, src in ((sg_sb, sg), (su_sb, su), (b1_sb, b1), (bl_sb, b2qkv)):
                    sp.dma_start(dst[:], src).then_inc(small_loaded, 16)
                for dst, src in ((sd_b, sd), (b2_b, b2)):
                    sp.dma_start(dst[:], src.partition_broadcast(P)).then_inc(small_loaded, 16)
                sp.dma_start(wo_sb[:], wo.rearrange("(k p) n -> p k n", p=P)).then_inc(wo_loaded, 16)
                sp.dma_start(bo_b[:], bo.partition_broadcast(P)).then_inc(small_loaded, 16)
                sp.wait_ge(w0_done, 1)
                for n, w in enumerate((wg, wu, wd)):
                    sp.dma_start(i8_words[:, n, :].rearrange("p (k n) -> p k n", n=w.shape[1]),
                                 w.rearrange("(k p) n -> p k n", p=P)).then_inc(i8_loaded, 16)
                store_qk(0, range(4))
                store_qk(1, range(2))
                stacks(0)
                store_qk(1, range(2, 4))
                stacks(1)
                store_qk(2, range(4))
                stacks(2)
                store_qk(3, range(4))
                max_rows(0)
                for i in range(NQUADS):
                    if i >= 2:
                        gather(i - 2)
                    if i >= 1 and i + NST - 1 < NQUADS:
                        stacks(i + NST - 1)
                    if i >= 1:
                        denominators(i - 1)
                    if i + 1 < NQUADS:
                        max_rows(i + 1)
                denominators(NQUADS - 1)
                gather(NQUADS - 1)
                n = 0
                for s in ORDER:
                    if s[0] == "ADD3":
                        n += 1
                        sp.wait_ge(x_final, adds[("STAT3", *s[1:])])
                        tiles = slice(TC * s[1] + part_of(s).start, TC * s[1] + part_of(s).stop)
                        dst = out.rearrange("b (n p) d -> p (b n) d", p=P)[:, tiles, :]
                        sp.dma_start(dst, x[:, tiles, :]).then_inc(stored, 16)
                sp.wait_ge(stored, 16 * n)

            @block.tensor
            def _(pe):
                def take_slot(s):
                    n = slot_use[s[0:2]]
                    if n == 0:
                        pe.wait_ge(max_split, NQUADS)
                    elif n == 3:
                        pe.wait_ge(o_copied, CB * NQUADS)
                    else:
                        pe.wait_ge(slot_free, freed[used[n - 1 if n <= 2 else n - 2]])
                    return slot_of(s)

                def take_pair(key):
                    if pair_use[key] >= 2:
                        pe.wait_ge(*pair_freed[pair_use[key] - 2])
                    elif pair_use[key] == 0:
                        pe.wait_ge(exp_done, 2 * NU * NQUADS)
                    return pair_of(key)

                def blocks(s, halves):
                    par = turns[(BEFORE[s[0]], s[1])] % 2
                    ps = take_pair(s)
                    for i, (terms, col) in enumerate(halves):
                        cols = slice(col * P, (col + 1) * P)
                        jobs = [(w, r, k) for k in range(KC) for w, r in terms]
                        for j, (w, r, k) in enumerate(jobs):
                            last = nc.tensor.matmul(ps[:, i, :], w[:, k, cols], r[:, par, k, :],
                                                    start=j == 0, stop=j == len(jobs) - 1)
                    last.then_inc(pair_made, 1)

                def project(s):
                    c, i = s[1:3]
                    if i == 0:
                        pe.wait_ge(wo_loaded, 16)
                        for arrived in attn_in:
                            pe.wait_ge(arrived, 16 * QUAD * (NQ // 2) * (c // CB + 1))
                        take_slot(s)
                    rows = slice((TC * c + i) * P, (TC * c + i + 1) * P)
                    for k in range(KC):
                        last = nc.tensor.matmul(slot_of(s)[:, i * D:(i + 1) * D], attn[:, k, rows], wo_sb[:, k, :],
                                                start=k == 0, stop=k == KC - 1)
                    if i == TC - 1:
                        last.then_inc(slot_made, 1)

                def stage(s):
                    kind, c = s[0:2]
                    if kind == "WO":
                        project(s)
                    elif kind.startswith("TURN"):
                        ps = take_slot(s)
                        pe.wait_ge(xn_ready, turns[s] + 1)
                        for i in range(TC):
                            for k in range(KC):
                                last = nc.tensor.transpose(ps[:, k * CH + i * P:k * CH + (i + 1) * P],
                                                           xn[:, turns[s] % 2, i, k * P:(k + 1) * P], ident[:])
                        last.then_inc(slot_made, 1)
                    elif kind in ("GU", "UP", "QKV"):
                        f = s[2]
                        if f == 0:
                            pe.wait_ge(slot_free, freed[(BEFORE[kind], c)])
                        if kind == "GU":
                            blocks(s, [([(w, xt_hi), (w, xt_lo)], f) for w in (wg16, wu16)])
                        elif kind == "UP":
                            blocks(s, [([(w1_16, xt_hi), (w1_16, xt_lo)], 2 * f + i) for i in range(2)])
                        else:
                            blocks(s, [([(wl_hi, xt_hi), (wl_hi, xt_lo), (wl_lo, xt_hi)], 2 * f + i) for i in range(2)])
                    elif kind in ("DOWN1", "DOWN3"):
                        n, w = hiddens[(BEFORE[kind], c)], wd16 if kind == "DOWN1" else w2_16
                        if s[2] == 0:
                            take_slot(s)
                            pe.wait_ge(lo_done, FB * (n + 1))
                            pe.wait_ge(hi_done, FB * (n + 1))
                        i = s[2]
                        for f in range(FB):
                            for h in (h_hi, h_lo):
                                last = nc.tensor.matmul(slot_of(s)[:, i * D:(i + 1) * D], h[:, n % 2, f, i * P:(i + 1) * P],
                                                        w[:, f, :], start=f == 0 and h is h_hi,
                                                        stop=f == FB - 1 and h is h_lo)
                        if s == ("DOWN3", NC - 1, TC // 2 - 1):
                            last.then_inc(half_made, 1)
                        if i == TC - 1:
                            last.then_inc(slot_made, 1)
                    elif kind == "BACK":
                        ps = take_slot(s)
                        pe.wait_ge(q_scaled, c // CB + 1)
                        for i in range(TC):
                            for k in range(KC):
                                last = nc.tensor.transpose(ps[:, i * D + k * P:i * D + (k + 1) * P],
                                                           qt[:, k, (TC * c + i) * P:(TC * c + i + 1) * P], ident[:])
                        last.then_inc(slot_made, 1)

                def piece(i, n):
                    h, (t, p) = n // NP, PIECES[n % NP]
                    if n == 0:
                        pe.wait_ge(stacks_in[i % NST], 16 * 8 * (i // NST + 1))
                    if n == 2 and i == 0:
                        pe.wait_ge(wsum_done, 1)
                    elif n == 2:
                        pe.wait_ge(max_split, i)
                    elif i or n >= 3:
                        pe.wait_ge(max_read, i * MAXES + n - 2 + (1 if n < 2 else 0))
                    keys = slice(CH * p, min(CH * (p + 1), P * (t + 1)))
                    nc.tensor.matmul(ps_m[:, max_slot(i, n), 0:keys.stop - keys.start],
                                     q_st[i % NST][0:64, h, t * P:(t + 1) * P], k_st[i % NST][0:64, h, keys],
                                     start=True, stop=True).then_inc(max_made, 1)

                def turn_max(i):
                    pe.wait_ge(max_full, i + 1)
                    nc.tensor.transpose(ps_m[0:QUAD * KT, max_slot(i, MAXES), 0:P],
                                        rowmax[:, i % 2].rearrange("p h t -> p (h t)"), ident[:]).then_inc(max_turned, 1)

                def scores(i, u, pair):
                    c, j = UNITS[u]
                    first, w = width(u)
                    if u == 0 and pair == 0:
                        pe.wait_ge(max_rows_in[i % 2], 32 * (i // 2 + 1))
                        if i < 2:
                            pe.wait_ge(stack_rows, 1 if i == 0 else NST)
                        if i == 0:
                            pe.wait_ge(xt_lo_done, NC)
                            pe.wait_ge(qk_t32, 4 * NC)
                            pe.wait_ge(v_done, 2 * NC)
                    n = 2 * (i * NU + u) + pair
                    if n >= 2:
                        pe.wait_ge(exp_done, n - 1)
                    for h in range(2):
                        last = nc.tensor.matmul(ps_s[:, pair, h, 0:w], k_st[i % NST][:, 2 * pair + h, j * P:(j + 1) * P],
                                                q_st[i % NST][:, 2 * pair + h, first:first + w], start=True, stop=True)
                    last.then_inc(scores_made, 1)

                def product(i, u):
                    c, j = UNITS[u]
                    first, w = width(u)
                    n = i * NU + u
                    pe.wait_ge(exp_done, 2 * n + 2)
                    if n == 0:
                        pe.wait_ge(v_ones, 2)
                    if u in DIAGS:
                        pe.wait_ge(masked, i * len(DIAGS) + DIAGS.index(u) + 1)
                    if j == 0 and i * CB + c >= 1:
                        pe.wait_ge(o_copied, i * CB + c)
                    at = first - CH * c
                    tile = (i // NQ) * KT + j
                    for h in range(QUAD):
                        head = QUAD * (i % NQ) + h
                        last = nc.tensor.matmul(ps_o[32 * h:32 * h + 32, at:at + w],
                                                v_aug[:, tile, VW * head:VW * head + 32], probs[:, n % 3, h, 0:w],
                                                start=j == 0, stop=j == TC * (c + 1) - 1)
                    last.then_inc(pv_done, 1)

                issued = [0]

                def pieces(stop):
                    start, stop = issued[0], min(stop, NQUADS * MAXES)
                    issued[0] = max(start, stop)
                    for m in range(start, stop):
                        i, k = divmod(m, MAXES)
                        piece(i, k)
                        if k == 1 and i:
                            turn_max(i - 1)
                    if start < NQUADS * MAXES <= stop:
                        turn_max(NQUADS - 1)

                def turn(c):
                    pe.wait_ge(xn_done, c + 1)
                    pe.wait_ge(consts, 3)
                    if c >= 1:
                        pe.wait_ge(xt_lo_done, c)
                    for i in range(TC):
                        for k in range(KC):
                            last = nc.tensor.transpose(ps_t[:, k, i * P:(i + 1) * P], xn[:, c % 2, i, k * P:(k + 1) * P],
                                                       ident[:])
                    last.then_inc(turned, 1)

                def make_qk(c, u):
                    n = 4 * c + u
                    if u == 0:
                        pe.wait_ge(w0_done, 1)
                        pe.wait_ge(xt_lo_done, c + 1)
                    if n >= 2:
                        pe.wait_ge(qk_t32, n - 1)
                    hi, lo = xt_hi0[:, c % 2], xt_lo0[:, c % 2]
                    cols = slice(D * (u % 2) + (u // 2) * P, D * (u % 2) + (u // 2 + 1) * P)
                    terms = [(w, r, k) for k in range(KC) for w, r in ((w0_hi, hi), (w0_hi, lo), (w0_lo, hi))]
                    for j, (w, r, k) in enumerate(terms):
                        last = nc.tensor.matmul(ps_q[u % 2], w[:, k, cols], r[:, k, :], start=j == 0, stop=j == len(terms) - 1)
                    last.then_inc(qk_made, 1)

                def make_v(c, half):
                    if 2 * c + half:
                        pe.wait_ge(v_done, 2 * c + half)
                    hi, lo = xt_hi0[:, c % 2], xt_lo0[:, c % 2]
                    for i in range(2):
                        rows = slice((2 * half + i) * P, (2 * half + i + 1) * P)
                        terms = [(r, w, k) for k in range(KC) for r, w in ((hi, w0_hi), (hi, w0_lo), (lo, w0_hi))]
                        for j, (r, w, k) in enumerate(terms):
                            last = nc.tensor.matmul(ps_v[:, i, :], r[:, k, rows], w[:, k, 2 * D:3 * D],
                                                    start=j == 0, stop=j == len(terms) - 1)
                    last.then_inc(v_made, 1)

                turn(0)
                for c in range(NC):
                    for u in range(4):
                        make_qk(c, u)
                        if u == 0 and c + 1 < NC:
                            turn(c + 1)
                        pieces(PIECES_AT[c, u][1])
                        if u % 2:
                            make_v(c, u // 2)
                            if c == 0 and u == 3:
                                pe.wait_ge(act_step, 2)
                                nc.tensor.matmul(ps_w, ones[:], wsum[:], start=True, stop=True).then_inc(wsum_all, 1)

                pieces(pieces_by(0, 0))
                for n in range(NQUADS * NU):
                    i, u = divmod(n, NU)
                    for pair in range(2):
                        scores(i, u, pair)
                        pieces(pieces_by(n, pair + 1))
                    if n >= LAG:
                        product(*divmod(n - LAG, NU))
                    pieces(pieces_by(n + 1, 0))
                    if n in EARLY_TILE:
                        stage(FIRST[EARLY_TILE[n]])
                    elif n == EARLY_TURN:
                        stage(FIRST[-2])
                for u in range(NU - LAG, NU):
                    product(NQUADS - 1, u)

                for s in LATE:
                    stage(s)

            @block.scalar
            def _(act):
                sc = 1.0 / (XS * WS)
                def stage(s):
                    kind, c = s[0:2]
                    if kind.startswith("TURN"):
                        act.wait_ge(slot_made, filled[s])
                        if turns[s] >= 2:
                            before = max(n for b, n in pair_use.items() if turns[(BEFORE[b[0]], b[1])] == turns[s] - 2)
                            act.wait_ge(pair_made, before + 1)
                        nc.scalar.activation(xt_hi[:, turns[s] % 2].rearrange("p k n -> p (k n)"), slot_of(s),
                                             ACT.Copy).then_inc(turn_hi, 1)
                    elif kind == "GU":
                        f, m = s[2], hidden[s]
                        if m == 0:
                            act.wait_ge(pv_done, NU * NQUADS)
                        act.wait_ge(pair_made, pair_use[s] + 1)
                        if m >= NA:
                            act.wait_ge(h32_done, m - NA + 1)
                        nc.scalar.activation(act_out[:, m % NA, :], pair_of(s)[:, 0, :], ACT.Silu,
                                             scale=sg_sb[:, f:f + 1]).then_inc(silu_done, 1)
                    elif kind == "UP":
                        act.wait_ge(pair_made, pair_use[s] + 1)
                        for f in (2 * s[2], 2 * s[2] + 1):
                            m = hidden[(kind, c, f)]
                            act.wait_ge(lo_done, m - NH + 1)
                            nc.scalar.activation(h32[:, m % NH, :], pair_of(s)[:, f % 2, :], ACT.Gelu,
                                                 bias=b1_sb[:, f:f + 1], scale=1.0 / XS).then_inc(h32_done, 1)
                    elif kind == "QKV" and s[2] < 2:
                        f = s[2]
                        act.wait_ge(pair_made, pair_use[s] + 1)
                        for i in range(2):
                            bias = bl_sb[:, 2 * f + i:2 * f + i + 1]
                            src = pair_of(s)[:, i, :]
                            if f == 0:
                                nc.scalar.activation(qt[:, i, c * CH:(c + 1) * CH], src, ACT.Identity, bias=bias, scale=sc)
                            else:
                                if c >= 1:
                                    act.wait_ge(kv_done, 2 * (c - 1) + i + 1)
                                nc.scalar.activation(kt32[:, i, :], src, ACT.Identity, bias=bias, scale=sc).then_inc(k_done, 1)
                            if 4 * c + 2 * f + i:
                                act.wait_ge(q_done, 4 * c + 2 * f + i)
                            nc.scalar.activation(sq_junk[:], src, ACT.Square, bias=bias, scale=sc,
                                                 accum_out=sums[:, f, i, c:c + 1]).then_inc(q_done, 1)
                    if kind in ("GU", "DOWN1"):
                        for m in HIGH.get(s, ()):
                            high_half(act, m)

                def copy_out(n):
                    i, c = divmod(n, CB)
                    act.wait_ge(pv_done, i * NU + (TC if c == 0 else NU))
                    if i >= 2 and c == 0:
                        act.wait_ge(attn_in[i % 2], 16 * QUAD * (i // 2))
                    nc.scalar.activation(o_sb[:, i % 2, c * CH:(c + 1) * CH], ps_o, ACT.Copy).then_inc(o_copied, 1)

                for n, w in enumerate((wq, wk, wv)):
                    act.dma_start(w0f[:, :, n * D:(n + 1) * D], w.rearrange("(k p) n -> p k n", p=P)).then_inc(qkv_w_loaded, 16)
                act.dma_start(bqk_sb[:], bqk).then_inc(bqk_loaded, 16)
                act.dma_start(bv_b[:], bv.partition_broadcast(P)).then_inc(bqk_loaded, 16)
                act.wait_ge(qkv_w_loaded, 48)
                nc.scalar.activation(w0_hi[:], w0f, ACT.Copy, scale=WS).then_inc(w0_hi_done, 1)

                def high(c):
                    act.wait_ge(turned, c + 1)
                    if c >= 2:
                        act.wait_ge(v_made, 2 * (c - 1))
                        act.wait_ge(qk_made, 4 * (c - 1))
                    nc.scalar.activation(xt_hi0[:, c % 2], ps_t, ACT.Copy).then_inc(xt_hi_done, 1)

                high(0)
                act.wait_ge(bq_done, 1)
                for c in range(NC):
                    for u in range(4):
                        n, a, m = 4 * c + u, u % 2, u // 2
                        act.wait_ge(qk_made, n + 1)
                        if n >= 2:
                            act.wait_ge(qk_lo, n - 1)
                        nc.scalar.activation(t32[:, n % 2, :], ps_q[u % 2], ACT.Identity,
                                             bias=bqk16[:, 2 * a + m:2 * a + m + 1], scale=QS / (XS * WS)).then_inc(qk_t32, 1)
                        act.wait_ge(qk_t32, n + 1)
                        if c >= 2:
                            act.wait_ge(qk_stored[c - 2][m], 16 * 2)
                        nc.scalar.activation(qk16[:, c % 2, 2 * a, m, :], t32[:, n % 2, :], ACT.Copy).then_inc(qk_hi, 1)
                        if u == 0 and c + 1 < NC:
                            high(c + 1)
                        if c == 0 and u == 1:
                            act.wait_ge(tern_loaded, 32)
                            for i in range(2):
                                then(act, "act", nc.scalar.activation(below[:], w12f[:, i, :], ACT.Abs,
                                                                      accum_out=wsum[:, i:i + 1]))
                        if c == 1 and u == 3:
                            act.wait_ge(wl_loaded, 16)
                            nc.scalar.activation(wl_hi[:], wlf[:], ACT.Copy, scale=WS).then_inc(wl_hi_done, 1)
                act.wait_ge(i8_loaded, 48)
                for n, dst in enumerate((wg16, wu16, wd16)):
                    nc.scalar.activation(dst[:].rearrange("p a b -> p (a b)"), i8[:, n, :], ACT.Copy).then_inc(i8_cast, 1)
                for c in range(2, NC):
                    for m in range(KC):
                        act.wait_ge(qk_stored[c][m], 16 * 2)

                copied = 0
                for i in range(NQUADS):
                    for u in range(NU):
                        n = i * NU + u
                        first, w = width(u)
                        if n >= 3:
                            act.wait_ge(pv_done, n - 2)
                        for pair in range(2):
                            act.wait_ge(scores_made, 2 * n + pair + 1)
                            nc.scalar.activation(probs[:, n % 3, 2 * pair:2 * pair + 2, 0:w], ps_s[:, pair, :, 0:w],
                                                 ACT.Exp, scale=0.25 / (QS * QS)).then_inc(exp_done, 1)
                        if n == EARLY_TURN:
                            stage(FIRST[-2])
                        if (u == TC - 1 + LAG) or (u == LAG - 1 and i):
                            copy_out(copied)
                            copied += 1
                copy_out(copied)

                for s in LATE:
                    stage(s)

            @block.gpsimd
            def _(pool):
                def rstd(var, dst, scale, done):
                    then(pool, "pool", nc.gpsimd.tensor_scalar(dst, var, EPS, None, ALU.add))
                    last = nc.gpsimd.tensor_tensor(dst, dst, minus_half[:, 0:dst.shape[1]], ALU.pow)
                    if scale != 1.0:
                        then(pool, "pool", last)
                        last = nc.gpsimd.tensor_scalar(dst, dst, scale, None, ALU.mult)
                    last.then_inc(done, 1)

                def stage(s):
                    kind, c = s[0:2]
                    if kind == "NORM":
                        normalise(NQUADS - 1)
                    elif kind.startswith("STAT"):
                        pool.wait_ge(out_stats, outs[s] + 1)
                        rstd(mv_o[:, part_of(s), 1], rstd_o[:, part_of(s)], 1.0, out_rstd)
                    elif kind.startswith("LNS"):
                        pool.wait_ge(x_stats, lns[("LNN" + kind[-1], c)] + 1)
                        rstd(mv_x[:, :, 1], rstd_x[:], XS, x_rstd)
                    elif kind == "FACTOR":
                        b = c
                        pool.wait_ge(q_done, 4 * CB * (b + 1))
                        pool.wait_ge(kv_done, 2 * CB * (b + 1))
                        t = tot[:, b]
                        then(pool, "pool", nc.gpsimd.tensor_tensor(t, sums[:, :, :, CB * b], sums[:, :, :, CB * b + 1], ALU.add))
                        half = minus_half[:, 0:2 * KC].rearrange("p (a k) -> p a k", a=2)
                        then(pool, "pool", nc.gpsimd.tensor_tensor(t[:, 0:2], t[:, 0:2], half, ALU.pow))
                        then(pool, "pool", nc.gpsimd.tensor_tensor(t[:, 2], t[:, 2], t[:, 1], ALU.mult))
                        nc.gpsimd.tensor_tensor(t[:, 2], t[:, 2], t[:, 0], ALU.mult).then_inc(factor_done, 1)
                    for m in LOW.get(s, ()):
                        n, f = hiddens[HIDDEN[m][0:2]], HIDDEN[m][2]
                        pool.wait_ge(hi_done, m + 1)
                        if n >= 2 and f == 0:
                            pool.wait_ge(slot_made, down_made[n - 2])
                        nc.gpsimd.tensor_tensor(h_lo[:, n % 2, f, :], h32[:, m % NH, :], h_hi[:, n % 2, f, :],
                                                ALU.subtract).then_inc(lo_done, 1)

                def normalise(i):
                    pool.wait_ge(rec_in[i % 2], 16 * QUAD * (i // 2 + 1))
                    pool.wait_ge(o_copied, CB * (i + 1))
                    nc.gpsimd.tensor_tensor(o_sb[:, i % 2, :], o_sb[:, i % 2, :], rec_b[:, i % 2, :], ALU.mult).then_inc(attn_done, 1)

                then(pool, "pool", nc.gpsimd.memset(ident[:], 0.0))
                nc.gpsimd.affine_select(out=ident[:], in_=ident[:], compare_op=ALU.not_equal, fill=1.0,
                                        base=0, pattern=[[-1, P]], channel_multiplier=1).then_inc(consts, 1)
                nc.gpsimd.memset(minus_half[:], -0.5).then_inc(consts, 1)
                nc.gpsimd.memset(ones[:], 1.0).then_inc(consts, 1)
                pool.wait_ge(consts, 3)

                def spare_rows(st):
                    return nc.gpsimd.memset(st[64:].rearrange("p a b -> p (a b)").bitcast(F32), 0.0)

                def max_partners(st):
                    return nc.gpsimd.memset(st[64:66].rearrange("p a b -> p (a b)").bitcast(F32), TWICE_QQ)

                spare_rows(q_st[0])
                then(pool, "pool", spare_rows(k_st[0]))

                def rstd_of(c):
                    pool.wait_ge(stats_done, c + 1)
                    if c >= 2:
                        pool.wait_ge(xn_done, c - 1)
                    r = rstd0[:, c % 2, :]
                    then(pool, "pool", nc.gpsimd.tensor_scalar(r, mv0[:, c % 2, :, 1], EPS, None, ALU.add))
                    then(pool, "pool", nc.gpsimd.tensor_tensor(r, r, minus_half[:, 0:TC], ALU.pow))
                    nc.gpsimd.tensor_scalar(r, r, XS, None, ALU.mult).then_inc(rstd_done, 1)

                rstd_of(0)
                rstd_of(1)
                pool.wait_ge(rstd_done, 2)
                max_partners(k_st[0]).then_inc(stack_rows, 1)
                pool.wait_ge(stack_rows, 1)
                then(pool, "pool", nc.gpsimd.memset(mask[:], 0.0))
                nc.gpsimd.affine_select(out=mask[:, BANK - P:BANK], in_=mask[:, BANK - P:BANK],
                                        compare_op=ALU.is_ge, fill=-BIG, base=0, pattern=[[-1, P]],
                                        channel_multiplier=1).then_inc(mask_made, 1)
                nc.gpsimd.memset(v_aug[:, :, 0:HEADS * VW].rearrange("p n (h e) -> p n h e", e=VW)[:, :, :, DH], 1.0).then_inc(v_ones, 1)
                nc.gpsimd.memset(v_aug[:, :, HEADS * VW:], 1.0).then_inc(v_ones, 1)
                for c in range(NC):
                    if c + 2 < NC:
                        rstd_of(c + 2)
                    for u in range(4):
                        n, a, m = 4 * c + u, u % 2, u // 2
                        pool.wait_ge(qk_hi, n + 1)
                        if c >= 2:
                            pool.wait_ge(qk_stored[c - 2][m], 16 * 2)
                        nc.gpsimd.tensor_tensor(qk16[:, c % 2, 2 * a + 1, m, :], t32[:, n % 2, :], qk16[:, c % 2, 2 * a, m, :],
                                                ALU.subtract).then_inc(qk_lo, 1)
                pool.wait_ge(qk_lo, 4 * NC)
                for st in (q_st[1], k_st[1], q_st[2], k_st[2]):
                    last = spare_rows(st)
                then(pool, "pool", last)
                for st in k_st[1:]:
                    max_partners(st).then_inc(stack_rows, 1)
                pool.wait_ge(stack_rows, NST)

                for i in range(NQUADS):
                    for k, u in enumerate(DIAGS):
                        n = i * NU + u
                        if i == NQUADS - 1 and k == TC:
                            for s in FIRST:
                                stage(s)
                        pool.wait_ge(exp_done, 2 * n + 2)
                        tri = probs[:, n % 3, :, 0:P]
                        nc.gpsimd.affine_select(out=tri, in_=tri, compare_op=ALU.is_ge, fill=0.0, base=0,
                                                pattern=[[0, QUAD], [1, P]], channel_multiplier=-1).then_inc(masked, 1)
                        if k == len(DIAGS) - 1 and i >= 1:
                            normalise(i - 1)

                for s in LATE:
                    stage(s)

            @block.vector
            def _(dve):
                def stage(s):
                    kind, c = s[0:2]
                    tiles = range(TC * c, TC * (c + 1))
                    if kind == "RECIP":
                        reciprocals(NQUADS - 1)
                    elif kind.startswith("STAT"):
                        source = (BEFORE[kind], c)
                        src = slot_of(source).rearrange("p (i d) -> p i d", d=D)
                        part = part_of(s)
                        if s[2:] == (0,):
                            dve.wait_ge(half_made, 1)
                        else:
                            dve.wait_ge(slot_made, filled[source])
                        if outs[s]:
                            dve.wait_ge(x_final, outs[s] - (s[2:] == (1,)))
                        src, to, n = src[:, part], y[:, part], part.stop - part.start
                        if kind != "STAT2":
                            row, op = {"STAT0": (bo_b, ALU.add), "STAT1": (sd_b, ALU.mult), "STAT3": (b2_b, ALU.add)}[kind]
                            then(dve, "dve", nc.vector.tensor_tensor(to, src, row[:].unsqueeze(1).broadcast_to([P, n, D]), op))
                            src = to
                        ln_rows(dve, mv_o[:, part], stats_o[:, part], [src[:, i, :] for i in range(n)]).then_inc(out_stats, 1)
                    elif kind.startswith("ADD"):
                        stat = ("STAT" + kind[-1], *s[1:])
                        source = (BEFORE[stat[0]], *s[1:])
                        part = part_of(s)
                        src = y if kind[-1] in "013" else slot_of(source[0:2]).rearrange("p (i d) -> p i d", d=D)
                        dve.wait_ge(out_rstd, outs[stat] + 1)
                        dve.wait_ge(out_stats, outs[stat] + 1)
                        for i in range(part.start, part.stop):
                            last = nc.vector.tensor_scalar(y[:, i, :], src[:, i, :], mv_o[:, i, 0:1], rstd_o[:, i:i + 1],
                                                           ALU.subtract, ALU.mult)
                        last.then_inc(slot_free, 1)
                        dve.wait_ge(slot_free, freed[source])
                        xs = x[:, TC * c + part.start:TC * c + part.stop, :]
                        nc.vector.tensor_tensor(xs, xs, y[:, part], ALU.add).then_inc(x_final, 1)
                    elif kind.startswith("LNS"):
                        dve.wait_ge(x_final, adds[(BEFORE[kind], c)])
                        ln_rows(dve, mv_x, stats_x, [x[:, t, :] for t in tiles]).then_inc(x_stats, 1)
                    elif kind.startswith("LNN"):
                        dve.wait_ge(x_rstd, lns[s] + 1)
                        dve.wait_ge(x_stats, lns[s] + 1)
                        if lns[s] >= 2:
                            dve.wait_ge(slot_made, xn_turned[lns[s] - 2])
                        for i, t in enumerate(tiles):
                            last = nc.vector.tensor_scalar(xn[:, lns[s] % 2, i, :], x[:, t, :], mv_x[:, i, 0:1],
                                                           rstd_x[:, i:i + 1], ALU.subtract, ALU.mult)
                        last.then_inc(xn_ready, 1)
                    elif kind.startswith("LOW"):
                        turn = ("TURN" + kind[-1], c)
                        dve.wait_ge(turn_hi, turns[turn] + 1)
                        par = turns[turn] % 2
                        nc.vector.tensor_tensor(xt_lo[:, par].rearrange("p k n -> p (k n)"), slot_of(turn),
                                                xt_hi[:, par].rearrange("p k n -> p (k n)"), ALU.subtract).then_inc(slot_free, 1)
                    elif kind == "KV":
                        v_blocks = ("QKV", c, 2)
                        dve.wait_ge(pair_made, pair_use[v_blocks] + 1)
                        for i in range(2):
                            if c >= 1:
                                dve.wait_ge(kv_done, 2 * (c - 1) + i + 1)
                            then(dve, "dve", nc.vector.tensor_scalar(vt32[:, i, :], pair_of(v_blocks)[:, i, :], 1.0 / (XS * WS),
                                                                     bl_sb[:, 4 + i:5 + i], ALU.mult, ALU.add))
                            dve.wait_ge(k_done, 2 * c + i + 1)
                            if 2 * c + i:
                                dve.wait_ge(kv_done, 2 * c + i)
                            nc.vector.tensor_tensor_reduce(kv_junk[:], vt32[:, i, :], kt32[:, i, :], 1.0, 0.0, ALU.mult, ALU.add,
                                                           sums[:, 2, i, c:c + 1]).then_inc(kv_done, 1)
                    elif kind == "FACTOR":
                        dve.wait_ge(factor_done, c + 1)
                        for k in range(KC):
                            q = qt[:, k, c * S:(c + 1) * S]
                            last = nc.vector.tensor_scalar(q, q, tot[:, c, 2, k:k + 1], None, ALU.mult)
                        last.then_inc(q_scaled, 1)
                    for m in GATED.get(s, ()):
                        f = HIDDEN[m][2]
                        if m == 0:
                            dve.wait_ge(pv_done, NU * NQUADS)
                        dve.wait_ge(silu_done, m + 1)
                        if m >= NH:
                            dve.wait_ge(lo_done, m - NH + 1)
                        nc.vector.scalar_tensor_tensor(h32[:, m % NH, :], pair_of(HIDDEN[m])[:, 1, :], su_sb[:, f:f + 1],
                                                       act_out[:, m % NA, :], ALU.mult, ALU.mult).then_inc(h32_done, 1)
                    if kind in ("UP", "DOWN3"):
                        for m in HIGH.get(s, ()):
                            high_half(dve, m)

                def maxima(i, n):
                    h, (t, p) = n // NP, PIECES[n % NP]
                    w = min(CH, P * (t + 1) - CH * p)
                    dve.wait_ge(max_made, i * MAXES + n + 1)
                    if i == 0 and n == 0:
                        dve.wait_ge(mask_made, 1)
                    src, dst = ps_m[:, max_slot(i, n), 0:w], parts[:, i % 2, h, n % NP:n % NP + 1]
                    m = i * MAXES + n
                    if p == t // TC:
                        if m >= 2:
                            dve.wait_ge(max_read, m - 1)
                        nc.vector.tensor_tensor_reduce(junk[:, m % 2, 0:w], src, mask[:, CH - w:CH], 1.0, -BIG, ALU.add,
                                                       ALU.max, dst).then_inc(max_read, 1)
                    else:
                        nc.vector.tensor_reduce(dst, src, axis=AX_X, op=ALU.max).then_inc(max_read, 1)

                def finish_max(i):
                    pi, mi = parts[:, i % 2], rowmax[:, i % 2]
                    dve.wait_ge(max_read, MAXES * (i + 1))
                    nc.vector.tensor_copy(mi[:, :, 0:TC], pi[:, :, 0:TC])
                    two = pi[:, :, TC:NP].rearrange("p h (t c) -> p h t c", c=2)
                    nc.vector.tensor_tensor(mi[:, :, TC:KT], two[:, :, :, 0], two[:, :, :, 1], ALU.max).then_inc(max_full, 1)

                def split_max(i):
                    dve.wait_ge(max_turned, i + 1)
                    if i >= 2:
                        dve.wait_ge(max_rows_in[i % 2], 32 * (i // 2))
                    src = ps_m[0:QUAD * KT, max_slot(i, MAXES), 0:P]
                    then(dve, "dve", nc.vector.tensor_scalar(max_hi[:, i % 2, :], src, -1.0 / (QS * QS), None, ALU.mult))
                    nc.vector.scalar_tensor_tensor(max_lo[:, i % 2, :], src, -1.0 / (QS * QS), max_hi[:, i % 2, :],
                                                   ALU.mult, ALU.subtract).then_inc(max_split, 1)

                def reciprocals(i):
                    dve.wait_ge(den_in, 16 * (i + 1))
                    nc.vector.reciprocal(den[:, i % 2, :], den[:, i % 2, :]).then_inc(rec_done, 1)

                def ternary(n):
                    if n == 0:
                        dve.wait_ge(tern_loaded, 32)
                        dve.wait_ge(wsum_done, 1)
                        dve.wait_ge(act_step, 2)
                    then(dve, "dve", nc.vector.tensor_scalar(below[:], w12f[:, n, :], thr[:, 1, n:n + 1], None, ALU.is_lt))
                    then(dve, "dve", nc.vector.scalar_tensor_tensor(
                        (w1_16, w2_16)[n][:].rearrange("p a b -> p (a b)"), w12f[:, n, :], thr[:, 0, n:n + 1], below[:],
                        ALU.is_gt, ALU.subtract))

                def ln(c):
                    dve.wait_ge(x_loaded[c], 16)
                    if c >= 2:
                        dve.wait_ge(rstd_done, c - 1)
                    ln_rows(dve, mv0[:, c % 2], stats0, [x[:, TC * c + i, :] for i in range(TC)]).then_inc(stats_done, 1)

                def normalise(c):
                    dve.wait_ge(rstd_done, c + 1)
                    dve.wait_ge(stats_done, c + 1)
                    if c >= 2:
                        dve.wait_ge(turned, c - 1)
                    for i in range(TC):
                        last = nc.vector.tensor_scalar(xn[:, c % 2, i, :], x[:, TC * c + i, :], mv0[:, c % 2, i, 0:1],
                                                       rstd0[:, c % 2, i:i + 1], ALU.subtract, ALU.mult)
                    last.then_inc(xn_done, 1)

                def low(c):
                    dve.wait_ge(xt_hi_done, c + 1)
                    if c >= 2:
                        dve.wait_ge(v_made, 2 * (c - 1))
                        dve.wait_ge(qk_made, 4 * (c - 1))
                    nc.vector.tensor_tensor(xt_lo0[:, c % 2], ps_t, xt_hi0[:, c % 2], ALU.subtract).then_inc(xt_lo_done, 1)

                def copy_v(c, half):
                    dve.wait_ge(v_made, 2 * c + half + 1)
                    if c == 0:
                        dve.wait_ge(bqk_loaded, 32)
                    for i in range(2):
                        last = nc.vector.scalar_tensor_tensor(
                            v_aug[:, TC * c + 2 * half + i, 0:HEADS * VW].rearrange("p (h e) -> p h e", e=VW)[:, :, 0:DH],
                            ps_v[:, i, :].rearrange("p (h d) -> p h d", d=DH),
                            1.0 / (XS * WS), bv_b[:].rearrange("p (h d) -> p h d", d=DH), ALU.mult, ALU.add)
                    last.then_inc(v_done, 1)

                ln(0)
                normalise(0)
                ln(1)
                dve.wait_ge(w0_hi_done, 1)
                nc.vector.scalar_tensor_tensor(w0_lo[:].rearrange("p a b -> p (a b)"), w0f.rearrange("p a b -> p (a b)"),
                                               WS, w0_hi[:].rearrange("p a b -> p (a b)"),
                                               ALU.mult, ALU.subtract).then_inc(w0_done, 1)
                low(0)
                normalise(1)
                dve.wait_ge(bqk_loaded, 32)
                nc.vector.tensor_scalar(bqk16[:], bqk_sb[:], QS, None, ALU.mult).then_inc(bq_done, 1)
                for c in range(NC):
                    if c + 1 < NC:
                        low(c + 1)
                    if c + 2 < NC:
                        ln(c + 2)
                    for half in range(2):
                        for u in (2 * half, 2 * half + 1):
                            for n in range(*PIECES_AT[c, u]):
                                maxima(0, n)
                        copy_v(c, half)
                        if half == 0 and c + 2 < NC:
                            normalise(c + 2)
                    if c == 1:
                        dve.wait_ge(wsum_all, 1)
                        then(dve, "dve", nc.vector.tensor_scalar(thr[:, 0, :], ps_w, 1.0 / (D * INTER), QUANT_EPS,
                                                                 ALU.mult, ALU.max))
                        then(dve, "dve", nc.vector.tensor_scalar(thr[:, 1, :], thr[:, 0, :], -0.5, None, ALU.mult))
                        nc.vector.tensor_scalar(thr[:, 0, :], thr[:, 0, :], 0.5, None, ALU.mult).then_inc(wsum_done, 1)
                        dve.wait_ge(small_loaded, 112)
                        nc.vector.tensor_scalar(sg_sb[:], sg_sb[:], 1.0 / XS, None, ALU.mult)
                        nc.vector.tensor_scalar(su_sb[:], su_sb[:], FS / XS, None, ALU.mult)
                        nc.vector.tensor_scalar(sd_b[:], sd_b[:], 1.0 / FS, None, ALU.mult)
                        dve.wait_ge(wl_hi_done, 1)
                        nc.vector.scalar_tensor_tensor(wl_lo[:].rearrange("p a b -> p (a b)"), wlf[:].rearrange("p a b -> p (a b)"),
                                                       WS, wl_hi[:].rearrange("p a b -> p (a b)"), ALU.mult, ALU.subtract)

                for i in range(NQUADS):
                    for n in range(PIECES_AT[NC - 1, 3][1] if i == 0 else 0, MAXES):
                        maxima(i, n)
                        if n == 1 and i:
                            split_max(i - 1)
                        if n == 3 * NP and i >= 2:
                            reciprocals(i - 2)
                    finish_max(i)
                split_max(NQUADS - 1)
                for n in range(2):
                    ternary(n)
                for s in FIRST:
                    if s[0] == "LNN1":
                        reciprocals(NQUADS - 2)
                    stage(s)

                for s in LATE:
                    stage(s)





def kernel(**inputs):
    import numpy as np
    import concourse.bacc as bacc
    from concourse import mybir as mb
    from concourse.bass_utils import run_bass_kernel_spmd

    a = {k: np.asarray(v) for k, v in inputs.items()}

    def columns(v):
        return np.ascontiguousarray(v.reshape(-1, 128).T)

    def words(v):
        return np.ascontiguousarray(v).view(np.int32)

    arrays = {
        "x": a["L0_attn_X"],
        "wq": a["L0_attn_Wq"].T, "wk": a["L0_attn_Wk"].T, "wv": a["L0_attn_Wv"].T, "wo": a["L0_attn_Wo"].T,
        "bqk": np.concatenate([columns(a["L0_attn_bq"]), columns(a["L0_attn_bk"])], axis=1),
        "bv": a["L0_attn_bv"], "bo": a["L0_attn_bo"],
        "wg": words(a["L0_ffn_w_gate"]), "wu": words(a["L0_ffn_w_up"]), "wd": words(a["L0_ffn_w_down"]),
        "sg": columns(a["L0_ffn_s_gate"]), "su": columns(a["L0_ffn_s_up"]), "sd": a["L0_ffn_s_down"],
        "w2": a["L1_attn_W"], "b2qkv": columns(a["L1_attn_b"]),
        "w1t": a["L1_ffn_w1"].T, "b1": columns(a["L1_ffn_b1"]), "w2t": a["L1_ffn_w2"].T, "b2": a["L1_ffn_b2"],
    }
    nc = bacc.Bacc("TRN2", target_bir_lowering=False, num_devices=1)
    fed, args = {}, []
    for name, v in arrays.items():
        v = np.ascontiguousarray(v)
        fed[f"in_{name}"] = v
        args.append(nc.dram_tensor(f"in_{name}", list(v.shape), mb.dt.from_np(v.dtype), kind="ExternalInput").ap())
    shape = a["L0_attn_X"].shape
    out = nc.dram_tensor("out_x", list(shape), mb.dt.float32, kind="ExternalOutput").ap()
    sandwich(nc, *args, out)
    return run_bass_kernel_spmd(nc, [fed], core_ids=[0]).results[0]["out_x"]
```
